# Optimizing a Trainium2 kernel written in Bass

```python
import numpy as np
import jax
import jax.numpy as jnp

def _softmax(x, axis=-1):
    return jax.nn.softmax(x, axis=axis)

def _gelu(x):
    return jax.nn.gelu(x, approximate=True)

def _silu(x):
    return jax.nn.silu(x)

def _sigmoid(x):
    return jax.nn.sigmoid(x)

def _layernorm(x, axis=-1, eps=1e-05):
    m = jnp.mean(x, axis=axis, keepdims=True)
    v = jnp.var(x, axis=axis, keepdims=True)
    return (x - m) / jnp.sqrt(v + eps)

def _scatter_add(tgt, idx, src, axis=0):
    return tgt.at[idx].add(src)

def _segment_sum(src, seg, n):
    return jax.ops.segment_sum(src, seg, n)
kernel_name = 'mk_seq_postln_d1_jaxref_r4_c38f5d'

def setup_inputs(seed: int=0):
    np.random.seed(seed)
    _w = jnp.asarray

    def _L0_attn_setup():
        import jax, jax.numpy as jnp
        import numpy as np
        import math
        B, L, E, H, K = (4, 256, 256, 16, 64)
        D = E // H

        def _attend(q, in_proj_weight, in_proj_bias, out_w, out_b, rel_pe):
            b, l, e = q.shape
            h, d = (H, D)
            qkv = q @ in_proj_weight.T + in_proj_bias
            qh, kh, vh = jnp.split(qkv, 3, axis=-1)
            qh = qh.reshape(b, l, h, d).transpose(0, 2, 1, 3)
            kh = kh.reshape(b, l, h, d).transpose(0, 2, 1, 3)
            vh = vh.reshape(b, l, h, d).transpose(0, 2, 1, 3)
            qh = qh / math.sqrt(d)
            scores = jnp.einsum('bhid,bhjd->bhij', qh, kh)
            pos = jnp.arange(l)
            rel = jnp.clip(pos[None, :] - pos[:, None], -K, K) + K
            bias_r = jnp.einsum('bhid,rd->bhir', qh, rel_pe)
            bias = jnp.take_along_axis(bias_r, jnp.broadcast_to(rel[None, None], (b, h, l, l)), axis=-1)
            attn = jax.nn.softmax(scores + bias, axis=-1)
            out = jnp.einsum('bhij,bhjd->bhid', attn, vh)
            out = out.transpose(0, 2, 1, 3).reshape(b, l, e)
            return out @ out_w.T + out_b
        key = jax.random.key(seed)
        ks = jax.random.split(key, 4)
        s = 1.0 / math.sqrt(E)
        return {'q': jax.random.normal(ks[0], (B, L, E), dtype=jnp.float32), 'in_proj_weight': jax.random.normal(ks[1], (3 * E, E), dtype=jnp.float32) * s, 'in_proj_bias': jnp.zeros((3 * E,), dtype=jnp.float32), 'out_w': jax.random.normal(ks[2], (E, E), dtype=jnp.float32) * s, 'out_b': jnp.zeros((E,), dtype=jnp.float32), 'rel_pe': jax.random.normal(ks[3], (2 * K + 1, D), dtype=jnp.float32) * (1.0 / math.sqrt(D))}
    _L0_attn_in = _L0_attn_setup()

    def _L0_ffn_setup():
        import jax, jax.numpy as jnp
        import numpy as np

        def _binarize(w):
            alpha = jax.lax.stop_gradient(jnp.mean(jnp.abs(w), axis=1, keepdims=True))
            bw = alpha * jnp.sign(w)
            return w + jax.lax.stop_gradient(bw - w)
        key = jax.random.key(seed)
        k1, k2, k3, k4, k5 = jax.random.split(key, 5)
        D, H = (256, 1024)
        x = jax.random.normal(k1, (64, 196, D), dtype=jnp.float32)
        w1 = jax.random.normal(k2, (H, D), dtype=jnp.float32) * 0.02
        b1 = jax.random.normal(k3, (H,), dtype=jnp.float32) * 0.02
        w2 = jax.random.normal(k4, (D, H), dtype=jnp.float32) * 0.02
        b2 = jax.random.normal(k5, (D,), dtype=jnp.float32) * 0.02
        return {'x': x, 'w1': w1, 'b1': b1, 'w2': w2, 'b2': b2}
    _L0_ffn_in = _L0_ffn_setup()
    _d = {'L0_attn_q': _L0_attn_in['q'], 'L0_attn_in_proj_weight': _L0_attn_in['in_proj_weight'], 'L0_attn_in_proj_bias': _L0_attn_in['in_proj_bias'], 'L0_attn_out_w': _L0_attn_in['out_w'], 'L0_attn_out_b': _L0_attn_in['out_b'], 'L0_attn_rel_pe': _L0_attn_in['rel_pe'], 'L0_ffn_w1': _L0_ffn_in['w1'], 'L0_ffn_b1': _L0_ffn_in['b1'], 'L0_ffn_w2': _L0_ffn_in['w2'], 'L0_ffn_b2': _L0_ffn_in['b2']}
    _x0 = _d['L0_attn_q']
    _d['L0_attn_q'] = jax.random.normal(jax.random.fold_in(jax.random.key(seed), 1), (8, 1024, 256), dtype=_x0.dtype)
    del _x0
    return _d

def reference(L0_attn_q, L0_attn_in_proj_weight, L0_attn_in_proj_bias, L0_attn_out_w, L0_attn_out_b, L0_attn_rel_pe, L0_ffn_w1, L0_ffn_b1, L0_ffn_w2, L0_ffn_b2):

    def _L0_attn_ref(q, in_proj_weight, in_proj_bias, out_w, out_b, rel_pe):
        import jax, jax.numpy as jnp
        import numpy as np
        import math
        B, L, E, H, K = (4, 256, 256, 16, 64)
        D = E // H

        def _attend(q, in_proj_weight, in_proj_bias, out_w, out_b, rel_pe):
            b, l, e = q.shape
            h, d = (H, D)
            qkv = q @ in_proj_weight.T + in_proj_bias
            qh, kh, vh = jnp.split(qkv, 3, axis=-1)
            qh = qh.reshape(b, l, h, d).transpose(0, 2, 1, 3)
            kh = kh.reshape(b, l, h, d).transpose(0, 2, 1, 3)
            vh = vh.reshape(b, l, h, d).transpose(0, 2, 1, 3)
            qh = qh / math.sqrt(d)
            scores = jnp.einsum('bhid,bhjd->bhij', qh, kh)
            pos = jnp.arange(l)
            rel = jnp.clip(pos[None, :] - pos[:, None], -K, K) + K
            bias_r = jnp.einsum('bhid,rd->bhir', qh, rel_pe)
            bias = jnp.take_along_axis(bias_r, jnp.broadcast_to(rel[None, None], (b, h, l, l)), axis=-1)
            attn = jax.nn.softmax(scores + bias, axis=-1)
            out = jnp.einsum('bhij,bhjd->bhid', attn, vh)
            out = out.transpose(0, 2, 1, 3).reshape(b, l, e)
            return out @ out_w.T + out_b
        return _attend(q, in_proj_weight, in_proj_bias, out_w, out_b, rel_pe)

    def _L0_ffn_ref(x, w1, b1, w2, b2):
        import jax, jax.numpy as jnp
        import numpy as np

        def _binarize(w):
            alpha = jax.lax.stop_gradient(jnp.mean(jnp.abs(w), axis=1, keepdims=True))
            bw = alpha * jnp.sign(w)
            return w + jax.lax.stop_gradient(bw - w)
        bw1 = _binarize(w1)
        h = jnp.einsum('bsd,hd->bsh', x, bw1) + b1
        h = jax.nn.gelu(h, approximate=False)
        bw2 = _binarize(w2)
        out = jnp.einsum('bsh,dh->bsd', h, bw2) + b2
        return out
    x = L0_attn_q
    x = _layernorm(x + _L0_attn_ref(x, L0_attn_in_proj_weight, L0_attn_in_proj_bias, L0_attn_out_w, L0_attn_out_b, L0_attn_rel_pe), axis=-1)
    x = _layernorm(x + _L0_ffn_ref(x, L0_ffn_w1, L0_ffn_b1, L0_ffn_w2, L0_ffn_b2), axis=-1)
    return x

_drawn_inputs = setup_inputs


def setup_inputs(seed=0):
    import zlib

    import numpy as np

    out = dict(_drawn_inputs(seed))
    spreads = {'L0_attn_in_proj_bias': (0.0, 0.1), 'L0_attn_out_b': (0.0, 0.1)}
    factors = {'L0_attn_rel_pe': 5.861, 'L0_ffn_b1': 8.0, 'L0_ffn_b2': 2.923}
    for name, (base, spread) in spreads.items():
        noise = np.random.default_rng([zlib.crc32(name.encode()), seed]).standard_normal(out[name].shape)
        drawn = base * np.exp(spread * noise) if base else spread * noise
        out[name] = jnp.asarray(drawn.astype(out[name].dtype))
    for name, factor in factors.items():
        out[name] = (out[name] * factor).astype(out[name].dtype)
    return out
```

```python
from contextlib import ExitStack

import concourse.bass as bass
from concourse import mybir

F32 = mybir.dt.float32
BF16 = mybir.dt.bfloat16
ALU = mybir.AluOpType
ACT = mybir.ActivationFunctionType
AX_X = mybir.AxisListType.X

P = 128
TERM_Q = (0, 0, 1, 0, 2, 1)
TERM_K = (0, 1, 0, 2, 0, 1)
TERMS = len(TERM_Q)
PARTS = 3
LOWEST = -3.0e38


def flat(ap, offset, dims):
    return bass.AP(tensor=ap.tensor, offset=ap.offset + offset, ap=[list(d) for d in dims])


def over(ap, count, at):
    dims = [list(d) for d in ap.ap]
    return bass.AP(tensor=ap.tensor, offset=ap.offset, ap=dims[:at] + [[0, count]] + dims[at:])


def post_ln_block(nc, x, w_in, b_in, w_out, b_out, rel, w1, b1, w2, b2, out):
    B, T, E = x.shape
    R, D = rel.shape
    H = E // D
    HID = w1.shape[0]
    REACH = R // 2
    NT = T // P
    HG = 4
    NG = H // HG
    G = B * NG
    KE = E // P
    KH = HID // P
    PAD = 32
    HALF = REACH
    ROWS = TERMS * D
    QROWS = ROWS + 2
    EPS = 1e-5
    assert R == P + 1 and D * HG * 2 == P and KE == 2 and T % 512 == 0

    outer = ExitStack()
    with outer:
        def sem_in(ctx, name):
            return ctx.enter_context(nc.semaphore(name))

        def sb_in(ctx, name, shape, dt):
            return ctx.enter_context(nc.sbuf_tensor(name, shape, dt))

        split_scr = nc.dram_tensor("split_scr", [3, PARTS, G, HG * D, T], BF16).ap()
        v_scr = nc.dram_tensor("v_scr", [G, P, NT, HG * PAD], F32).ap()
        band_scr = nc.dram_tensor("band_scr", [2, HG, NT, P, 4 * P], F32).ap()
        o_scr = nc.dram_tensor("o_scr", [G, P, T], F32).ap()

        ident = sb_in(outer, "ident", [P, P], F32)
        wo_pad = sb_in(outer, "wo_pad", [P, NG, E], F32)
        sign1T = sb_in(outer, "sign1T", [P, KE, HID], F32)
        sign2T = sb_in(outer, "sign2T", [P, KH, E], F32)
        alpha1 = sb_in(outer, "alpha1", [P, KH], F32)
        b1_col = sb_in(outer, "b1_col", [P, KH], F32)
        alpha2_row = sb_in(outer, "alpha2_row", [P, E], F32)
        bo_row = sb_in(outer, "bo_row", [P, E], F32)
        b2_row = sb_in(outer, "b2_row", [P, E], F32)
        rel_terms = sb_in(outer, "rel_terms", [ROWS, 2 * P], BF16)
        eps_col = sb_in(outer, "eps_col", [P, 1], F32)

        with ExitStack() as ctx:
            def sb(name, shape, dt):
                return sb_in(ctx, name, shape, dt)

            def sem(name):
                return sem_in(ctx, name)

            wT = sb("wT", [P, KE, 3 * E], F32)
            bq_col = sb("bq_col", [P, 2], F32)
            bk_left = sb("bk_left", [P, 2], F32)
            bk_right = sb("bk_right", [P, 2], F32)
            bv_row = sb("bv_row", [P, E], F32)
            bank = [ctx.enter_context(nc.psum_tensor(f"bank{i}", [P, 512], F32)) for i in range(8)]

            with ExitStack() as c0:
                w_in_s = sb_in(c0, "w_in_s", [P, 6, E], F32)
                w_out_s = sb_in(c0, "w_out_s", [P, 2, E], F32)
                w_out_p = sb_in(c0, "w_out_p", [P, 2, NG, HG, PAD], F32)
                w1_s = sb_in(c0, "w1_s", [P, KH, E], F32)
                w2_s = sb_in(c0, "w2_s", [P, 2, HID], F32)
                sgn1 = sb_in(c0, "sgn1", [P, KH, E], F32)
                sgn2 = sb_in(c0, "sgn2", [P, 2, HID], F32)
                junk1 = sb_in(c0, "junk1", [P, KH, E], F32)
                junk2 = sb_in(c0, "junk2", [P, 2, HID], F32)
                b_col = sb_in(c0, "b_col", [P, 4], F32)
                rel_ends = sb_in(c0, "rel_ends", [P, 2], F32)
                relT = sb_in(c0, "relT", [D, R], F32)
                rel_d = sb_in(c0, "rel_d", [D, 2 * P], F32)
                rel_r = sb_in(c0, "rel_r", [D, 2 * P], F32)
                rel_parts = sb_in(c0, "rel_parts", [D, PARTS, 2 * P], BF16)
                alpha2 = sb_in(c0, "alpha2", [P, 2], F32)
                alpha2_wide = sb_in(c0, "alpha2_wide", [P, 2, P], F32)
                zeros = sb_in(c0, "zeros", [P, NT, P], F32)
                s_w = sem_in(c0, "weights_in")
                s_small = sem_in(c0, "small_in")
                s_set = sem_in(c0, "pool_set")
                s_sgn = sem_in(c0, "signs_ready")
                s_dve = sem_in(c0, "dve_chain")
                s_rel = sem_in(c0, "rel_parts_ready")
                s_relt = sem_in(c0, "rel_terms_in")
                s_zero = sem_in(c0, "pads_zeroed")
                s_src = sem_in(c0, "sources_ready")
                s_tr = sem_in(c0, "transposed")
                s_eva = sem_in(c0, "evacuated_act")
                s_evd = sem_in(c0, "evacuated_dve")

                jobs = []
                for kt in range(KE):
                    for j0, nj in ((0, 4), (4, 2)):
                        jobs.append(([w_in_s[:, j, kt * P:(kt + 1) * P] for j in range(j0, j0 + nj)],
                                     wT[:, kt, j0 * P:(j0 + nj) * P]))
                for kt in range(KE):
                    for j0 in range(0, KH, 4):
                        jobs.append(([sgn1[:, j, kt * P:(kt + 1) * P] for j in range(j0, j0 + 4)],
                                     sign1T[:, kt, j0 * P:(j0 + 4) * P]))
                for kt in range(0, KH, 2):
                    jobs.append(([sgn2[:, j, k * P:(k + 1) * P] for k in (kt, kt + 1) for j in range(2)],
                                 sign2T[:, kt:kt + 2, :].rearrange("p a b -> p (a b)")))
                for g in range(0, NG, 2):
                    jobs.append(([w_out_p[:, j, k].rearrange("p h d -> p (h d)") for k in (g, g + 1)
                                  for j in range(2)],
                                 wo_pad[:, g:g + 2, :].rearrange("p a b -> p (a b)")))
                jobs.append(([alpha2_wide[:, j, :] for j in range(2)], alpha2_row[:, :]))

                block = c0.enter_context(nc.Block())

                @block.sync
                def _(sp):
                    sp.dma_start(w_in_s[:], w_in.rearrange("(j p) e -> p j e", p=P)).then_inc(s_w, 16)
                    sp.dma_start(w1_s[:], w1.rearrange("(j p) e -> p j e", p=P)).then_inc(s_w, 16)
                    sp.dma_start(w2_s[:], w2.rearrange("(j p) e -> p j e", p=P)).then_inc(s_w, 16)
                    sp.dma_start(w_out_s[:], w_out.rearrange("(j p) e -> p j e", p=P)).then_inc(s_w, 16)
                    sp.wait_ge(s_set, 1)
                    for a in range(2):
                        for h in range(HG):
                            row = NT * P * 4 * P
                            for side in range(2):
                                sp.dma_start(flat(band_scr, (a * HG + h) * row + side * 3 * P,
                                                  [[4 * P, P], [P * 4 * P, NT], [1, P]]),
                                             zeros[:]).then_inc(s_zero, 16)
                    sp.wait_ge(s_rel, 3)
                    for t in range(TERMS):
                        sp.dma_start(rel_terms[t * D:(t + 1) * D, :],
                                     rel_parts[:, TERM_K[t], :]).then_inc(s_relt, 16)
                    sp.wait_ge(s_relt, 16 * TERMS)
                    sp.wait_ge(s_zero, 16 * 4 * HG)

                @block.scalar
                def _(act):
                    act.dma_start(b_col[:], b_in[0:2 * E].rearrange("(j p) -> p j", p=P),
                                  allow_slow_non_contiguous=True).then_inc(s_small, 16)
                    act.dma_start(b1_col[:], b1.rearrange("(j p) -> p j", p=P),
                                  allow_slow_non_contiguous=True).then_inc(s_small, 16)
                    act.dma_start(relT[:], rel.rearrange("r d -> d r"),
                                  allow_slow_non_contiguous=True).then_inc(s_small, 16)
                    for n, r in enumerate((0, R - 1)):
                        for h in range(P // D):
                            act.dma_start(rel_ends[h * D:(h + 1) * D, n:n + 1],
                                          flat(rel, r * D, [[1, D], [1, 1]]),
                                          allow_slow_non_contiguous=True).then_inc(s_small, 16)
                    act.dma_start(bv_row[:], flat(b_in, 2 * E, [[0, P], [1, E]])).then_inc(s_small, 16)
                    act.dma_start(bo_row[:], flat(b_out, 0, [[0, P], [1, E]])).then_inc(s_small, 16)
                    act.dma_start(b2_row[:], flat(b2, 0, [[0, P], [1, E]])).then_inc(s_small, 16)
                    act.wait_ge(s_w, 64)
                    nc.scalar.activation(sgn1[:], w1_s[:], ACT.Sign).then_inc(s_sgn, 1)
                    nc.scalar.activation(sgn2[:], w2_s[:], ACT.Sign).then_inc(s_sgn, 1)
                    for n, (src, dst) in enumerate(jobs):
                        if n % 2 == 0:
                            act.wait_ge(s_tr, n + 1)
                            nc.scalar.activation(dst, bank[n % 8][:, 0:len(src) * P],
                                                 ACT.Copy).then_inc(s_eva, 1)

                @block.gpsimd
                def _(pool):
                    nc.gpsimd.memset(zeros[:], 0.0).then_inc(s_set, 1)
                    nc.gpsimd.memset(ident[:], 0.0).then_inc(s_set, 1)
                    nc.gpsimd.memset(w_out_p[:], 0.0).then_inc(s_set, 1)
                    nc.gpsimd.memset(eps_col[:], EPS).then_inc(s_set, 1)
                    pool.wait_ge(s_set, 2)
                    nc.gpsimd.affine_select(out=ident[:], in_=ident[:], compare_op=ALU.not_equal, fill=1.0,
                                            base=0, pattern=[[-1, P]], channel_multiplier=1).then_inc(s_set, 1)
                    pool.wait_ge(s_set, 5)
                    pool.wait_ge(s_w, 64)
                    for j in range(2):
                        nc.gpsimd.tensor_copy(
                            w_out_p[:, j, :, :, 0:D],
                            w_out_s[:, j, :].rearrange("p (g h d) -> p g h d", g=NG, h=HG)).then_inc(s_src, 1)

                @block.vector
                def _(dve):
                    dve.wait_ge(s_small, 16 * (6 + 2 * (P // D)))
                    nc.vector.tensor_scalar(bq_col[:], b_col[:, 0:2], float(D) ** -0.5, None, ALU.mult)
                    nc.vector.tensor_scalar(bk_left[:], b_col[:, 2:4], rel_ends[:, 0:1], None, ALU.add)
                    nc.vector.tensor_scalar(bk_right[:], b_col[:, 2:4], rel_ends[:, 1:2], None, ALU.add)
                    nc.vector.tensor_scalar(rel_d[:, 0:P], relT[:, 0:P], relT[:, 0:1], None,
                                            ALU.subtract).then_inc(s_dve, 1)
                    nc.vector.tensor_scalar(rel_d[:, P:2 * P], relT[:, 0:P], relT[:, R - 1:R], None,
                                            ALU.subtract).then_inc(s_dve, 1)
                    dve.wait_ge(s_dve, 2)
                    nc.vector.tensor_copy(rel_parts[:, 0, :], rel_d[:]).then_inc(s_rel, 1)
                    dve.wait_ge(s_rel, 1)
                    nc.vector.tensor_tensor(rel_r[:], rel_d[:], rel_parts[:, 0, :], ALU.subtract).then_inc(s_dve, 1)
                    dve.wait_ge(s_dve, 3)
                    nc.vector.tensor_copy(rel_parts[:, 1, :], rel_r[:]).then_inc(s_rel, 1)
                    dve.wait_ge(s_rel, 2)
                    nc.vector.tensor_tensor(rel_parts[:, 2, :], rel_r[:], rel_parts[:, 1, :],
                                            ALU.subtract).then_inc(s_rel, 1)
                    dve.wait_ge(s_sgn, 2)
                    for j in range(KH):
                        nc.vector.tensor_tensor_reduce(out=junk1[:, j, :], in0=w1_s[:, j, :], in1=sgn1[:, j, :],
                                                       scale=1.0 / E, scalar=0.0, op0=ALU.mult, op1=ALU.add,
                                                       accum_out=alpha1[:, j:j + 1])
                    for j in range(2):
                        nc.vector.tensor_tensor_reduce(out=junk2[:, j, :], in0=w2_s[:, j, :], in1=sgn2[:, j, :],
                                                       scale=1.0 / HID, scalar=0.0, op0=ALU.mult, op1=ALU.add,
                                                       accum_out=alpha2[:, j:j + 1]).then_inc(s_dve, 1)
                    dve.wait_ge(s_dve, 5)
                    for j in range(2):
                        nc.vector.tensor_copy(alpha2_wide[:, j, :], over(alpha2[:, j], P, 1)).then_inc(s_src, 1)
                    for n, (src, dst) in enumerate(jobs):
                        if n % 2 == 1:
                            dve.wait_ge(s_tr, n + 1)
                            nc.vector.tensor_copy(dst, bank[n % 8][:, 0:len(src) * P]).then_inc(s_evd, 1)

                @block.tensor
                def _(pe):
                    pe.wait_ge(s_set, 5)
                    pe.wait_ge(s_w, 64)
                    for n, (src, dst) in enumerate(jobs):
                        if n == 4:
                            pe.wait_ge(s_sgn, 2)
                        if n == 12:
                            pe.wait_ge(s_src, 4)
                        if n >= 8:
                            pe.wait_ge(s_evd if n % 2 else s_eva, (n - 8) // 2 + 1)
                        for j, a in enumerate(src):
                            last = nc.tensor.transpose(bank[n % 8][:, j * P:(j + 1) * P], a, ident[:])
                        last.then_inc(s_tr, 1)

            x_s = sb("x_s", [P, 2, NT, E], F32)
            xT = sb("xT", [P, 2, KE, HALF + T], F32)
            whole = sb("whole", [P, 3, 512], F32)
            rest = sb("rest", [P, 2, 512], F32)
            parts = sb("parts", [P, 2, 3, PARTS, 2, T], BF16)
            v_s = sb("v_s", [P, 2, NG, NT, HG, PAD], F32)
            PRODUCTS = 12
            token = sb("token", [P, 4], F32)
            CHUNKS = 12
            STORES = 3 * PARTS + NG
            s_x = [sem(f"x_in{a}") for a in range(2)]
            s_turned = sem("x_turned")
            s_job = sem("product_ready")
            s_xev = sem("xT_ready")
            s_vev = sem("v_ready")
            s_chunk = sem("chunk_ready")
            s_rest = sem("rest_ready")
            s_mid = sem("middle_part_ready")
            s_split = sem("chunk_split")
            s_store = [sem(f"stored{a}") for a in range(2)]
            block = ctx.enter_context(nc.Block())

            @block.gpsimd
            def _(pool):
                nc.gpsimd.memset(token[:, 0:1], 0.0).then_inc(s_turned, 8)
                nc.gpsimd.memset(token[:, 1:2], 0.0).then_inc(s_split, 3)
                nc.gpsimd.memset(token[:, 2:3], 0.0).then_inc(s_chunk, CHUNKS)
                nc.gpsimd.memset(token[:, 3:4], 0.0).then_inc(s_vev, 4)
                nc.gpsimd.memset(v_s[:, 0, :, :, :, D:PAD], 1.0).then_inc(s_store[0], 16 * STORES)
                nc.gpsimd.memset(v_s[:, 1, :, :, :, D:PAD], 1.0).then_inc(s_store[1], 16 * STORES)
                with pool.Fori(0, B // 2) as i:
                    for a in range(2):
                        pool.wait_ge(s_turned, i * 8 + (4 * a + 4))
                        pool.dma_start(x_s[:, a], x[i * 2 + a].rearrange("(j p) e -> p j e", p=P)).then_inc(s_x[a], 16)

            @block.sync
            def _(sp):
                with sp.Fori(0, B // 2) as i:
                    for a in range(2):
                        b = i * 2 + a
                        sp.wait_ge(s_vev, b * 4 + 8)
                        for g in range(NG):
                            sp.dma_start(v_scr[b * NG + g],
                                           v_s[:, a, g].rearrange("p n h d -> p n (h d)")).then_inc(s_store[a], 16)
                        sp.wait_ge(s_split, b * CHUNKS + (3 + CHUNKS))
                        for w in range(3):
                            for c in range(PARTS):
                                dst = split_scr[w, c, bass.ds(b * NG, NG)].rearrange("g r t -> (g r) t")
                                sp.dma_start(dst.rearrange("(m p) t -> p m t", p=P),
                                               parts[:, a, w, c]).then_inc(s_store[a], 16)
                for a in range(2):
                    sp.wait_ge(s_store[a], 16 * STORES * (1 + B // 2))

            @block.tensor
            def _(pe):
                with pe.Fori(0, B // 2) as i:
                    for a in range(2):
                        b = i * 2 + a
                        job = 0

                        def free_bank():
                            if job < 4:
                                pe.wait_ge(s_chunk, b * CHUNKS + (6 + 2 * job))
                            elif job < 8:
                                pe.wait_ge(s_vev, b * 4 + (job - 3))
                            elif job < 12:
                                pe.wait_ge(s_xev, b * 4 + (job - 7))
                            else:
                                pe.wait_ge(s_chunk, b * CHUNKS + (CHUNKS + job - 11))
                            return bank[job % 8]

                        pe.wait_ge(s_x[a], i * 16 + 16)
                        for half in range(2):
                            for kt in range(KE):
                                dst = free_bank()
                                for j in range(4):
                                    last = nc.tensor.transpose(dst[:, j * P:(j + 1) * P],
                                                               x_s[:, a, half * 4 + j, kt * P:(kt + 1) * P], ident[:])
                                last.then_inc(s_turned, 1)
                                job += 1
                        pe.wait_ge(s_xev, b * 4 + 4)
                        for what in range(2):
                            shift = HALF if what == 0 else 0
                            for m in range(2):
                                for half in range(2):
                                    dst = free_bank()
                                    for kt in range(KE):
                                        c0 = shift + half * 512
                                        last = nc.tensor.matmul(dst[:, :],
                                                                wT[:, kt, what * E + m * P:what * E + (m + 1) * P],
                                                                xT[:, a, kt, c0:c0 + 512],
                                                                start=(kt == 0), stop=(kt == KE - 1))
                                    last.then_inc(s_job, 1)
                                    job += 1
                        for n0 in range(0, NT, 2):
                            dst = free_bank()
                            for n in (n0, n0 + 1):
                                for kt in range(KE):
                                    last = nc.tensor.matmul(dst[:, (n - n0) * E:(n - n0 + 1) * E],
                                                            xT[:, a, kt, n * P:(n + 1) * P],
                                                            wT[:, kt, 2 * E:3 * E],
                                                            start=(kt == 0), stop=(kt == KE - 1))
                            last.then_inc(s_job, 1)
                            job += 1

            @block.scalar
            def _(act):
                with act.Fori(0, B // 2) as i:
                    for a in range(2):
                        b = i * 2 + a
                        job = 0
                        for half in range(2):
                            for kt in range(KE):
                                act.wait_ge(s_turned, b * 4 + (8 + job + 1))
                                if half == 1:
                                    nc.scalar.activation(xT[:, a, kt, 0:HALF], bank[job][:, 512 - HALF:512], ACT.Copy)
                                last = nc.scalar.activation(xT[:, a, kt, HALF + half * 512:HALF + (half + 1) * 512],
                                                            bank[job][:, :], ACT.Copy)
                                last.then_inc(s_xev, 1)
                                job += 1
                        act.wait_ge(s_store[a], i * 16 * STORES + 16 * STORES)
                        chunk = 0
                        for what in range(2):
                            for m in range(2):
                                for half in range(2):
                                    act.wait_ge(s_job, b * PRODUCTS + (job - 3))
                                    src = bank[job % 8]
                                    kinds = [(0, [(0, 512, bq_col, float(D) ** -0.5)])] if what == 0 else [
                                        (1, [(0, HALF, bk_right, 1.0), (HALF, 512, bk_left, 1.0)] if half == 0
                                         else [(0, 512, bk_left, 1.0)]),
                                        (2, [(0, 512, bk_right, 1.0)])]
                                    for w, pieces in kinds:
                                        act.wait_ge(s_split, b * CHUNKS + (chunk + 1))
                                        for c0, c1, bias, scale in pieces:
                                            nc.scalar.activation(whole[:, chunk % 3, c0:c1], src[:, c0:c1],
                                                                 ACT.Identity, bias=bias[:, m:m + 1], scale=scale)
                                        for c0, c1, bias, scale in pieces:
                                            last = nc.scalar.activation(
                                                parts[:, a, w, 0, m, half * 512 + c0:half * 512 + c1], src[:, c0:c1],
                                                ACT.Identity, bias=bias[:, m:m + 1], scale=scale)
                                        last.then_inc(s_chunk, 1)
                                        chunk += 1
                                    job += 1

            @block.vector
            def _(dve):
                with dve.Fori(0, B // 2) as i:
                    for a in range(2):
                        b = i * 2 + a
                        dve.wait_ge(s_store[a], i * 16 * STORES + 16 * STORES)
                        chunk = 0
                        for what in range(2):
                            for m in range(2):
                                for half in range(2):
                                    for w in ((0,), (1, 2))[what]:
                                        col = slice(half * 512, (half + 1) * 512)
                                        dve.wait_ge(s_chunk, b * CHUNKS + (CHUNKS + chunk + 1))
                                        nc.vector.tensor_tensor(rest[:, chunk % 2, :], whole[:, chunk % 3, :],
                                                                parts[:, a, w, 0, m, col],
                                                                ALU.subtract).then_inc(s_rest, 1)
                                        dve.wait_ge(s_rest, b * CHUNKS + (chunk + 1))
                                        nc.vector.tensor_copy(parts[:, a, w, 1, m, col],
                                                              rest[:, chunk % 2, :]).then_inc(s_mid, 1)
                                        dve.wait_ge(s_mid, b * CHUNKS + (chunk + 1))
                                        nc.vector.tensor_tensor(parts[:, a, w, 2, m, col], rest[:, chunk % 2, :],
                                                                parts[:, a, w, 1, m, col],
                                                                ALU.subtract).then_inc(s_split, 1)
                                        chunk += 1
                        for j in range(4):
                            dve.wait_ge(s_job, b * PRODUCTS + (9 + j))
                            for n in range(2):
                                last = nc.vector.tensor_tensor(
                                    v_s[:, a, :, 2 * j + n, :, 0:D],
                                    bank[4 + j][:, n * E:(n + 1) * E].rearrange("p (g h d) -> p g h d", g=NG, h=HG),
                                    bv_row[:].rearrange("p (g h d) -> p g h d", g=NG, h=HG), ALU.add)
                            last.then_inc(s_vev, 1)

        with ExitStack() as ctx:
            def sb(name, shape, dt):
                return sb_in(ctx, name, shape, dt)

            def sem(name):
                return sem_in(ctx, name)

            KBUF = 3
            IP = NT // 2
            UNITS = IP * NT
            ITEMS = NT * HG
            CH = ITEMS // 2
            PROLOGUE_CH = CH + CH * (IP - 1) // IP
            LOOK_SLOTS = UNITS - 3
            CHUNK_SLOT = [4, 5, 6, 7] + [8 * (k + 1) + 3 + j for k in range(IP - 1) for j in range(4)]
            BAND_READS = [16 * HG * (2 if t in (0, NT - 1) else 1) for t in range(NT)]
            UNROLL = 6
            LOOPS = (G - 2) // UNROLL
            assert LOOPS * UNROLL == G - 2

            keys = sb("keys", [QROWS, KBUF, 2, HG, T], BF16)
            queries = sb("queries", [QROWS, 2, HG, T], BF16)
            values = sb("values", [P, 2, NT, HG * PAD], F32)
            band_all = sb("band_all", [P, 2 * ITEMS * 2 * P + 2 * P], F32)
            band = band_all[:, 0:2 * ITEMS * 2 * P].rearrange("p (a n h s c) -> p a n h s c", a=2, n=NT, h=HG, s=2)
            no_band = band_all[:, 2 * ITEMS * 2 * P:]
            band_out = sb("band_out", [P, 2, 2, 2 * P], F32)
            probs = sb("probs", [P, 2, HG, 2 * P], F32)
            partial_max = sb("partial_max", [P, 2, ITEMS], F32)
            row_max = sb("row_max", [P, ITEMS], F32)
            minus_max = sb("minus_max", [ITEMS, 2, P], BF16)
            weighted_s = sb("weighted_s", [P, 2, 2 * P], F32)
            sums = sb("sums", [P, 2 * P], F32)
            inverse = sb("inverse", [P, 2 * P], F32)
            heads_out = sb("heads_out", [P, IP, 2 * P], F32)
            token = sb("token2", [P, 8], F32)

            weigh_ps = [ctx.enter_context(nc.psum_tensor(f"weigh_ps{a}", [P, HG, 2 * P], F32)) for a in range(2)]
            look_ps = [ctx.enter_context(nc.psum_tensor(f"look_ps{a}", [P, 512], F32)) for a in range(2)]
            band_ps = ctx.enter_context(nc.psum_tensor("band_ps", [P, 2, 2 * P], F32))
            sum_ps = ctx.enter_context(nc.psum_tensor("sum_ps", [P, 2 * P], F32))

            s_set = sem("constants_set")
            s_passed = sem("waits_passed")
            s_keys = [sem(f"keys_in{a}") for a in range(KBUF)]
            s_q = [[sem(f"queries_in{a}_{k}") for k in range(IP)] for a in range(2)]
            s_v = [sem(f"values_in{a}") for a in range(2)]
            s_bp = sem("band_product_ready")
            s_be = sem("band_product_read")
            s_bw = [sem(f"band_written{a}") for a in range(2)]
            s_b = [sem(f"band_in{t}") for t in range(NT)]
            s_look = [sem(f"look_ready{a}") for a in range(2)]
            s_seen = [sem(f"look_read{a}") for a in range(2)]
            s_rm = sem("row_max_ready")
            s_rmT = sem("row_max_turned")
            s_hi = sem("minus_max_high_ready")
            s_mm = sem("minus_max_ready")
            s_min = [sem(f"minus_max_in{a}") for a in range(2)]
            s_sc = sem("scores_ready")
            s_pr = sem("probs_ready")
            s_av = sem("weighted_sum_ready")
            s_ws = sem("weighted_sum_copied")
            s_sum = sem("sums_spread")
            s_inv = sem("inverse_ready")
            s_norm = sem("heads_out_ready")
            s_hofree = sem("heads_out_free")
            s_ho = [sem(f"heads_stored{k}") for k in range(IP)]

            def key_kind(n, t):
                return 0 if n == 0 or n <= t else 1

            def look_pieces(t):
                pieces = []
                for pos in range(NT):
                    n = (t + pos) % NT
                    kind, half = key_kind(n, t), pos // 4
                    last = pieces[-1] if pieces else None
                    if last and last[0] == half and last[2] == kind and last[3] + last[4] == n:
                        last[4] += 1
                    else:
                        pieces.append([half, pos % 4 * P, kind, n, 1])
                return pieces

            def items_at(u):
                return [i for i in range(ITEMS) if i * LOOK_SLOTS // ITEMS == u]

            def chunk_of(j):
                per = CH // IP
                k = (j // per + IP - 1) % IP
                ahead = 1 if j < per else 2
                return ahead, 2 * k + j % per // 2, 2 * (j % 2)

            def wait_apart(eng, *waits):
                for what, count in waits:
                    eng.wait_ge(what, count)
                eng.sem_inc(s_passed, 1)

            block = ctx.enter_context(nc.Block())

            @block.sync
            def _(sp):
                def load_keys(s, k):
                    for kind in range(2):
                        for t in range(TERMS):
                            sp.dma_start(keys[t * D:(t + 1) * D, k % KBUF, kind],
                                         split_scr[1 + kind, TERM_K[t], s].rearrange("(h d) t -> d h t", h=HG)
                                         ).then_inc(s_keys[k % KBUF], 16)

                def load_values(s, k):
                    sp.dma_start(values[:, k % 2], v_scr[s]).then_inc(s_v[k % 2], 16)

                def load_queries(s, k, pair):
                    col = slice(pair * 2 * P, (pair + 1) * 2 * P)
                    for t in range(TERMS):
                        sp.dma_start(queries[t * D:(t + 1) * D, k % 2, :, col],
                                     split_scr[0, TERM_Q[t], s].rearrange("(h d) t -> d h t", h=HG)[:, :, col]
                                     ).then_inc(s_q[k % 2][pair], 16)

                def write_band(count, k, tile, h0):
                    sp.wait_ge(s_be, count + 1)
                    a = tile * 2 + h0 // 2
                    sp.dma_start(flat(band_scr, ((k % 2) * HG + h0) * NT * P * 4 * P + tile * P * 4 * P + P,
                                      [[4 * P, P], [NT * P * 4 * P, 2], [1, 2 * P]]),
                                 band_out[:, a % 2]).then_inc(s_bw[a % 2], 16)

                def read_band(written, k, tile, h0):
                    a = tile * 2 + h0 // 2
                    sp.wait_ge(s_bw[a % 2], written)
                    for h in range(h0, h0 + 2):
                        base = ((k % 2) * HG + h) * NT * P * 4 * P + tile * P * 4 * P + P
                        if tile == 0:
                            sp.dma_start(band[:, k % 2, tile, h, 0, HALF:P],
                                         flat(band_scr, base + HALF, [[4 * P - 1, P], [1, P - HALF]])
                                         ).then_inc(s_b[tile], 16)
                            sp.dma_start(band[:, k % 2, tile, h, 1],
                                         flat(band_scr, base + 2 * P, [[4 * P - 1, P], [1, P]])
                                         ).then_inc(s_b[tile], 16)
                        elif tile == NT - 1:
                            sp.dma_start(band[:, k % 2, tile, h, 0],
                                         flat(band_scr, base, [[4 * P - 1, P], [1, P]])
                                         ).then_inc(s_b[tile], 16)
                            sp.dma_start(band[:, k % 2, tile, h, 1, 0:HALF],
                                         flat(band_scr, base + 2 * P, [[4 * P - 1, P], [1, HALF]])
                                         ).then_inc(s_b[tile], 16)
                        else:
                            sp.dma_start(band[:, k % 2, tile, h],
                                         flat(band_scr, base, [[4 * P - 1, P], [2 * P, 2], [1, P]])
                                         ).then_inc(s_b[tile], 16)

                def load_minus_max(s, k):
                    sp.wait_ge(s_mm, s + 1)
                    for c in range(2):
                        row = queries[ROWS + c:ROWS + c + 1, k % 2]
                        sp.dma_start(flat(row, 0, [row.ap[0], [P, ITEMS], [1, P]]),
                                     minus_max[:, c, :].rearrange("r (a p) -> r a p", a=1)
                                     ).then_inc(s_min[k % 2], 16)

                def step(s, k, look=True, ahead=True):
                    base = s * CH + PROLOGUE_CH
                    queue = []
                    for j, slot in enumerate(CHUNK_SLOT):
                        d, tile, h0 = chunk_of(j)
                        if not (look if d == 1 else ahead):
                            continue
                        queue.append((slot + 1, 1, "write", j, k + d, tile, h0))
                        queue.append((slot + 3, 2, "read", j, k + d, tile, h0))
                    queue.append((1, 0, "load", 0, 0, 0, 0))
                    for u in range(NT, UNITS, NT):
                        queue.append((u, 0, "q", u, 0, 0, 0))
                    queue.append((UNITS, 1.5, "max", 0, 0, 0, 0))
                    for _, _, what, j, kk, tile, h0 in sorted(queue, key=lambda e: (min(e[0], UNITS), e[1])):
                        if what == "write":
                            write_band(base + j, kk, tile, h0)
                        elif what == "read":
                            read_band(s * (8 * CH) + 16 * (PROLOGUE_CH // 2 + j // 2 + 1), kk, tile, h0)
                        elif what == "load":
                            wait_apart(sp, (s_sc, s * UNITS + 1))
                            if look:
                                load_queries(s + 1, k + 1, IP - 1)
                                load_values(s + 1, k + 1)
                            if ahead:
                                load_keys(s + 2, k + 2)
                        elif what == "q" and ahead:
                            wait_apart(sp, (s_sc, s * UNITS + j))
                            load_queries(s + 2, k + 2, j // NT - 1)
                        elif what == "max" and look:
                            load_minus_max(s + 1, k + 1)

                for pair in range(IP):
                    load_queries(0, 0, pair)
                load_keys(0, 0)
                for pair in range(IP - 1):
                    load_queries(1, 1, pair)
                load_keys(1, 1)
                load_values(0, 0)
                sp.wait_ge(s_set, 5)
                for j in range(PROLOGUE_CH):
                    tile, h0 = j % CH // 2, 2 * (j % 2)
                    write_band(j, j // CH, tile, h0)
                    if j:
                        p = j - 1
                        read_band(16 * (p // 2 + 1), p // CH, p % CH // 2, 2 * (p % 2))
                p = PROLOGUE_CH - 1
                read_band(16 * (p // 2 + 1), p // CH, p % CH // 2, 2 * (p % 2))
                load_minus_max(0, 0)
                with sp.Fori(0, LOOPS) as i:
                    for k in range(UNROLL):
                        step(i * UNROLL + k, k)
                step(G - 2, G - 2, ahead=False)
                step(G - 1, G - 1, look=False, ahead=False)

            @block.gpsimd
            def _(pool):
                nc.gpsimd.memset(no_band, 0.0).then_inc(s_set, 1)
                pool.wait_ge(s_set, 1)
                for a in range(2):
                    nc.gpsimd.memset(band[:, a, 0, :, 0, 0:HALF], 0.0).then_inc(s_set, 1)
                    nc.gpsimd.memset(band[:, a, NT - 1, :, 1, HALF:P], 0.0).then_inc(s_set, 1)
                pool.wait_ge(s_set, 5)
                for a in range(KBUF):
                    nc.gpsimd.memset(keys[ROWS:QROWS, a], 1.0).then_inc(s_set, 1)
                pool.wait_ge(s_set, 5 + KBUF)
                nc.gpsimd.memset(token[:, 0:1], 0.0).then_inc(s_norm, 2)
                nc.gpsimd.memset(token[:, 2:3], 0.0).then_inc(s_ws, 1)
                nc.gpsimd.memset(token[:, 1:2], 0.0).then_inc(s_hofree, IP)

                def step(s):
                    for pair in range(IP):
                        pool.wait_ge(s_norm, s * IP + (pair + 3))
                        pool.dma_start(o_scr[s][:, pair * 2 * P:(pair + 1) * 2 * P],
                                       heads_out[:, pair]).then_inc(s_ho[pair], 16)
                        wait_apart(pool, (s_ho[pair], s * 16 + 16))
                        nc.gpsimd.memset(token[:, 1:2], 0.0).then_inc(s_hofree, 1)
                        pool.wait_ge(s_hofree, s * IP + (pair + IP + 1))

                with pool.Fori(0, G) as i:
                    step(i)

            @block.scalar
            def _(act):
                def copy_band(count, written):
                    act.wait_ge(s_bp, count + 1)
                    if written is not None:
                        act.wait_ge(s_bw[written[0]], written[1])

                def copy_sums(s, pair):
                    act.wait_ge(s_av, s * IP + (pair + 1))
                    act.wait_ge(s_norm, s * IP + (pair + 1))
                    nc.scalar.activation(weighted_s[:, pair % 2], sum_ps[:], ACT.Copy).then_inc(s_ws, 1)

                def step(s, k, look=True, ahead=True):
                    for u in range(UNITS):
                        act.wait_ge(s_sc, s * UNITS + (u + 1))
                        nc.scalar.activation(probs[:, u % 2], weigh_ps[u % 2][:], ACT.Exp).then_inc(s_pr, 1)
                        if u and u % NT == 0:
                            copy_sums(s, u // NT - 1)
                        for j, slot in enumerate(CHUNK_SLOT):
                            if slot == u and (look if chunk_of(j)[0] == 1 else ahead):
                                copy_band(s * CH + (PROLOGUE_CH + j),
                                          (j % 2, s * (8 * CH) + 16 * (PROLOGUE_CH // 2 + j // 2)))
                                nc.scalar.activation(band_out[:, j % 2], band_ps[:], ACT.Copy).then_inc(s_be, 1)
                    copy_sums(s, IP - 1)

                for j in range(PROLOGUE_CH):
                    copy_band(j, (j % 2, 16 * (j // 2)) if j >= 2 else None)
                    nc.scalar.activation(band_out[:, j % 2], band_ps[:], ACT.Copy).then_inc(s_be, 1)
                with act.Fori(0, LOOPS) as i:
                    for k in range(UNROLL):
                        step(i * UNROLL + k, k)
                step(G - 2, G - 2, ahead=False)
                step(G - 1, G - 1, look=False, ahead=False)

            @block.vector
            def _(dve):
                def look(s, k, item):
                    tile, h = item // HG, item % HG
                    count = s * ITEMS + (item + 1)
                    col = h * NT + tile
                    wait_apart(dve, (s_look[0], count), (s_b[tile], (s + 1) * BAND_READS[tile]))
                    mine = band[:, k % 2, tile, h]
                    bias = flat(mine, 0, [mine.ap[0], [no_band.offset - mine.offset, 2], [1, 2 * P]])
                    both = look_ps[0][:].rearrange("p (a c) -> p a c", a=2)
                    nc.vector.tensor_tensor_reduce(
                        out=both, in0=both, in1=bias, scale=1.0, scalar=LOWEST, op0=ALU.add, op1=ALU.max,
                        accum_out=partial_max[:, 0, col:col + 1]).then_inc(s_seen[0], 1)
                    dve.wait_ge(s_look[1], count)
                    nc.vector.reduce_max(partial_max[:, 1, col:col + 1], look_ps[1][:], AX_X).then_inc(s_seen[1], 1)

                def finish_max(s):
                    count = s + 1
                    dve.wait_ge(s_seen[1], s * ITEMS + ITEMS)
                    nc.vector.tensor_reduce(row_max[:], partial_max[:].rearrange("p a i -> p i a"), AX_X,
                                            ALU.max).then_inc(s_rm, 1)
                    dve.wait_ge(s_rmT, count)
                    nc.vector.tensor_scalar(minus_max[:, 0, :], look_ps[0][0:ITEMS, 0:P], -1.0, None,
                                            ALU.mult).then_inc(s_hi, 1)
                    dve.wait_ge(s_hi, count)
                    nc.vector.scalar_tensor_tensor(out=minus_max[:, 1, :], in0=look_ps[0][0:ITEMS, 0:P], scalar=-1.0,
                                                   in1=minus_max[:, 0, :], op0=ALU.mult,
                                                   op1=ALU.subtract).then_inc(s_mm, 1)

                def divide(s, pair):
                    count = s * IP + (pair + 1)
                    wait_apart(dve, (s_ws, s * IP + (pair + 2)))
                    nc.vector.stream_shuffle(sums[:], weighted_s[:, pair % 2], [D] * 32).then_inc(s_sum, 1)
                    dve.wait_ge(s_sum, count)
                    nc.vector.reciprocal(inverse[:], sums[:]).then_inc(s_inv, 1)
                    dve.wait_ge(s_inv, count)
                    dve.wait_ge(s_hofree, count)
                    nc.vector.tensor_tensor(heads_out[:, pair], weighted_s[:, pair % 2], inverse[:],
                                            ALU.mult).then_inc(s_norm, 1)

                def step(s, k, look_on=True, ahead=True):
                    for u in range(UNITS):
                        if look_on:
                            for item in items_at(u):
                                look(s + 1, k + 1, item)
                        if u >= NT and u % NT == 2:
                            divide(s, u // NT - 1)
                    if look_on:
                        finish_max(s + 1)
                    divide(s, IP - 1)

                for item in range(ITEMS):
                    look(0, 0, item)
                finish_max(0)
                with dve.Fori(0, LOOPS) as i:
                    for k in range(UNROLL):
                        step(i * UNROLL + k, k)
                step(G - 2, G - 2)
                step(G - 1, G - 1, look_on=False)

            @block.tensor
            def _(pe):
                def band_product(count, k, tile, h0, first=False):
                    if not first:
                        pe.wait_ge(s_be, count)
                    for h in range(2):
                        last = nc.tensor.matmul(band_ps[:, h], queries[0:ROWS, k % 2, h0 + h, tile * P:(tile + 1) * P],
                                                rel_terms[:], start=True, stop=True)
                    last.then_inc(s_bp, 1)

                def look(s, k, item, half, first=False):
                    tile, h = item // HG, item % HG
                    if not first:
                        pe.wait_ge(s_seen[half], s * ITEMS + item)
                    for bank, col, kind, n, tiles in look_pieces(tile):
                        if bank == half:
                            last = nc.tensor.matmul(look_ps[half][:, col:col + tiles * P],
                                                    queries[0:ROWS, k % 2, h, tile * P:(tile + 1) * P],
                                                    keys[0:ROWS, k % KBUF, kind, h, n * P:(n + tiles) * P],
                                                    start=True, stop=True)
                    last.then_inc(s_look[half], 1)

                def turn_max(s):
                    pe.wait_ge(s_rm, s + 1)
                    nc.tensor.transpose(look_ps[0][0:ITEMS, 0:P], row_max[:], ident[:]).then_inc(s_rmT, 1)

                def scores(s, k, u):
                    pair, n = u // NT, u % NT
                    for h in range(HG):
                        dst = weigh_ps[u % 2][:, h]
                        started = False
                        for e in range(2):
                            tile = 2 * pair + e
                            side = (n - tile) % NT
                            if side < 2:
                                nc.tensor.matmul(dst[:, e * P:(e + 1) * P], band[:, k % 2, tile, h, side], ident[:],
                                                 is_transpose=True, start=not started, stop=False,
                                                 skip_group_check=True)
                                started = True
                        kinds = [key_kind(n, 2 * pair + e) for e in range(2)]
                        spans = [(0, 2, kinds[0])] if kinds[0] == kinds[1] else [(0, 1, kinds[0]), (1, 2, kinds[1])]
                        for e0, e1, kind in spans:
                            last = nc.tensor.matmul(dst[:, e0 * P:e1 * P], keys[:, k % KBUF, kind, h, n * P:(n + 1) * P],
                                                    queries[:, k % 2, h, (2 * pair + e0) * P:(2 * pair + e1) * P],
                                                    start=not started, stop=(e1 == 2), skip_group_check=True)
                            started = True
                    last.then_inc(s_sc, 1)

                def weighted(s, k, u):
                    pair, n = u // NT, u % NT
                    pe.wait_ge(s_pr, s * UNITS + (u + 1))
                    if n == 0:
                        pe.wait_ge(s_ws, s * IP + (pair + 1))
                    for h in range(HG):
                        last = nc.tensor.matmul(sum_ps[h * PAD:(h + 1) * PAD, :],
                                                values[:, k % 2, n, h * PAD:(h + 1) * PAD], probs[:, u % 2, h],
                                                start=(n == 0), stop=(n == NT - 1), tile_position=(0, h * PAD))
                    if n == NT - 1:
                        last.then_inc(s_av, 1)

                def step(s, k, look_on=True, ahead=True):
                    pe.wait_ge(s_min[k % 2], (s + (2 - k % 2)) * 16)
                    pe.wait_ge(s_v[k % 2], (s + (2 - k % 2)) * 8)
                    for u in range(UNITS):
                        scores(s, k, u)
                        if look_on:
                            if u == 0:
                                pe.wait_ge(s_keys[(k + 1) % KBUF], key_count(s + 1, k + 1))
                            for item in items_at(u):
                                if item % (2 * HG) == 0:
                                    pair = item // (2 * HG)
                                    pe.wait_ge(s_q[(k + 1) % 2][pair], query_count(s + 1, k + 1))
                                look(s + 1, k + 1, item, 0)
                                if item != items_at(u)[-1]:
                                    look(s + 1, k + 1, item, 1)
                        for j, slot in enumerate(CHUNK_SLOT):
                            d, tile, h0 = chunk_of(j)
                            if slot == u and (look_on if d == 1 else ahead):
                                if j % 4 == 0:
                                    pe.wait_ge(s_q[(k + d) % 2][tile // 2], query_count(s + d, k + d))
                                band_product(s * CH + (PROLOGUE_CH + j), k + d, tile, h0)
                        if u:
                            weighted(s, k, u - 1)
                        if look_on and items_at(u):
                            look(s + 1, k + 1, items_at(u)[-1], 1)
                        if look_on and u == UNITS - 2:
                            turn_max(s + 1)
                    weighted(s, k, UNITS - 1)

                def query_count(s, k):
                    return (s - k % 2 + 2) * (16 * TERMS // 2)

                def key_count(s, k):
                    return (s - k % KBUF + KBUF) * (16 * 2 * TERMS // KBUF)

                pe.wait_ge(s_set, 5 + KBUF)
                for j in range(PROLOGUE_CH):
                    tile, h0 = j % CH // 2, 2 * (j % 2)
                    if j % 4 == 0:
                        pe.wait_ge(s_q[j // CH][tile // 2], 16 * TERMS)
                    band_product(j, j // CH, tile, h0, first=(j == 0))
                    if j == 0:
                        pe.wait_ge(s_keys[0], 16 * 2 * TERMS)
                for item in range(ITEMS):
                    for half in range(2):
                        look(0, 0, item, half, first=(item == 0))
                turn_max(0)
                with pe.Fori(0, LOOPS) as i:
                    for k in range(UNROLL):
                        step(i * UNROLL + k, k)
                step(G - 2, G - 2, ahead=False)
                step(G - 1, G - 1, look_on=False, ahead=False)

        with ExitStack() as ctx:
            def sb(name, shape, dt):
                return sb_in(ctx, name, shape, dt)

            def sem(name):
                return sem_in(ctx, name)

            TOK = 512
            TT = TOK // P
            IT = B * T // TOK
            assert T == 2 * TOK and IT >= 4

            heads = sb("heads", [P, 2, NG, TOK], F32)
            x_in = sb("x_in", [P, 2, TT, E], F32)
            x_bo = sb("x_bo", [P, 2, TT, E], F32)
            y = sb("y", [P, TT, E], F32)
            x1 = sb("x1", [P, 2, TT, E], F32)
            x1_b2 = sb("x1_b2", [P, 2, TT, E], F32)
            x1T = sb("x1T", [P, 2, KE, TOK], F32)
            hidden = sb("hidden", [P, KH, TOK], F32)
            z = sb("z", [P, TT, E], F32)
            fin = sb("fin", [P, 2, TT, E], F32)
            stats = sb("stats", [P, 2 * TT, 6], F32)
            mean_var = sb("mean_var", [P, 2 * TT, 2], F32)
            std = sb("std", [P, 2 * TT], F32)
            rstd = sb("rstd", [P, 2 * TT], F32)

            att_ps = ctx.enter_context(nc.psum_tensor("att_ps", [P, TT, E], F32))
            turn_ps = ctx.enter_context(nc.psum_tensor("turn_ps", [P, KE, TOK], F32))
            hid_ps = [ctx.enter_context(nc.psum_tensor(f"hid_ps{a}", [P, TOK], F32)) for a in range(2)]
            out_ps = ctx.enter_context(nc.psum_tensor("out_ps", [P, TT, E], F32))

            s_set = sem("stats_set")
            s_passed = sem("waits_passed3")
            s_heads = [sem(f"heads_in{a}") for a in range(2)]
            s_x = [sem(f"residual_in{a}") for a in range(2)]
            s_xb = sem("residual_with_bias")
            s_att = sem("projection_ready")
            s_y = sem("y_ready")
            s_yst = sem("y_stats")
            s_zp = sem("z_scaled")
            s_z = sem("z_ready")
            s_zst = sem("z_stats")
            s_mv = sem("mean_var_ready")
            s_sd = sem("std_ready")
            s_rs = sem("rstd_ready")
            s_x1 = sem("x1_ready")
            s_x1b = sem("x1_with_bias")
            s_turn = sem("x1_turned")
            s_x1T = sem("x1T_ready")
            s_h = sem("hidden_product")
            s_hid = sem("hidden_ready")
            s_ff = sem("out_product")
            s_fin = sem("fin_ready")
            s_out = [sem(f"out_stored{a}") for a in range(2)]

            x_rows = x.rearrange("b t e -> (b t) e")
            out_rows = out.rearrange("b t e -> (b t) e")
            INNER = (IT - 2) // 2
            block = ctx.enter_context(nc.Block())

            @block.sync
            def _(sp):
                def load(it, b, a, first=False):
                    if not first:
                        sp.wait_ge(s_att, it - 1)
                        sp.wait_ge(s_xb, it - 1)
                    sp.dma_start(heads[:, a], o_scr[bass.ds(b * NG, NG), :, a * TOK:(a + 1) * TOK]
                                 .rearrange("g p t -> p g t")).then_inc(s_heads[a], 16)
                    sp.dma_start(x_in[:, a], x_rows[bass.ds(it * TOK, TOK), :]
                                 .rearrange("(j p) e -> p j e", p=P)).then_inc(s_x[a], 16)

                load(0, 0, 0, first=True)
                load(1, 0, 1, first=True)
                with sp.Fori(0, B - 1) as i:
                    for a in range(2):
                        load(i * 2 + (2 + a), i + 1, a)

            @block.gpsimd
            def _(pool):
                for a in range(2):
                    nc.gpsimd.memset(fin[:, a, 0, 0:1], 0.0).then_inc(s_out[a], 16)
                nc.gpsimd.memset(y[:, 0, 0:1], 0.0).then_inc(s_fin, 1)
                nc.gpsimd.memset(mean_var[:], 1.0).then_inc(s_set, 1)

                def residual(it, a, wait=True):
                    pool.wait_ge(s_x[a], (it + (2 - a)) * 8)
                    if wait:
                        pool.wait_ge(s_y, it - 1)
                    nc.gpsimd.tensor_tensor(x_bo[:, a], x_in[:, a], over(bo_row[:], TT, 1), ALU.add).then_inc(s_xb, 1)

                def skip(it, a):
                    pool.wait_ge(s_x1, it + 1)
                    nc.gpsimd.tensor_tensor(x1_b2[:, a], x1[:, a], over(b2_row[:], TT, 1), ALU.add).then_inc(s_x1b, 1)

                residual(0, 0, wait=False)
                residual(1, 1, wait=False)
                skip(0, 0)
                with pool.Fori(0, INNER) as i:
                    for a in (1, 0):
                        it = i * 2 + (1 if a else 2)
                        residual(it + 1, 1 - a)
                        skip(it, a)
                skip(IT - 1, 1)

            @block.vector
            def _(dve):
                def norms(n, z_of=None, y_of=None):
                    if z_of is not None:
                        it, a = z_of
                        dve.wait_ge(s_ff, it + 1)
                        dve.wait_ge(s_fin, it + 1)
                        nc.vector.tensor_tensor(z[:], out_ps[:], over(alpha2_row[:], TT, 1), ALU.mult).then_inc(s_zp, 1)
                        dve.wait_ge(s_zp, it + 1)
                        dve.wait_ge(s_x1b, it + 1)
                        nc.vector.tensor_tensor(z[:], z[:], x1_b2[:, a], ALU.add).then_inc(s_z, 1)
                        dve.wait_ge(s_z, it + 1)
                        for t in range(TT):
                            last = nc.vector.bn_stats(stats[:, TT + t, :], z[:, t])
                        last.then_inc(s_zst, 1)
                    if y_of is not None:
                        it, a = y_of
                        dve.wait_ge(s_att, it + 1)
                        dve.wait_ge(s_xb, it + 1)
                        if z_of is not None or n > 0:
                            dve.wait_ge(s_x1, it)
                        nc.vector.tensor_tensor(y[:], att_ps[:], x_bo[:, a], ALU.add).then_inc(s_y, 1)
                        dve.wait_ge(s_y, it + 1)
                        for t in range(TT):
                            last = nc.vector.bn_stats(stats[:, t, :], y[:, t])
                        last.then_inc(s_yst, 1)
                    if z_of is not None:
                        dve.wait_ge(s_zst, z_of[0] + 1)
                    if y_of is not None:
                        dve.wait_ge(s_yst, y_of[0] + 1)
                    dve.sem_inc(s_passed, 1)
                    cols = range(0 if y_of is not None else TT, 2 * TT if z_of is not None else TT)
                    for t in cols:
                        last = nc.vector.bn_aggr(mean_var[:, t, :], stats[:, t, :])
                    last.then_inc(s_mv, 1)
                    dve.wait_ge(s_sd, n + 1)
                    nc.vector.reciprocal(rstd[:], std[:]).then_inc(s_rs, 1)
                    dve.wait_ge(s_rs, n + 1)
                    if y_of is not None:
                        it, a = y_of
                        for t in range(TT):
                            last = nc.vector.tensor_scalar(x1[:, a, t], y[:, t], mean_var[:, t, 0:1], rstd[:, t:t + 1],
                                                           ALU.subtract, ALU.mult)
                        last.then_inc(s_x1, 1)
                    if z_of is not None:
                        it, a = z_of
                        dve.wait_ge(s_out[a], (it + (2 - a)) * 8)
                        for t in range(TT):
                            last = nc.vector.tensor_scalar(fin[:, a, t], z[:, t], mean_var[:, TT + t, 0:1],
                                                           rstd[:, TT + t:TT + t + 1], ALU.subtract, ALU.mult)
                        last.then_inc(s_fin, 1)

                dve.wait_ge(s_set, 1)
                norms(0, y_of=(0, 0))
                norms(1, y_of=(1, 1))
                with dve.Fori(0, INNER) as i:
                    for a in (1, 0):
                        it = i * 2 + (1 if a else 2)
                        norms(it + 1, z_of=(it - 1, 1 - a), y_of=(it + 1, 1 - a))
                norms(IT, z_of=(IT - 2, 0))
                norms(IT + 1, z_of=(IT - 1, 1))

            @block.scalar
            def _(act):
                def roots(n):
                    act.wait_ge(s_mv, n + 1)
                    nc.scalar.activation(std[:], mean_var[:, :, 1], ACT.Sqrt, bias=eps_col[:, 0:1]).then_inc(s_sd, 1)

                def gelus(it):
                    for j in range(KH):
                        act.wait_ge(s_h, it * KH + (j + 1))
                        nc.scalar.activation(hidden[:, j], hid_ps[j % 2][:], ACT.Gelu, bias=b1_col[:, j:j + 1],
                                             scale=alpha1[:, j:j + 1]).then_inc(s_hid, 1)

                def copy_turned(it, a):
                    act.wait_ge(s_turn, it + 1)
                    nc.scalar.activation(x1T[:, a], turn_ps[:], ACT.Copy).then_inc(s_x1T, 1)

                def store(it, a):
                    act.wait_ge(s_fin, it + 2)
                    act.dma_start(out_rows[bass.ds(it * TOK, TOK), :].rearrange("(j p) e -> p j e", p=P),
                                  fin[:, a]).then_inc(s_out[a], 16)

                roots(0)
                copy_turned(0, 0)
                gelus(0)
                roots(1)
                copy_turned(1, 1)
                with act.Fori(0, INNER) as i:
                    for a in (1, 0):
                        it = i * 2 + (1 if a else 2)
                        gelus(it)
                        roots(it + 1)
                        copy_turned(it + 1, 1 - a)
                        store(it - 1, 1 - a)
                gelus(IT - 1)
                roots(IT)
                store(IT - 2, 0)
                roots(IT + 1)
                store(IT - 1, 1)
                for a in range(2):
                    act.wait_ge(s_out[a], 16 + 16 * IT // 2)

            @block.tensor
            def _(pe):
                def project(it, a, first=False):
                    pe.wait_ge(s_heads[a], (it + (2 - a)) * 8)
                    if not first:
                        pe.wait_ge(s_y, it)
                    for t in range(TT):
                        for g in range(NG):
                            last = nc.tensor.matmul(att_ps[:, t], heads[:, a, g, t * P:(t + 1) * P], wo_pad[:, g],
                                                    start=(g == 0), stop=(g == NG - 1))
                    last.then_inc(s_att, 1)

                def turn(it, a):
                    pe.wait_ge(s_x1, it + 1)
                    for kt in range(KE):
                        for t in range(TT):
                            last = nc.tensor.transpose(turn_ps[:, kt, t * P:(t + 1) * P],
                                                       x1[:, a, t, kt * P:(kt + 1) * P], ident[:])
                    last.then_inc(s_turn, 1)

                def layer1(it, a, first=False):
                    pe.wait_ge(s_x1T, it + 1)
                    for j in range(KH):
                        if not (first and j < 2):
                            pe.wait_ge(s_hid, it * KH + (j - 1))
                        for kt in range(KE):
                            last = nc.tensor.matmul(hid_ps[j % 2][:], sign1T[:, kt, j * P:(j + 1) * P], x1T[:, a, kt],
                                                    start=(kt == 0), stop=(kt == KE - 1))
                        last.then_inc(s_h, 1)

                def layer2(it, tiles, first=False):
                    if 0 in tiles:
                        pe.wait_ge(s_hid, it * KH + KH)
                        if not first:
                            pe.wait_ge(s_zp, it)
                    for t in tiles:
                        for j in range(KH):
                            last = nc.tensor.matmul(out_ps[:, t], hidden[:, j, t * P:(t + 1) * P], sign2T[:, j],
                                                    start=(j == 0), stop=(j == KH - 1))
                    if TT - 1 in tiles:
                        last.then_inc(s_ff, 1)

                def iteration(it, a, first=False, last=False):
                    layer1(it, a, first)
                    if not last:
                        project(it + 1, 1 - a)
                    layer2(it, range(0, TT - 1), first)
                    if not last:
                        turn(it + 1, 1 - a)
                    layer2(it, range(TT - 1, TT))

                project(0, 0, first=True)
                turn(0, 0)
                iteration(0, 0, first=True)
                with pe.Fori(0, INNER) as i:
                    for a in (1, 0):
                        iteration(i * 2 + (1 if a else 2), a)
                iteration(IT - 1, 1, last=True)


_INS = ['L0_attn_q', 'L0_attn_in_proj_weight', 'L0_attn_in_proj_bias', 'L0_attn_out_w', 'L0_attn_out_b',
        'L0_attn_rel_pe', 'L0_ffn_w1', 'L0_ffn_b1', 'L0_ffn_w2', 'L0_ffn_b2']
_OUTS = [((8, 1024, 256), 'float32')]


def kernel(**inputs):
    import numpy as _np
    import concourse.bacc as _bacc
    from concourse import mybir as _mybir
    from concourse.bass_utils import run_bass_kernel_spmd as _run

    nc = _bacc.Bacc("TRN2", target_bir_lowering=False, num_devices=1)
    arrays, args = {}, []
    for name in _INS:
        a = _np.ascontiguousarray(inputs[name])
        arrays[f"in_{name}_dram"] = a
        args.append(nc.dram_tensor(f"in_{name}_dram", a.shape, _mybir.dt.from_np(a.dtype), kind="ExternalInput").ap())
    for i, (shape, dtype) in enumerate(_OUTS):
        dt = _mybir.dt.from_np(_np.dtype(dtype))
        args.append(nc.dram_tensor(f"out_{i}_dram", shape, dt, kind="ExternalOutput").ap())
    post_ln_block(nc, *args)
    r = _run(nc, [arrays], core_ids=[0])
    got = tuple(r.results[0][f"out_{i}_dram"] for i in range(len(_OUTS)))
    return got[0]
```

```python
from contextlib import ExitStack

import concourse.bass as bass
from concourse import mybir

F32 = mybir.dt.float32
BF16 = mybir.dt.bfloat16
ALU = mybir.AluOpType
ACT = mybir.ActivationFunctionType
AX_X = mybir.AxisListType.X

P = 128
TERM_Q = (0, 0, 1, 0, 2, 1)
TERM_K = (0, 1, 0, 2, 0, 1)
TERMS = len(TERM_Q)
PARTS = 3
LOWEST = -3.0e38


def flat(ap, offset, dims):
    return bass.AP(tensor=ap.tensor, offset=ap.offset + offset, ap=[list(d) for d in dims])


def over(ap, count, at):
    dims = [list(d) for d in ap.ap]
    return bass.AP(tensor=ap.tensor, offset=ap.offset, ap=dims[:at] + [[0, count]] + dims[at:])


def post_ln_block(nc, x, w_in, b_in, w_out, b_out, rel, w1, b1, w2, b2, out):
    B, T, E = x.shape
    R, D = rel.shape
    H = E // D
    HID = w1.shape[0]
    REACH = R // 2
    NT = T // P
    HG = 4
    NG = H // HG
    G = B * NG
    KE = E // P
    KH = HID // P
    PAD = 32
    HALF = REACH
    ROWS = TERMS * D
    QROWS = ROWS + 2
    EPS = 1e-5
    assert R == P + 1 and D * HG * 2 == P and KE == 2 and T % 512 == 0

    outer = ExitStack()
    with outer:
        def sem_in(ctx, name):
            return ctx.enter_context(nc.semaphore(name))

        def sb_in(ctx, name, shape, dt):
            return ctx.enter_context(nc.sbuf_tensor(name, shape, dt))

        split_scr = nc.dram_tensor("split_scr", [3, PARTS, G, HG * D, T], BF16).ap()
        v_scr = nc.dram_tensor("v_scr", [G, P, NT, HG * PAD], F32).ap()
        BAND_ROW = 3 * P
        band_scr = nc.dram_tensor("band_scr", [2 * HG * NT * P + 1, BAND_ROW], F32).ap()
        o_scr = nc.dram_tensor("o_scr", [B, H, D + 1, T], F32).ap()

        inverse_scr = nc.dram_tensor("inverse_scr", [B * T // 512, H, 512], F32).ap()

        ident = sb_in(outer, "ident", [P, P], F32)
        woT = sb_in(outer, "woT", [P, KE, E], F32)
        sign1T = sb_in(outer, "sign1T", [P, KE, HID], BF16)
        sign2T = sb_in(outer, "sign2T", [P, KH, E], BF16)
        alpha1 = sb_in(outer, "alpha1", [P, KH], F32)
        b1_col = sb_in(outer, "b1_col", [P, KH], F32)
        alpha2_row = sb_in(outer, "alpha2_row", [P, E], F32)
        bo_row = sb_in(outer, "bo_row", [P, E], F32)
        b2_row = sb_in(outer, "b2_row", [P, E], F32)
        rel_terms = sb_in(outer, "rel_terms", [ROWS, 2 * P], BF16)
        eps_col = sb_in(outer, "eps_col", [P, 1], F32)

        with ExitStack() as ctx:
            def sb(name, shape, dt):
                return sb_in(ctx, name, shape, dt)

            def sem(name):
                return sem_in(ctx, name)

            wT = sb("wT", [P, KE, 3 * E], F32)
            bq_col = sb("bq_col", [P, 2], F32)
            bk_left = sb("bk_left", [P, 2], F32)
            bk_right = sb("bk_right", [P, 2], F32)
            bv_row = sb("bv_row", [P, E], F32)
            bank = [ctx.enter_context(nc.psum_tensor(f"bank{i}", [P, 512], F32)) for i in range(8)]

            with ExitStack() as c0:
                w_in_s = sb_in(c0, "w_in_s", [P, 6, E], F32)
                w_out_s = sb_in(c0, "w_out_s", [P, 2, E], F32)
                w1_s = sb_in(c0, "w1_s", [P, KH, E], F32)
                w2_s = sb_in(c0, "w2_s", [P, 2, HID], F32)
                sgn1 = sb_in(c0, "sgn1", [P, KH, E], F32)
                sgn2 = sb_in(c0, "sgn2", [P, 2, HID], F32)
                junk1 = sb_in(c0, "junk1", [P, KH, E], F32)
                junk2 = sb_in(c0, "junk2", [P, 2, HID], F32)
                b_col = sb_in(c0, "b_col", [P, 4], F32)
                rel_ends = sb_in(c0, "rel_ends", [P, 2], F32)
                relT = sb_in(c0, "relT", [D, R], F32)
                rel_d = sb_in(c0, "rel_d", [D, 2 * P], F32)
                rel_r = sb_in(c0, "rel_r", [D, 2 * P], F32)
                rel_parts = sb_in(c0, "rel_parts", [D, PARTS, 2 * P], BF16)
                alpha2 = sb_in(c0, "alpha2", [P, 2], F32)
                alpha2_wide = sb_in(c0, "alpha2_wide", [P, 2, P], F32)
                zeros = sb_in(c0, "zeros", [P, HG * NT, P], F32)
                s_w = sem_in(c0, "weights_in")
                s_small = sem_in(c0, "small_in")
                s_set = sem_in(c0, "pool_set")
                s_sgn = sem_in(c0, "signs_ready")
                s_dve = sem_in(c0, "dve_chain")
                s_rel = sem_in(c0, "rel_parts_ready")
                s_relt = sem_in(c0, "rel_terms_in")
                s_zero = sem_in(c0, "pads_zeroed")
                s_src = sem_in(c0, "sources_ready")
                s_tr = sem_in(c0, "transposed")
                s_eva = sem_in(c0, "evacuated_act")
                s_evd = sem_in(c0, "evacuated_dve")

                jobs = []
                for kt in range(KE):
                    for j0, nj in ((0, 4), (4, 2)):
                        jobs.append(([w_in_s[:, j, kt * P:(kt + 1) * P] for j in range(j0, j0 + nj)],
                                     wT[:, kt, j0 * P:(j0 + nj) * P]))
                for kt in range(KE):
                    for j0 in range(0, KH, 4):
                        jobs.append(([sgn1[:, j, kt * P:(kt + 1) * P] for j in range(j0, j0 + 4)],
                                     sign1T[:, kt, j0 * P:(j0 + 4) * P]))
                for kt in range(0, KH, 2):
                    jobs.append(([sgn2[:, j, k * P:(k + 1) * P] for k in (kt, kt + 1) for j in range(2)],
                                 sign2T[:, kt:kt + 2, :].rearrange("p a b -> p (a b)")))
                jobs.append(([w_out_s[:, j, k * P:(k + 1) * P] for k in range(KE) for j in range(2)],
                             woT[:].rearrange("p a b -> p (a b)")))
                jobs.append(([alpha2_wide[:, j, :] for j in range(2)], alpha2_row[:, :]))

                block = c0.enter_context(nc.Block())

                @block.sync
                def _(sp):
                    sp.dma_start(w_in_s[:], w_in.rearrange("(j p) e -> p j e", p=P)).then_inc(s_w, 16)
                    sp.dma_start(w1_s[:], w1.rearrange("(j p) e -> p j e", p=P)).then_inc(s_w, 16)
                    sp.dma_start(w2_s[:], w2.rearrange("(j p) e -> p j e", p=P)).then_inc(s_w, 16)
                    sp.dma_start(w_out_s[:], w_out.rearrange("(j p) e -> p j e", p=P)).then_inc(s_w, 16)
                    sp.wait_ge(s_set, 1)
                    for a in range(2):
                        sp.dma_start(flat(band_scr, a * HG * NT * P * BAND_ROW,
                                          [[BAND_ROW, P], [P * BAND_ROW, HG * NT], [1, P]]),
                                     zeros[:]).then_inc(s_zero, 16)
                    sp.dma_start(band_scr[2 * HG * NT * P:, 0:P], zeros[0:1, 0]).then_inc(s_zero, 16)
                    sp.wait_ge(s_rel, 3)
                    for t in range(TERMS):
                        sp.dma_start(rel_terms[t * D:(t + 1) * D, :],
                                     rel_parts[:, TERM_K[t], :]).then_inc(s_relt, 16)
                    sp.wait_ge(s_relt, 16 * TERMS)
                    sp.wait_ge(s_zero, 16 * 3)

                @block.scalar
                def _(act):
                    act.dma_start(b_col[:], b_in[0:2 * E].rearrange("(j p) -> p j", p=P),
                                  allow_slow_non_contiguous=True).then_inc(s_small, 16)
                    act.dma_start(b1_col[:], b1.rearrange("(j p) -> p j", p=P),
                                  allow_slow_non_contiguous=True).then_inc(s_small, 16)
                    act.dma_start(relT[:], rel.rearrange("r d -> d r"),
                                  allow_slow_non_contiguous=True).then_inc(s_small, 16)
                    for n, r in enumerate((0, R - 1)):
                        for h in range(P // D):
                            act.dma_start(rel_ends[h * D:(h + 1) * D, n:n + 1],
                                          flat(rel, r * D, [[1, D], [1, 1]]),
                                          allow_slow_non_contiguous=True).then_inc(s_small, 16)
                    act.dma_start(bv_row[:], flat(b_in, 2 * E, [[0, P], [1, E]])).then_inc(s_small, 16)
                    act.dma_start(bo_row[:], flat(b_out, 0, [[0, P], [1, E]])).then_inc(s_small, 16)
                    act.dma_start(b2_row[:], flat(b2, 0, [[0, P], [1, E]])).then_inc(s_small, 16)
                    act.wait_ge(s_w, 64)
                    nc.scalar.activation(sgn1[:], w1_s[:], ACT.Sign).then_inc(s_sgn, 1)
                    nc.scalar.activation(sgn2[:], w2_s[:], ACT.Sign).then_inc(s_sgn, 1)
                    for n, (src, dst) in enumerate(jobs):
                        if n % 2 == 0:
                            act.wait_ge(s_tr, n + 1)
                            nc.scalar.activation(dst, bank[n % 8][:, 0:len(src) * P],
                                                 ACT.Copy).then_inc(s_eva, 1)

                @block.gpsimd
                def _(pool):
                    nc.gpsimd.memset(zeros[:], 0.0).then_inc(s_set, 1)
                    nc.gpsimd.memset(ident[:], 0.0).then_inc(s_set, 1)
                    nc.gpsimd.memset(eps_col[:], EPS).then_inc(s_set, 1)
                    pool.wait_ge(s_set, 2)
                    nc.gpsimd.affine_select(out=ident[:], in_=ident[:], compare_op=ALU.not_equal, fill=1.0,
                                            base=0, pattern=[[-1, P]], channel_multiplier=1).then_inc(s_set, 1)

                @block.vector
                def _(dve):
                    dve.wait_ge(s_small, 16 * (6 + 2 * (P // D)))
                    nc.vector.tensor_scalar(bq_col[:], b_col[:, 0:2], float(D) ** -0.5, None, ALU.mult)
                    nc.vector.tensor_scalar(bk_left[:], b_col[:, 2:4], rel_ends[:, 0:1], None, ALU.add)
                    nc.vector.tensor_scalar(bk_right[:], b_col[:, 2:4], rel_ends[:, 1:2], None, ALU.add)
                    nc.vector.tensor_scalar(rel_d[:, 0:P], relT[:, 0:P], relT[:, 0:1], None,
                                            ALU.subtract).then_inc(s_dve, 1)
                    nc.vector.tensor_scalar(rel_d[:, P:2 * P], relT[:, 0:P], relT[:, R - 1:R], None,
                                            ALU.subtract).then_inc(s_dve, 1)
                    dve.wait_ge(s_dve, 2)
                    nc.vector.tensor_copy(rel_parts[:, 0, :], rel_d[:]).then_inc(s_rel, 1)
                    dve.wait_ge(s_rel, 1)
                    nc.vector.tensor_tensor(rel_r[:], rel_d[:], rel_parts[:, 0, :], ALU.subtract).then_inc(s_dve, 1)
                    dve.wait_ge(s_dve, 3)
                    nc.vector.tensor_copy(rel_parts[:, 1, :], rel_r[:]).then_inc(s_rel, 1)
                    dve.wait_ge(s_rel, 2)
                    nc.vector.tensor_tensor(rel_parts[:, 2, :], rel_r[:], rel_parts[:, 1, :],
                                            ALU.subtract).then_inc(s_rel, 1)
                    dve.wait_ge(s_sgn, 2)
                    for j in range(KH):
                        nc.vector.tensor_tensor_reduce(out=junk1[:, j, :], in0=w1_s[:, j, :], in1=sgn1[:, j, :],
                                                       scale=1.0 / E, scalar=0.0, op0=ALU.mult, op1=ALU.add,
                                                       accum_out=alpha1[:, j:j + 1])
                    for j in range(2):
                        nc.vector.tensor_tensor_reduce(out=junk2[:, j, :], in0=w2_s[:, j, :], in1=sgn2[:, j, :],
                                                       scale=1.0 / HID, scalar=0.0, op0=ALU.mult, op1=ALU.add,
                                                       accum_out=alpha2[:, j:j + 1]).then_inc(s_dve, 1)
                    dve.wait_ge(s_dve, 5)
                    for j in range(2):
                        nc.vector.tensor_copy(alpha2_wide[:, j, :], over(alpha2[:, j], P, 1)).then_inc(s_src, 1)
                    for n, (src, dst) in enumerate(jobs):
                        if n % 2 == 1:
                            dve.wait_ge(s_tr, n + 1)
                            nc.vector.tensor_copy(dst, bank[n % 8][:, 0:len(src) * P]).then_inc(s_evd, 1)

                @block.tensor
                def _(pe):
                    pe.wait_ge(s_set, 4)
                    pe.wait_ge(s_w, 64)
                    for n, (src, dst) in enumerate(jobs):
                        if n == 4:
                            pe.wait_ge(s_sgn, 2)
                        if n == len(jobs) - 1:
                            pe.wait_ge(s_src, 2)
                        if n >= 8:
                            pe.wait_ge(s_evd if n % 2 else s_eva, (n - 8) // 2 + 1)
                        for j, a in enumerate(src):
                            last = nc.tensor.transpose(bank[n % 8][:, j * P:(j + 1) * P], a, ident[:])
                        last.then_inc(s_tr, 1)

            x_s = sb("x_s", [P, 2, NT, E], F32)
            xT = sb("xT", [P, 2, KE, HALF + T], F32)
            whole = sb("whole", [P, 3, 512], F32)
            rest = sb("rest", [P, 2, 512], F32)
            parts = sb("parts", [P, 2, 3, PARTS, 2, T], BF16)
            v_s = sb("v_s", [P, 2, NG, NT, HG, PAD], F32)
            PRODUCTS = 12
            token = sb("token", [P, 4], F32)
            CHUNKS = 12
            STORES = 3 * PARTS + NG
            s_x = [sem(f"x_in{a}") for a in range(2)]
            s_turned = sem("x_turned")
            s_job = sem("product_ready")
            s_xev = sem("xT_ready")
            s_vev = sem("v_ready")
            s_chunk = sem("chunk_ready")
            s_rest = sem("rest_ready")
            s_mid = sem("middle_part_ready")
            s_split = sem("chunk_split")
            s_store = [sem(f"stored{a}") for a in range(2)]
            block = ctx.enter_context(nc.Block())

            @block.gpsimd
            def _(pool):
                nc.gpsimd.memset(token[:, 0:1], 0.0).then_inc(s_turned, 8)
                nc.gpsimd.memset(token[:, 1:2], 0.0).then_inc(s_split, 3)
                nc.gpsimd.memset(token[:, 2:3], 0.0).then_inc(s_chunk, CHUNKS)
                nc.gpsimd.memset(token[:, 3:4], 0.0).then_inc(s_vev, 4)
                nc.gpsimd.memset(v_s[:, 0, :, :, :, D:PAD], 1.0).then_inc(s_store[0], 16 * STORES)
                nc.gpsimd.memset(v_s[:, 1, :, :, :, D:PAD], 1.0).then_inc(s_store[1], 16 * STORES)
                with pool.Fori(0, B // 2) as i:
                    for a in range(2):
                        pool.wait_ge(s_turned, i * 8 + (4 * a + 4))
                        pool.dma_start(x_s[:, a], x[i * 2 + a].rearrange("(j p) e -> p j e", p=P)).then_inc(s_x[a], 16)

            @block.sync
            def _(sp):
                with sp.Fori(0, B // 2) as i:
                    for a in range(2):
                        b = i * 2 + a
                        sp.wait_ge(s_vev, b * 4 + 8)
                        for g in range(NG):
                            sp.dma_start(v_scr[b * NG + g],
                                           v_s[:, a, g].rearrange("p n h d -> p n (h d)")).then_inc(s_store[a], 16)
                        sp.wait_ge(s_split, b * CHUNKS + (3 + CHUNKS))
                        for w in range(3):
                            for c in range(PARTS):
                                dst = split_scr[w, c, bass.ds(b * NG, NG)].rearrange("g r t -> (g r) t")
                                sp.dma_start(dst.rearrange("(m p) t -> p m t", p=P),
                                               parts[:, a, w, c]).then_inc(s_store[a], 16)
                for a in range(2):
                    sp.wait_ge(s_store[a], 16 * STORES * (1 + B // 2))

            @block.tensor
            def _(pe):
                with pe.Fori(0, B // 2) as i:
                    for a in range(2):
                        b = i * 2 + a
                        job = 0

                        def free_bank():
                            if job < 4:
                                pe.wait_ge(s_chunk, b * CHUNKS + (6 + 2 * job))
                            elif job < 8:
                                pe.wait_ge(s_vev, b * 4 + (job - 3))
                            elif job < 12:
                                pe.wait_ge(s_xev, b * 4 + (job - 7))
                            else:
                                pe.wait_ge(s_chunk, b * CHUNKS + (CHUNKS + job - 11))
                            return bank[job % 8]

                        pe.wait_ge(s_x[a], i * 16 + 16)
                        for half in range(2):
                            for kt in range(KE):
                                dst = free_bank()
                                for j in range(4):
                                    last = nc.tensor.transpose(dst[:, j * P:(j + 1) * P],
                                                               x_s[:, a, half * 4 + j, kt * P:(kt + 1) * P], ident[:])
                                last.then_inc(s_turned, 1)
                                job += 1
                        pe.wait_ge(s_xev, b * 4 + 4)
                        for what in range(2):
                            shift = HALF if what == 0 else 0
                            for m in range(2):
                                for half in range(2):
                                    dst = free_bank()
                                    for kt in range(KE):
                                        c0 = shift + half * 512
                                        last = nc.tensor.matmul(dst[:, :],
                                                                wT[:, kt, what * E + m * P:what * E + (m + 1) * P],
                                                                xT[:, a, kt, c0:c0 + 512],
                                                                start=(kt == 0), stop=(kt == KE - 1))
                                    last.then_inc(s_job, 1)
                                    job += 1
                        for n0 in range(0, NT, 2):
                            dst = free_bank()
                            for n in (n0, n0 + 1):
                                for kt in range(KE):
                                    last = nc.tensor.matmul(dst[:, (n - n0) * E:(n - n0 + 1) * E],
                                                            xT[:, a, kt, n * P:(n + 1) * P],
                                                            wT[:, kt, 2 * E:3 * E],
                                                            start=(kt == 0), stop=(kt == KE - 1))
                            last.then_inc(s_job, 1)
                            job += 1

            @block.scalar
            def _(act):
                with act.Fori(0, B // 2) as i:
                    for a in range(2):
                        b = i * 2 + a
                        job = 0
                        for half in range(2):
                            for kt in range(KE):
                                act.wait_ge(s_turned, b * 4 + (8 + job + 1))
                                if half == 1:
                                    nc.scalar.activation(xT[:, a, kt, 0:HALF], bank[job][:, 512 - HALF:512], ACT.Copy)
                                last = nc.scalar.activation(xT[:, a, kt, HALF + half * 512:HALF + (half + 1) * 512],
                                                            bank[job][:, :], ACT.Copy)
                                last.then_inc(s_xev, 1)
                                job += 1
                        act.wait_ge(s_store[a], i * 16 * STORES + 16 * STORES)
                        chunk = 0
                        for what in range(2):
                            for m in range(2):
                                for half in range(2):
                                    act.wait_ge(s_job, b * PRODUCTS + (job - 3))
                                    src = bank[job % 8]
                                    kinds = [(0, [(0, 512, bq_col, float(D) ** -0.5)])] if what == 0 else [
                                        (1, [(0, HALF, bk_right, 1.0), (HALF, 512, bk_left, 1.0)] if half == 0
                                         else [(0, 512, bk_left, 1.0)]),
                                        (2, [(0, 512, bk_right, 1.0)])]
                                    for w, pieces in kinds:
                                        act.wait_ge(s_split, b * CHUNKS + (chunk + 1))
                                        for c0, c1, bias, scale in pieces:
                                            nc.scalar.activation(whole[:, chunk % 3, c0:c1], src[:, c0:c1],
                                                                 ACT.Identity, bias=bias[:, m:m + 1], scale=scale)
                                        for c0, c1, bias, scale in pieces:
                                            last = nc.scalar.activation(
                                                parts[:, a, w, 0, m, half * 512 + c0:half * 512 + c1], src[:, c0:c1],
                                                ACT.Identity, bias=bias[:, m:m + 1], scale=scale)
                                        last.then_inc(s_chunk, 1)
                                        chunk += 1
                                    job += 1

            @block.vector
            def _(dve):
                with dve.Fori(0, B // 2) as i:
                    for a in range(2):
                        b = i * 2 + a
                        dve.wait_ge(s_store[a], i * 16 * STORES + 16 * STORES)
                        chunk = 0
                        for what in range(2):
                            for m in range(2):
                                for half in range(2):
                                    for w in ((0,), (1, 2))[what]:
                                        col = slice(half * 512, (half + 1) * 512)
                                        dve.wait_ge(s_chunk, b * CHUNKS + (CHUNKS + chunk + 1))
                                        nc.vector.tensor_tensor(rest[:, chunk % 2, :], whole[:, chunk % 3, :],
                                                                parts[:, a, w, 0, m, col],
                                                                ALU.subtract).then_inc(s_rest, 1)
                                        dve.wait_ge(s_rest, b * CHUNKS + (chunk + 1))
                                        nc.vector.tensor_copy(parts[:, a, w, 1, m, col],
                                                              rest[:, chunk % 2, :]).then_inc(s_mid, 1)
                                        dve.wait_ge(s_mid, b * CHUNKS + (chunk + 1))
                                        nc.vector.tensor_tensor(parts[:, a, w, 2, m, col], rest[:, chunk % 2, :],
                                                                parts[:, a, w, 1, m, col],
                                                                ALU.subtract).then_inc(s_split, 1)
                                        chunk += 1
                        for j in range(4):
                            dve.wait_ge(s_job, b * PRODUCTS + (9 + j))
                            for n in range(2):
                                last = nc.vector.tensor_tensor(
                                    v_s[:, a, :, 2 * j + n, :, 0:D],
                                    bank[4 + j][:, n * E:(n + 1) * E].rearrange("p (g h d) -> p g h d", g=NG, h=HG),
                                    bv_row[:].rearrange("p (g h d) -> p g h d", g=NG, h=HG), ALU.add)
                            last.then_inc(s_vev, 1)

        with ExitStack() as ctx:
            def sb(name, shape, dt):
                return sb_in(ctx, name, shape, dt)

            def sem(name):
                return sem_in(ctx, name)

            KBUF = 3
            IP = NT // 2
            UNITS = IP * NT
            ITEMS = NT * HG
            CH = ITEMS // 2
            CHUNK_EVERY = UNITS // CH
            CHUNKS_AHEAD = CH * 5 // 8
            PROLOGUE_CH = CH + CHUNKS_AHEAD
            PAIR_ITEMS = ITEMS // IP
            assert ITEMS == UNITS
            BAND_READS = [16 * HG * (2 if t in (0, NT - 1) else 1) for t in range(NT)]
            UNROLL = 6
            LOOPS = (G - 2) // UNROLL
            assert LOOPS * UNROLL == G - 2

            keys = sb("keys", [QROWS, KBUF, 2, HG, T], BF16)
            queries = sb("queries", [QROWS, 2, IP, HG, 2 * P], BF16)
            values = sb("values", [P, 2, NT, HG * PAD], F32)
            band_all = sb("band_all", [P, 2 * ITEMS * 2 * P + 2 * P], F32)
            band = band_all[:, 0:2 * ITEMS * 2 * P].rearrange("p (a n h s c) -> p a n h s c", a=2, n=NT, h=HG, s=2)
            no_band = band_all[:, 2 * ITEMS * 2 * P:]
            band_out = sb("band_out", [P, 2, 2, 2 * P], F32)
            probs = sb("probs", [P, 2, HG, 2 * P], F32)
            partial_max = sb("partial_max", [P, 2, ITEMS], F32)
            row_max = sb("row_max", [P, PAIR_ITEMS], F32)
            minus_max = sb("minus_max", [PAIR_ITEMS, IP, 2, P], BF16)
            weighted_s = sb("weighted_s", [P, IP, 2 * P], F32)
            token = sb("token2", [P, 8], F32)

            weigh_ps = [ctx.enter_context(nc.psum_tensor(f"weigh_ps{a}", [P, HG, 2 * P], F32)) for a in range(2)]
            look_ps = [ctx.enter_context(nc.psum_tensor(f"look_ps{a}", [P, 512], F32)) for a in range(2)]
            band_ps = ctx.enter_context(nc.psum_tensor("band_ps", [P, 2, 2 * P], F32))
            sum_ps = ctx.enter_context(nc.psum_tensor("sum_ps", [P, 2 * P], F32))

            s_set = sem("constants_set")
            s_passed = sem("waits_passed")
            s_keys = [sem(f"keys_in{a}") for a in range(KBUF)]
            s_q = [[sem(f"queries_in{a}_{k}") for k in range(IP)] for a in range(2)]
            s_v = [sem(f"values_in{a}") for a in range(2)]
            s_bp = sem("band_product_ready")
            s_be = sem("band_product_read")
            s_bw = [sem(f"band_written{a}") for a in range(2)]
            s_b = [sem(f"band_in{t}") for t in range(NT)]
            s_look = [sem(f"look_ready{a}") for a in range(2)]
            s_seen = [sem(f"look_read{a}") for a in range(2)]
            s_rm = sem("row_max_ready")
            s_rmT = sem("row_max_turned")
            s_hi = sem("minus_max_high_ready")
            s_mm = sem("minus_max_ready")
            s_min = [[sem(f"minus_max_in{a}_{k}") for k in range(IP)] for a in range(2)]
            s_sc = sem("scores_ready")
            s_pr = sem("probs_ready")
            s_av = sem("weighted_sum_ready")
            s_ws = sem("weighted_sum_copied")
            s_ho = [sem(f"weighted_sum_stored{k}") for k in range(IP)]

            def key_kind(n, t):
                return 0 if n == 0 or n <= t else 1

            def look_pieces(t):
                pieces = []
                for pos in range(NT):
                    n = (t + pos) % NT
                    kind, half = key_kind(n, t), pos // 4
                    last = pieces[-1] if pieces else None
                    if last and last[0] == half and last[2] == kind and last[3] + last[4] == n:
                        last[4] += 1
                    else:
                        pieces.append([half, pos % 4 * P, kind, n, 1])
                return pieces

            def chunk_of(j):
                n = (j + CHUNKS_AHEAD) % CH
                ahead = 1 if j + CHUNKS_AHEAD < CH else 2
                return ahead, n // 2, 2 * (n % 2)

            def wait_apart(eng, *waits):
                for what, count in waits:
                    eng.wait_ge(what, count)
                eng.sem_inc(s_passed, 1)

            block = ctx.enter_context(nc.Block())

            @block.sync
            def _(sp):
                def load_queries(s, k, pair):
                    col = slice(pair * 2 * P, (pair + 1) * 2 * P)
                    for t in range(TERMS):
                        sp.dma_start(queries[t * D:(t + 1) * D, k % 2, pair],
                                     split_scr[0, TERM_Q[t], s].rearrange("(h d) t -> d h t", h=HG)[:, :, col]
                                     ).then_inc(s_q[k % 2][pair], 16)

                def write_band(count, k, tile, h0):
                    sp.wait_ge(s_be, count + 1)
                    a = tile * 2 + h0 // 2
                    sp.dma_start(flat(band_scr, (((k % 2) * HG + h0) * NT + tile) * P * BAND_ROW + P,
                                      [[BAND_ROW, P], [NT * P * BAND_ROW, 2], [1, 2 * P]]),
                                 band_out[:, a % 2]).then_inc(s_bw[a % 2], 16)

                def read_band(written, k, tile, h0):
                    a = tile * 2 + h0 // 2
                    sp.wait_ge(s_bw[a % 2], written)
                    for h in range(h0, h0 + 2):
                        base = (((k % 2) * HG + h) * NT + tile) * P * BAND_ROW + P
                        if tile == 0:
                            sp.dma_start(band[:, k % 2, tile, h, 0, HALF:P],
                                         flat(band_scr, base + HALF, [[BAND_ROW - 1, P], [1, P - HALF]])
                                         ).then_inc(s_b[tile], 16)
                            sp.dma_start(band[:, k % 2, tile, h, 1],
                                         flat(band_scr, base + 2 * P, [[BAND_ROW - 1, P], [1, P]])
                                         ).then_inc(s_b[tile], 16)
                        elif tile == NT - 1:
                            sp.dma_start(band[:, k % 2, tile, h, 0],
                                         flat(band_scr, base, [[BAND_ROW - 1, P], [1, P]])
                                         ).then_inc(s_b[tile], 16)
                            sp.dma_start(band[:, k % 2, tile, h, 1, 0:HALF],
                                         flat(band_scr, base + 2 * P, [[BAND_ROW - 1, P], [1, HALF]])
                                         ).then_inc(s_b[tile], 16)
                        else:
                            sp.dma_start(band[:, k % 2, tile, h],
                                         flat(band_scr, base, [[BAND_ROW - 1, P], [2 * P, 2], [1, P]])
                                         ).then_inc(s_b[tile], 16)

                def load_minus_max(s, k, pair):
                    sp.wait_ge(s_mm, s * IP + (pair + 1))
                    for c in range(2):
                        row = queries[ROWS + c:ROWS + c + 1, k % 2, pair]
                        sp.dma_start(flat(row, 0, [row.ap[0], [P, PAIR_ITEMS], [1, P]]),
                                     minus_max[:, pair, c, :].rearrange("r (a p) -> r a p", a=1)
                                     ).then_inc(s_min[k % 2][pair], 16)

                o_heads = o_scr.rearrange("b h r t -> (b h) r t")

                def store_sums(s, pair):
                    sp.wait_ge(s_ws, s * IP + (pair + 2))
                    for h in range(HG):
                        sp.dma_start(o_heads[s * HG + h, :, pair * 2 * P:(pair + 1) * 2 * P],
                                     weighted_s[h * PAD:h * PAD + D + 1, pair]).then_inc(s_ho[pair], 16)

                def step(s, k, look=True, ahead=True):
                    base = s * CH + PROLOGUE_CH
                    queue = []
                    for j in range(CH):
                        slot = j * CHUNK_EVERY
                        d, tile, h0 = chunk_of(j)
                        if not (look if d == 1 else ahead):
                            continue
                        queue.append((slot + 1, 1, "write", j, k + d, tile, h0))
                        queue.append((slot + 3, 2, "read", j, k + d, tile, h0))
                    queue.append((1, 0, "load", 0, 0, 0, 0))
                    for u in range(NT, UNITS, NT):
                        queue.append((u, 0, "q", u, 0, 0, 0))
                    queue.append((2, 3, "max", IP - 1, s, k, 0))
                    for pair in range(IP):
                        queue.append((NT * (pair + 1) + 3, 4, "store", pair, 0, 0, 0))
                        if look and pair < IP - 1:
                            queue.append((NT * (pair + 1) + 2, 3, "max", pair, s + 1, k + 1, 0))
                    for _, _, what, j, kk, tile, h0 in sorted(queue, key=lambda e: (min(e[0], UNITS), e[1])):
                        if what == "write":
                            write_band(base + j, kk, tile, h0)
                        elif what == "read":
                            read_band(s * (8 * CH) + 16 * (PROLOGUE_CH // 2 + j // 2 + 1), kk, tile, h0)
                        elif what == "load":
                            wait_apart(sp, (s_sc, s * UNITS + 1))
                            if look:
                                load_queries(s + 1, k + 1, IP - 1)
                        elif what == "q" and ahead:
                            wait_apart(sp, (s_sc, s * UNITS + j))
                            load_queries(s + 2, k + 2, j // NT - 1)
                        elif what == "store":
                            store_sums(s, j)
                        elif what == "max":
                            load_minus_max(kk, tile, j)

                for pair in range(IP):
                    load_queries(0, 0, pair)
                for pair in range(IP - 1):
                    load_queries(1, 1, pair)
                sp.wait_ge(s_set, 5)
                for j in range(PROLOGUE_CH):
                    tile, h0 = j % CH // 2, 2 * (j % 2)
                    write_band(j, j // CH, tile, h0)
                    if j:
                        p = j - 1
                        read_band(16 * (p // 2 + 1), p // CH, p % CH // 2, 2 * (p % 2))
                p = PROLOGUE_CH - 1
                read_band(16 * (p // 2 + 1), p // CH, p % CH // 2, 2 * (p % 2))
                for pair in range(IP - 1):
                    load_minus_max(0, 0, pair)
                with sp.Fori(0, LOOPS) as i:
                    for k in range(UNROLL):
                        step(i * UNROLL + k, k)
                step(G - 2, G - 2, ahead=False)
                step(G - 1, G - 1, look=False, ahead=False)
                for pair in range(IP):
                    sp.wait_ge(s_ho[pair], 16 * HG * (G + 1))

            @block.gpsimd
            def _(pool):
                def load_keys(s, k):
                    for kind in range(2):
                        for t in range(TERMS):
                            pool.dma_start(keys[t * D:(t + 1) * D, k % KBUF, kind],
                                         split_scr[1 + kind, TERM_K[t], s].rearrange("(h d) t -> d h t", h=HG)
                                         ).then_inc(s_keys[k % KBUF], 16)

                def load_values(s, k):
                    pool.dma_start(values[:, k % 2], v_scr[s]).then_inc(s_v[k % 2], 16)

                load_keys(0, 0)
                load_keys(1, 1)
                load_values(0, 0)
                nc.gpsimd.memset(no_band, 0.0).then_inc(s_set, 1)
                pool.wait_ge(s_set, 1)
                for a in range(2):
                    nc.gpsimd.memset(band[:, a, 0, :, 0, 0:HALF], 0.0).then_inc(s_set, 1)
                    nc.gpsimd.memset(band[:, a, NT - 1, :, 1, HALF:P], 0.0).then_inc(s_set, 1)
                pool.wait_ge(s_set, 5)
                for a in range(KBUF):
                    nc.gpsimd.memset(keys[ROWS:QROWS, a], 1.0).then_inc(s_set, 1)
                pool.wait_ge(s_set, 5 + KBUF)
                nc.gpsimd.memset(token[:, 0:1], 0.0).then_inc(s_ws, 1)
                for pair in range(IP):
                    nc.gpsimd.memset(token[:, pair + 1:pair + 2], 0.0).then_inc(s_ho[pair], 16 * HG)

                def step(s, k, ahead=True):
                    wait_apart(pool, (s_sc, s * UNITS + 1))
                    load_values(s + 1, k + 1)
                    if ahead:
                        load_keys(s + 2, k + 2)

                with pool.Fori(0, LOOPS) as i:
                    for k in range(UNROLL):
                        step(i * UNROLL + k, k)
                step(G - 2, G - 2, ahead=False)

            @block.scalar
            def _(act):
                def copy_band(count, written):
                    act.wait_ge(s_bp, count + 1)
                    if written is not None:
                        act.wait_ge(s_bw[written[0]], written[1])

                def copy_sums(s, pair):
                    act.wait_ge(s_av, s * IP + (pair + 1))
                    act.wait_ge(s_ho[pair], s * (16 * HG) + 16 * HG)
                    nc.scalar.activation(weighted_s[:, pair], sum_ps[:], ACT.Copy).then_inc(s_ws, 1)

                def step(s, k, look=True, ahead=True):
                    for u in range(UNITS):
                        act.wait_ge(s_sc, s * UNITS + (u + 1))
                        nc.scalar.activation(probs[:, u % 2], weigh_ps[u % 2][:], ACT.Exp).then_inc(s_pr, 1)
                        if u and u % NT == 0:
                            copy_sums(s, u // NT - 1)
                        j = u // CHUNK_EVERY
                        if u % CHUNK_EVERY == 0 and (look if chunk_of(j)[0] == 1 else ahead):
                            copy_band(s * CH + (PROLOGUE_CH + j),
                                      (j % 2, s * (8 * CH) + 16 * (PROLOGUE_CH // 2 + j // 2)))
                            nc.scalar.activation(band_out[:, j % 2], band_ps[:], ACT.Copy).then_inc(s_be, 1)
                    copy_sums(s, IP - 1)

                for j in range(PROLOGUE_CH):
                    copy_band(j, (j % 2, 16 * (j // 2)) if j >= 2 else None)
                    nc.scalar.activation(band_out[:, j % 2], band_ps[:], ACT.Copy).then_inc(s_be, 1)
                with act.Fori(0, LOOPS) as i:
                    for k in range(UNROLL):
                        step(i * UNROLL + k, k)
                step(G - 2, G - 2, ahead=False)
                step(G - 1, G - 1, look=False, ahead=False)

            @block.vector
            def _(dve):
                def look(s, k, item):
                    tile, h = item // HG, item % HG
                    count = s * ITEMS + (item + 1)
                    col = tile // 2 * PAIR_ITEMS + h * 2 + tile % 2
                    wait_apart(dve, (s_look[0], count), (s_b[tile], (s + 1) * BAND_READS[tile]))
                    mine = band[:, k % 2, tile, h]
                    bias = flat(mine, 0, [mine.ap[0], [no_band.offset - mine.offset, 2], [1, 2 * P]])
                    both = look_ps[0][:].rearrange("p (a c) -> p a c", a=2)
                    nc.vector.tensor_tensor_reduce(
                        out=both, in0=both, in1=bias, scale=1.0, scalar=LOWEST, op0=ALU.add, op1=ALU.max,
                        accum_out=partial_max[:, 0, col:col + 1]).then_inc(s_seen[0], 1)
                    dve.wait_ge(s_look[1], count)
                    nc.vector.reduce_max(partial_max[:, 1, col:col + 1], look_ps[1][:], AX_X).then_inc(s_seen[1], 1)

                def finish_max(s, pair):
                    count = s * IP + (pair + 1)
                    col = slice(pair * PAIR_ITEMS, (pair + 1) * PAIR_ITEMS)
                    dve.wait_ge(s_seen[1], s * ITEMS + (pair + 1) * PAIR_ITEMS)
                    nc.vector.tensor_reduce(row_max[:], partial_max[:, :, col].rearrange("p a i -> p i a"), AX_X,
                                            ALU.max).then_inc(s_rm, 1)
                    turned = look_ps[0][0:PAIR_ITEMS, 0:P]
                    dve.wait_ge(s_rmT, count)
                    nc.vector.tensor_scalar(minus_max[:, pair, 0, :], turned, -1.0, None, ALU.mult).then_inc(s_hi, 1)
                    dve.wait_ge(s_hi, count)
                    nc.vector.scalar_tensor_tensor(out=minus_max[:, pair, 1, :], in0=turned, scalar=-1.0,
                                                   in1=minus_max[:, pair, 0, :], op0=ALU.mult,
                                                   op1=ALU.subtract).then_inc(s_mm, 1)

                def step(s, k):
                    finish_max(s, IP - 1)
                    for item in range(ITEMS):
                        look(s + 1, k + 1, item)
                        if (item + 1) % PAIR_ITEMS == 0 and item + 1 < ITEMS:
                            finish_max(s + 1, item // PAIR_ITEMS)

                for item in range(ITEMS):
                    look(0, 0, item)
                    if (item + 1) % PAIR_ITEMS == 0 and item + 1 < ITEMS:
                        finish_max(0, item // PAIR_ITEMS)
                with dve.Fori(0, LOOPS) as i:
                    for k in range(UNROLL):
                        step(i * UNROLL + k, k)
                step(G - 2, G - 2)
                finish_max(G - 1, IP - 1)

            @block.tensor
            def _(pe):
                def query_tile(k, h, tile):
                    return queries[0:ROWS, k % 2, tile // 2, h, tile % 2 * P:(tile % 2 + 1) * P]

                def band_product(count, k, tile, h0, first=False):
                    if not first:
                        pe.wait_ge(s_be, count)
                    for h in range(2):
                        last = nc.tensor.matmul(band_ps[:, h], query_tile(k, h0 + h, tile),
                                                rel_terms[:], start=True, stop=True)
                    last.then_inc(s_bp, 1)

                def look(s, k, item, half, first=False):
                    tile, h = item // HG, item % HG
                    if half == 0 and item % PAIR_ITEMS == 0 and not first:
                        pe.wait_ge(s_mm, s * IP + item // PAIR_ITEMS)
                    elif not first:
                        pe.wait_ge(s_seen[half], s * ITEMS + item)
                    for bank, col, kind, n, tiles in look_pieces(tile):
                        if bank == half:
                            last = nc.tensor.matmul(look_ps[half][:, col:col + tiles * P],
                                                    query_tile(k, h, tile),
                                                    keys[0:ROWS, k % KBUF, kind, h, n * P:(n + tiles) * P],
                                                    start=True, stop=True)
                    last.then_inc(s_look[half], 1)

                def turn_max(s, pair):
                    pe.wait_ge(s_rm, s * IP + (pair + 1))
                    nc.tensor.transpose(look_ps[0][0:PAIR_ITEMS, 0:P], row_max[:], ident[:]).then_inc(s_rmT, 1)

                def scores(s, k, u):
                    pair, n = u // NT, u % NT
                    for h in range(HG):
                        dst = weigh_ps[u % 2][:, h]
                        started = False
                        for e in range(2):
                            tile = 2 * pair + e
                            side = (n - tile) % NT
                            if side < 2:
                                nc.tensor.matmul(dst[:, e * P:(e + 1) * P], band[:, k % 2, tile, h, side], ident[:],
                                                 is_transpose=True, start=not started, stop=False,
                                                 skip_group_check=True)
                                started = True
                        kinds = [key_kind(n, 2 * pair + e) for e in range(2)]
                        spans = [(0, 2, kinds[0])] if kinds[0] == kinds[1] else [(0, 1, kinds[0]), (1, 2, kinds[1])]
                        for e0, e1, kind in spans:
                            last = nc.tensor.matmul(dst[:, e0 * P:e1 * P], keys[:, k % KBUF, kind, h, n * P:(n + 1) * P],
                                                    queries[:, k % 2, pair, h, e0 * P:e1 * P],
                                                    start=not started, stop=(e1 == 2), skip_group_check=True)
                            started = True
                    last.then_inc(s_sc, 1)

                def weighted(s, k, u):
                    pair, n = u // NT, u % NT
                    pe.wait_ge(s_pr, s * UNITS + (u + 1))
                    if n == 0:
                        pe.wait_ge(s_ws, s * IP + (pair + 1))
                    for h in range(HG):
                        last = nc.tensor.matmul(sum_ps[h * PAD:(h + 1) * PAD, :],
                                                values[:, k % 2, n, h * PAD:(h + 1) * PAD], probs[:, u % 2, h],
                                                start=(n == 0), stop=(n == NT - 1), tile_position=(0, h * PAD))
                    if n == NT - 1:
                        last.then_inc(s_av, 1)

                def step(s, k, look_on=True, ahead=True):
                    pe.wait_ge(s_v[k % 2], (s + (2 - k % 2)) * 8)
                    for u in range(UNITS):
                        if u % NT == 0:
                            pe.wait_ge(s_min[k % 2][u // NT], (s + (2 - k % 2)) * 16)
                        scores(s, k, u)
                        turns = u % PAIR_ITEMS == 0 and (look_on or u == 0)
                        if turns:
                            if u:
                                turn_max(s + 1, u // PAIR_ITEMS - 1)
                            else:
                                turn_max(s, IP - 1)
                        if look_on:
                            if u == 0:
                                pe.wait_ge(s_keys[(k + 1) % KBUF], key_count(s + 1, k + 1))
                            if u % PAIR_ITEMS == 0:
                                pe.wait_ge(s_q[(k + 1) % 2][u // PAIR_ITEMS], query_count(s + 1, k + 1))
                            if not turns:
                                look(s + 1, k + 1, u, 0)
                        j = u // CHUNK_EVERY
                        d, tile, h0 = chunk_of(j)
                        if u % CHUNK_EVERY == 0 and (look_on if d == 1 else ahead):
                            if tile % 2 == 0 and h0 == 0:
                                pe.wait_ge(s_q[(k + d) % 2][tile // 2], query_count(s + d, k + d))
                            band_product(s * CH + (PROLOGUE_CH + j), k + d, tile, h0)
                        if u:
                            weighted(s, k, u - 1)
                        if look_on:
                            if turns:
                                look(s + 1, k + 1, u, 0)
                            look(s + 1, k + 1, u, 1)
                    weighted(s, k, UNITS - 1)

                def query_count(s, k):
                    return (s - k % 2 + 2) * (16 * TERMS // 2)

                def key_count(s, k):
                    return (s - k % KBUF + KBUF) * (16 * 2 * TERMS // KBUF)

                pe.wait_ge(s_set, 5 + KBUF)
                for j in range(PROLOGUE_CH):
                    tile, h0 = j % CH // 2, 2 * (j % 2)
                    if j % 4 == 0:
                        pe.wait_ge(s_q[j // CH][tile // 2], 16 * TERMS)
                    band_product(j, j // CH, tile, h0, first=(j == 0))
                    if j == 0:
                        pe.wait_ge(s_keys[0], 16 * 2 * TERMS)
                for item in range(ITEMS):
                    if item and item % PAIR_ITEMS == 0:
                        turn_max(0, item // PAIR_ITEMS - 1)
                    for half in range(2):
                        look(0, 0, item, half, first=(item == 0))
                with pe.Fori(0, LOOPS) as i:
                    for k in range(UNROLL):
                        step(i * UNROLL + k, k)
                step(G - 2, G - 2, ahead=False)
                step(G - 1, G - 1, look_on=False, ahead=False)

        with ExitStack() as ctx:
            def sb(name, shape, dt):
                return sb_in(ctx, name, shape, dt)

            def sem(name):
                return sem_in(ctx, name)

            TOK = 512
            TT = TOK // P
            IT = B * T // TOK
            HM = P // D
            SPREAD = P // H
            assert T == 2 * TOK and IT % 2 == 0 and IT >= 8
            INNER = (IT - 4) // 2

            sums = sb("sums", [P, 2, TOK // SPREAD], F32)
            inverse = sb("inverse", [P, 2, TOK // SPREAD], F32)
            inverse_wide = sb("inverse_wide", [P, 2, KE, TOK], F32)
            heads_raw = sb("heads_raw", [P, 2, KE, TOK], F32)
            heads = sb("heads", [P, 2, KE, TOK], F32)
            x_in = sb("x_in", [P, 2, TT, E], F32)
            x_bo = sb("x_bo", [P, 2, TT, E], F32)
            y = sb("y", [P, TT, E], F32)
            x1 = sb("x1", [P, 2, TT, E], F32)
            x1_b2 = sb("x1_b2", [P, 2, TT, E], F32)
            x1T_rest = sb("x1T_rest", [P, KE, TOK], F32)
            x1T = sb("x1T", [P, 2, PARTS, KE, TOK], BF16)
            gelu = sb("gelu", [P, 2, TOK], F32)
            gelu_rest = sb("gelu_rest", [P, 2, TOK], F32)
            hidden = sb("hidden", [P, PARTS, KH, TOK], BF16)
            z = sb("z", [P, TT, E], F32)
            fin = sb("fin", [P, 2, TT, E], F32)
            stats = sb("stats", [P, 2 * TT, 6], F32)
            mean_var = sb("mean_var", [P, 2 * TT, 2], F32)
            std = sb("std", [P, 2 * TT], F32)
            rstd = sb("rstd", [P, 2 * TT], F32)
            token = sb("token3", [P, 4], F32)

            att_ps = ctx.enter_context(nc.psum_tensor("att_ps", [P, TT, E], F32))
            turn_ps = ctx.enter_context(nc.psum_tensor("turn_ps", [P, KE, TOK], F32))
            hid_ps = [ctx.enter_context(nc.psum_tensor(f"hid_ps{a}", [P, TOK], F32)) for a in range(2)]
            out_ps = ctx.enter_context(nc.psum_tensor("out_ps", [P, TT, E], F32))

            s_set = sem("stats_set")
            s_passed = sem("waits_passed3")
            s_sums = [sem(f"sums_in{a}") for a in range(2)]
            s_heads = [sem(f"heads_in{a}") for a in range(2)]
            s_x = [sem(f"residual_in{a}") for a in range(2)]
            s_rec = sem("inverse_ready")
            s_invw = [sem(f"inverse_written{a}") for a in range(2)]
            s_inv = [sem(f"inverse_in{a}") for a in range(2)]
            s_hn = sem("heads_divided")
            s_xb = sem("residual_with_bias")
            s_att = sem("projection_ready")
            s_y = sem("y_ready")
            s_yst = sem("y_stats")
            s_mv = sem("mean_var_ready")
            s_sd = sem("std_ready")
            s_rs = sem("rstd_ready")
            s_x1 = sem("x1_ready")
            s_x1b = sem("x1_with_bias")
            s_turn = sem("x1_turned")
            s_xh = sem("x1T_high_ready")
            s_xr = sem("x1T_rest_ready")
            s_xm = sem("x1T_middle_ready")
            s_x1T = sem("x1T_ready")
            s_h = sem("hidden_product")
            s_g = sem("gelu_ready")
            s_gr = sem("gelu_rest_ready")
            s_gm = sem("hidden_middle_ready")
            s_hid = sem("hidden_ready")
            s_ff = sem("out_product")
            s_zp = sem("z_scaled")
            s_z = sem("z_ready")
            s_zst = sem("z_stats")
            s_fin = sem("fin_ready")
            s_out = [sem(f"out_stored{a}") for a in range(2)]

            x_rows = x.rearrange("b t e -> (b t) e")
            out_rows = out.rearrange("b t e -> (b t) e")
            block = ctx.enter_context(nc.Block())

            @block.sync
            def _(sp):
                def load(it, b, a, first=False):
                    if not first:
                        sp.wait_ge(s_rec, it - 1)
                        sp.wait_ge(s_xb, it - 1)
                        sp.wait_ge(s_hn, it - 1)
                    col = a * TOK
                    weights = o_scr[b, :, D, col:col + TOK]
                    sp.dma_start(sums[:, a], weights.rearrange("h (c t) -> h c t", c=SPREAD)).then_inc(s_sums[a], 16)
                    for m in range(KE):
                        sp.dma_start(heads_raw[:, a, m], o_scr[b, m * HM:(m + 1) * HM, 0:D, col:col + TOK]
                                     ).then_inc(s_heads[a], 16)
                    sp.dma_start(x_in[:, a], x_rows[bass.ds(it * TOK, TOK), :]
                                 .rearrange("(j p) e -> p j e", p=P)).then_inc(s_x[a], 16)
                    sp.wait_ge(s_rec, it + 1)
                    sp.dma_start(inverse_scr[it].rearrange("h (c t) -> h c t", c=SPREAD),
                                 inverse[:, a]).then_inc(s_invw[a], 16)
                    sp.wait_ge(s_invw[a], (it + (2 - a)) * 8)
                    for m in range(KE):
                        sp.dma_start(inverse_wide[:, a, m], over(inverse_scr[it, m * HM:(m + 1) * HM, :], D, 1)
                                     ).then_inc(s_inv[a], 16)

                load(0, 0, 0, first=True)
                load(1, 0, 1, first=True)
                with sp.Fori(0, B - 1) as i:
                    for a in range(2):
                        load(i * 2 + (2 + a), i + 1, a)

            @block.gpsimd
            def _(pool):
                for a in range(2):
                    nc.gpsimd.memset(fin[:, a, 0, 0:1], 0.0).then_inc(s_out[a], 16)
                nc.gpsimd.memset(token[:, 0:1], 0.0).then_inc(s_fin, 1)
                nc.gpsimd.memset(token[:, 1:2], 0.0).then_inc(s_ff, 1)
                nc.gpsimd.memset(token[:, 2:3], 0.0).then_inc(s_gr, 2)
                nc.gpsimd.memset(token[:, 3:4], 0.0).then_inc(s_hid, 2)
                nc.gpsimd.memset(mean_var[:], 1.0).then_inc(s_set, 1)

                def divide(it, a, first=False):
                    pool.wait_ge(s_heads[a], (it + (2 - a)) * 16)
                    pool.wait_ge(s_inv[a], (it + (2 - a)) * 16)
                    if not first:
                        pool.wait_ge(s_att, it - 1)
                    nc.gpsimd.tensor_tensor(heads[:, a], heads_raw[:, a], inverse_wide[:, a],
                                            ALU.mult).then_inc(s_hn, 1)

                def residual(it, a, first=False):
                    pool.wait_ge(s_x[a], (it + (2 - a)) * 8)
                    if not first:
                        pool.wait_ge(s_y, it - 1)
                    nc.gpsimd.tensor_tensor(x_bo[:, a], x_in[:, a], over(bo_row[:], TT, 1), ALU.add).then_inc(s_xb, 1)

                def skip(it, a, early=False):
                    pool.wait_ge(s_x1, it + 1)
                    if not early:
                        pool.wait_ge(s_z, it - 1)
                    nc.gpsimd.tensor_tensor(x1_b2[:, a], x1[:, a], over(b2_row[:], TT, 1), ALU.add).then_inc(s_x1b, 1)

                def add_skip(it, a):
                    pool.wait_ge(s_zp, it + 1)
                    pool.wait_ge(s_x1b, it + 1)
                    nc.gpsimd.tensor_tensor(z[:], z[:], x1_b2[:, a], ALU.add).then_inc(s_z, 1)

                def iteration(it, a, before=True, skips=True, ahead=True):
                    if before:
                        add_skip(it - 1, 1 - a)
                    if skips:
                        skip(it + 1, 1 - a, early=not before)
                    if ahead:
                        divide(it + 3, 1 - a)
                        residual(it + 3, 1 - a)

                divide(0, 0, first=True)
                residual(0, 0, first=True)
                divide(1, 1, first=True)
                residual(1, 1, first=True)
                divide(2, 0)
                residual(2, 0)
                skip(0, 0, early=True)
                iteration(0, 0, before=False)
                with pool.Fori(0, INNER) as i:
                    for a in (1, 0):
                        iteration(i * 2 + (1 if a else 2), a)
                iteration(IT - 3, 1, ahead=False)
                iteration(IT - 2, 0, ahead=False)
                iteration(IT - 1, 1, skips=False, ahead=False)
                add_skip(IT - 1, 1)

            @block.vector
            def _(dve):
                def invert(it, a, first=False):
                    dve.wait_ge(s_sums[a], (it + (2 - a)) * 8)
                    if not first:
                        dve.wait_ge(s_invw[a], (it - a) * 8)
                    nc.vector.reciprocal(inverse[:, a], sums[:, a]).then_inc(s_rec, 1)

                def scale(it):
                    dve.wait_ge(s_ff, it + 2)
                    dve.wait_ge(s_fin, it + 1)
                    nc.vector.tensor_tensor(z[:], out_ps[:], over(alpha2_row[:], TT, 1), ALU.mult).then_inc(s_zp, 1)

                def split_hidden(it):
                    for j in range(KH + 1):
                        if j < KH:
                            count = it * KH + (j + 1)
                            dve.wait_ge(s_g, count)
                            dve.wait_ge(s_hid, count)
                            nc.vector.tensor_tensor(gelu_rest[:, j % 2], gelu[:, j % 2], hidden[:, 0, j],
                                                    ALU.subtract).then_inc(s_gr, 1)
                        if j:
                            dve.wait_ge(s_gm, it * KH + j)
                            nc.vector.tensor_tensor(hidden[:, 2, j - 1], gelu_rest[:, (j - 1) % 2],
                                                    hidden[:, 1, j - 1], ALU.subtract).then_inc(s_hid, 1)

                def split_x1T(it, a, first=False):
                    dve.wait_ge(s_xh, it + 1)
                    if not first:
                        dve.wait_ge(s_x1T, it)
                    nc.vector.tensor_tensor(x1T_rest[:], turn_ps[:], x1T[:, a, 0], ALU.subtract).then_inc(s_xr, 1)
                    dve.wait_ge(s_xm, it + 1)
                    nc.vector.tensor_tensor(x1T[:, a, 2], x1T_rest[:], x1T[:, a, 1], ALU.subtract).then_inc(s_x1T, 1)

                def norms(n, z_of=None, y_of=None, first=False, early=False):
                    if y_of is not None:
                        it, a = y_of
                        dve.wait_ge(s_att, it + 1)
                        dve.wait_ge(s_xb, it + 1)
                        if not first:
                            dve.wait_ge(s_x1, it)
                        nc.vector.tensor_tensor(y[:], att_ps[:], x_bo[:, a], ALU.add).then_inc(s_y, 1)
                        dve.wait_ge(s_y, it + 1)
                        for t in range(TT):
                            last = nc.vector.bn_stats(stats[:, t, :], y[:, t])
                        last.then_inc(s_yst, 1)
                    if z_of is not None:
                        dve.wait_ge(s_z, z_of[0] + 1)
                        for t in range(TT):
                            last = nc.vector.bn_stats(stats[:, TT + t, :], z[:, t])
                        last.then_inc(s_zst, 1)
                    if y_of is not None:
                        dve.wait_ge(s_yst, y_of[0] + 1)
                    if z_of is not None:
                        dve.wait_ge(s_zst, z_of[0] + 1)
                    dve.sem_inc(s_passed, 1)
                    cols = range(0 if y_of is not None else TT, 2 * TT if z_of is not None else TT)
                    for t in cols:
                        last = nc.vector.bn_aggr(mean_var[:, t, :], stats[:, t, :])
                    last.then_inc(s_mv, 1)
                    dve.wait_ge(s_sd, n + 1)
                    nc.vector.reciprocal(rstd[:], std[:]).then_inc(s_rs, 1)
                    dve.wait_ge(s_rs, n + 1)
                    if y_of is not None:
                        it, a = y_of
                        if not early:
                            dve.wait_ge(s_turn, it - 1)
                            dve.wait_ge(s_x1b, it - 1)
                        for t in range(TT):
                            last = nc.vector.tensor_scalar(x1[:, a, t], y[:, t], mean_var[:, t, 0:1], rstd[:, t:t + 1],
                                                           ALU.subtract, ALU.mult)
                        last.then_inc(s_x1, 1)
                    if z_of is not None:
                        it, a = z_of
                        dve.wait_ge(s_out[a], (it + (2 - a)) * 8)
                        for t in range(TT):
                            last = nc.vector.tensor_scalar(fin[:, a, t], z[:, t], mean_var[:, TT + t, 0:1],
                                                           rstd[:, TT + t:TT + t + 1], ALU.subtract, ALU.mult)
                        last.then_inc(s_fin, 1)

                def iteration(it, a, before=True, turns=True, ahead=True, inverts=True):
                    if before:
                        scale(it - 1)
                    if inverts:
                        invert(it + 3, 1 - a)
                    split_hidden(it)
                    if turns:
                        split_x1T(it + 1, 1 - a)
                    if before or ahead:
                        norms(it + 2, z_of=(it - 1, 1 - a) if before else None, y_of=(it + 2, a) if ahead else None)

                dve.wait_ge(s_set, 1)
                invert(0, 0, first=True)
                invert(1, 1, first=True)
                norms(0, y_of=(0, 0), first=True, early=True)
                invert(2, 0)
                split_x1T(0, 0, first=True)
                norms(1, y_of=(1, 1), early=True)
                iteration(0, 0, before=False)
                with dve.Fori(0, INNER) as i:
                    for a in (1, 0):
                        iteration(i * 2 + (1 if a else 2), a)
                iteration(IT - 3, 1, inverts=False)
                iteration(IT - 2, 0, ahead=False, inverts=False)
                iteration(IT - 1, 1, turns=False, ahead=False, inverts=False)
                scale(IT - 1)
                norms(IT + 2, z_of=(IT - 1, 1))

            @block.scalar
            def _(act):
                def roots(n):
                    act.wait_ge(s_mv, n + 1)
                    nc.scalar.activation(std[:], mean_var[:, :, 1], ACT.Sqrt, bias=eps_col[:, 0:1]).then_inc(s_sd, 1)

                def gelus(it):
                    act.wait_ge(s_ff, it + 1)
                    for j in range(KH + 1):
                        if j < KH:
                            count = it * KH + (j + 1)
                            act.wait_ge(s_h, count)
                            act.wait_ge(s_gr, count)
                            nc.scalar.activation(gelu[:, j % 2], hid_ps[j % 2][:], ACT.Gelu, bias=b1_col[:, j:j + 1],
                                                 scale=alpha1[:, j:j + 1])
                            nc.scalar.activation(hidden[:, 0, j], hid_ps[j % 2][:], ACT.Gelu, bias=b1_col[:, j:j + 1],
                                                 scale=alpha1[:, j:j + 1]).then_inc(s_g, 1)
                        if j:
                            act.wait_ge(s_gr, it * KH + (j + 2))
                            nc.scalar.activation(hidden[:, 1, j - 1], gelu_rest[:, (j - 1) % 2],
                                                 ACT.Copy).then_inc(s_gm, 1)

                def copy_turned(it, a):
                    act.wait_ge(s_turn, it + 1)
                    nc.scalar.activation(x1T[:, a, 0], turn_ps[:], ACT.Copy).then_inc(s_xh, 1)
                    act.wait_ge(s_xr, it + 1)
                    nc.scalar.activation(x1T[:, a, 1], x1T_rest[:], ACT.Copy).then_inc(s_xm, 1)

                def store(it, a):
                    act.wait_ge(s_fin, it + 2)
                    act.dma_start(out_rows[bass.ds(it * TOK, TOK), :].rearrange("(j p) e -> p j e", p=P),
                                  fin[:, a]).then_inc(s_out[a], 16)

                def iteration(it, a, before=True, turns=True, ahead=True):
                    gelus(it)
                    if turns:
                        copy_turned(it + 1, 1 - a)
                    if before or ahead:
                        roots(it + 2)
                    if before:
                        store(it - 1, 1 - a)

                roots(0)
                copy_turned(0, 0)
                roots(1)
                iteration(0, 0, before=False)
                with act.Fori(0, INNER) as i:
                    for a in (1, 0):
                        iteration(i * 2 + (1 if a else 2), a)
                iteration(IT - 3, 1)
                iteration(IT - 2, 0, ahead=False)
                iteration(IT - 1, 1, turns=False, ahead=False)
                roots(IT + 2)
                store(IT - 1, 1)
                for a in range(2):
                    act.wait_ge(s_out[a], 16 + 16 * IT // 2)

            @block.tensor
            def _(pe):
                def project(it, a, first=False):
                    pe.wait_ge(s_hn, it + 1)
                    if not first:
                        pe.wait_ge(s_y, it)
                    for t in range(TT):
                        for m in range(KE):
                            last = nc.tensor.matmul(att_ps[:, t], heads[:, a, m, t * P:(t + 1) * P], woT[:, m],
                                                    start=(m == 0), stop=(m == KE - 1))
                    last.then_inc(s_att, 1)

                def turn(it, a, first=False):
                    pe.wait_ge(s_x1, it + 1)
                    if not first:
                        pe.wait_ge(s_xr, it)
                    for kt in range(KE):
                        for t in range(TT):
                            last = nc.tensor.transpose(turn_ps[:, kt, t * P:(t + 1) * P],
                                                       x1[:, a, t, kt * P:(kt + 1) * P], ident[:])
                    last.then_inc(s_turn, 1)

                def layer1(it, a, first=False):
                    pe.wait_ge(s_x1T, it + 1)
                    for j in range(KH):
                        if not (first and j < 2):
                            pe.wait_ge(s_g, it * KH + (j - 1))
                        terms = [(c, kt) for c in range(PARTS) for kt in range(KE)]
                        for c, kt in terms:
                            last = nc.tensor.matmul(hid_ps[j % 2][:], sign1T[:, kt, j * P:(j + 1) * P],
                                                    x1T[:, a, c, kt], start=((c, kt) == terms[0]),
                                                    stop=((c, kt) == terms[-1]))
                        last.then_inc(s_h, 1)

                def layer2(it, first=False):
                    pe.wait_ge(s_hid, it * KH + (KH + 2))
                    if not first:
                        pe.wait_ge(s_zp, it)
                    terms = [(c, j) for c in range(PARTS) for j in range(KH)]
                    for t in range(TT):
                        for c, j in terms:
                            last = nc.tensor.matmul(out_ps[:, t], hidden[:, c, j, t * P:(t + 1) * P], sign2T[:, j],
                                                    start=((c, j) == terms[0]), stop=((c, j) == terms[-1]))
                    last.then_inc(s_ff, 1)

                def iteration(it, a, first=False, turns=True, ahead=True):
                    layer1(it, a, first)
                    if turns:
                        turn(it + 1, 1 - a)
                    if ahead:
                        project(it + 2, a)
                    layer2(it, first)

                project(0, 0, first=True)
                turn(0, 0, first=True)
                project(1, 1)
                iteration(0, 0, first=True)
                with pe.Fori(0, INNER) as i:
                    for a in (1, 0):
                        iteration(i * 2 + (1 if a else 2), a)
                iteration(IT - 3, 1)
                iteration(IT - 2, 0, ahead=False)
                iteration(IT - 1, 1, turns=False, ahead=False)



_INS = ['L0_attn_q', 'L0_attn_in_proj_weight', 'L0_attn_in_proj_bias', 'L0_attn_out_w', 'L0_attn_out_b',
        'L0_attn_rel_pe', 'L0_ffn_w1', 'L0_ffn_b1', 'L0_ffn_w2', 'L0_ffn_b2']
_OUTS = [((8, 1024, 256), 'float32')]


def kernel(**inputs):
    import numpy as _np
    import concourse.bacc as _bacc
    from concourse import mybir as _mybir
    from concourse.bass_utils import run_bass_kernel_spmd as _run

    nc = _bacc.Bacc("TRN2", target_bir_lowering=False, num_devices=1)
    arrays, args = {}, []
    for name in _INS:
        a = _np.ascontiguousarray(inputs[name])
        arrays[f"in_{name}_dram"] = a
        args.append(nc.dram_tensor(f"in_{name}_dram", a.shape, _mybir.dt.from_np(a.dtype), kind="ExternalInput").ap())
    for i, (shape, dtype) in enumerate(_OUTS):
        dt = _mybir.dt.from_np(_np.dtype(dtype))
        args.append(nc.dram_tensor(f"out_{i}_dram", shape, dt, kind="ExternalOutput").ap())
    post_ln_block(nc, *args)
    r = _run(nc, [arrays], core_ids=[0])
    got = tuple(r.results[0][f"out_{i}_dram"] for i in range(len(_OUTS)))
    return got[0]
```

```python
from contextlib import ExitStack

import concourse.bass as bass
from concourse import mybir

F32 = mybir.dt.float32
BF16 = mybir.dt.bfloat16
ALU = mybir.AluOpType
ACT = mybir.ActivationFunctionType
AX_X = mybir.AxisListType.X

P = 128
TERM_Q = (0, 0, 1, 0, 2, 1)
TERM_K = (0, 1, 0, 2, 0, 1)
TERMS = len(TERM_Q)
PARTS = 3
LOWEST = -3.0e38


def flat(ap, offset, dims):
    return bass.AP(tensor=ap.tensor, offset=ap.offset + offset, ap=[list(d) for d in dims])


def over(ap, count, at):
    dims = [list(d) for d in ap.ap]
    return bass.AP(tensor=ap.tensor, offset=ap.offset, ap=dims[:at] + [[0, count]] + dims[at:])


def post_ln_block(nc, x, w_in, b_in, w_out, b_out, rel, w1, b1, w2, b2, out):
    B, T, E = x.shape
    R, D = rel.shape
    H = E // D
    HID = w1.shape[0]
    REACH = R // 2
    NT = T // P
    HG = 4
    NG = H // HG
    G = B * NG
    KE = E // P
    KH = HID // P
    PAD = 32
    HALF = REACH
    ROWS = TERMS * D
    QROWS = ROWS + 2
    EPS = 1e-5
    assert R == P + 1 and D * HG * 2 == P and KE == 2 and T % 512 == 0

    outer = ExitStack()
    with outer:
        def sem_in(ctx, name):
            return ctx.enter_context(nc.semaphore(name))

        def sb_in(ctx, name, shape, dt):
            return ctx.enter_context(nc.sbuf_tensor(name, shape, dt))

        split_scr = nc.dram_tensor("split_scr", [3, PARTS, G, HG * D, T], BF16).ap()
        v_scr = nc.dram_tensor("v_scr", [G, P, NT, HG * PAD], F32).ap()
        BAND_ROW = 3 * P
        band_scr = nc.dram_tensor("band_scr", [2 * HG * NT * P + 1, BAND_ROW], F32).ap()
        o_scr = nc.dram_tensor("o_scr", [B, H, D + 1, T], F32).ap()

        inverse_scr = nc.dram_tensor("inverse_scr", [B * T // 512, H, 512], F32).ap()

        ident = sb_in(outer, "ident", [P, P], F32)
        woT = sb_in(outer, "woT", [P, KE, E], F32)
        sign1T = sb_in(outer, "sign1T", [P, KE, HID], BF16)
        sign2T = sb_in(outer, "sign2T", [P, KH, E], BF16)
        alpha1 = sb_in(outer, "alpha1", [P, KH], F32)
        b1_col = sb_in(outer, "b1_col", [P, KH], F32)
        alpha2_row = sb_in(outer, "alpha2_row", [P, E], F32)
        bo_row = sb_in(outer, "bo_row", [P, E], F32)
        b2_row = sb_in(outer, "b2_row", [P, E], F32)
        rel_terms = sb_in(outer, "rel_terms", [ROWS, 3 * P], BF16)
        eps_col = sb_in(outer, "eps_col", [P, 1], F32)

        with ExitStack() as ctx:
            def sb(name, shape, dt):
                return sb_in(ctx, name, shape, dt)

            def sem(name):
                return sem_in(ctx, name)

            wT = sb("wT", [P, KE, 3 * E], F32)
            bq_col = sb("bq_col", [P, 2], F32)
            bk_left = sb("bk_left", [P, 2], F32)
            bk_right = sb("bk_right", [P, 2], F32)
            bv_row = sb("bv_row", [P, E], F32)
            x_s = sb("x_s", [P, 2, NT, E], F32)
            zeros = sb("zeros", [P, NT, P], F32)
            s_x = [sem(f"x_in{a}") for a in range(2)]
            s_zero = sem("pads_zeroed")
            bank = [ctx.enter_context(nc.psum_tensor(f"bank{i}", [P, 512], F32)) for i in range(8)]

            with ExitStack() as c0:
                w_in_s = sb_in(c0, "w_in_s", [P, 6, E], F32)
                w_out_s = sb_in(c0, "w_out_s", [P, 2, E], F32)
                w1_s = sb_in(c0, "w1_s", [P, KH, E], F32)
                w2_s = sb_in(c0, "w2_s", [P, 2, HID], F32)
                sgn1 = sb_in(c0, "sgn1", [P, KH, E], F32)
                sgn2 = sb_in(c0, "sgn2", [P, 2, HID], F32)
                junk1 = sb_in(c0, "junk1", [P, KH, E], F32)
                junk2 = sb_in(c0, "junk2", [P, 2, HID], F32)
                b_col = sb_in(c0, "b_col", [P, 4], F32)
                rel_ends = sb_in(c0, "rel_ends", [P, 2], F32)
                relT = sb_in(c0, "relT", [D, R], F32)
                rel_d = sb_in(c0, "rel_d", [D, 3 * P], F32)
                rel_r = sb_in(c0, "rel_r", [D, 3 * P], F32)
                rel_parts = sb_in(c0, "rel_parts", [D, PARTS, 3 * P], BF16)
                alpha2 = sb_in(c0, "alpha2", [P, 2], F32)
                alpha2_wide = sb_in(c0, "alpha2_wide", [P, 2, P], F32)
                s_win = sem_in(c0, "projection_weights_in")
                s_w1 = sem_in(c0, "hidden_weights_in")
                s_w = sem_in(c0, "output_weights_in")
                s_small = sem_in(c0, "small_in")
                s_set = sem_in(c0, "pool_set")
                s_sgn = sem_in(c0, "signs_ready")
                s_dve = sem_in(c0, "dve_chain")
                s_rel = sem_in(c0, "rel_parts_ready")
                s_relt = sem_in(c0, "rel_terms_in")
                s_src = sem_in(c0, "sources_ready")
                s_tr = sem_in(c0, "transposed")
                s_eva = sem_in(c0, "evacuated_act")
                s_evd = sem_in(c0, "evacuated_dve")

                jobs = []
                for kt in range(KE):
                    for j0, nj in ((0, 4), (4, 2)):
                        jobs.append(([w_in_s[:, j, kt * P:(kt + 1) * P] for j in range(j0, j0 + nj)],
                                     wT[:, kt, j0 * P:(j0 + nj) * P]))
                for kt in range(KE):
                    for j0 in range(0, KH, 4):
                        jobs.append(([sgn1[:, j, kt * P:(kt + 1) * P] for j in range(j0, j0 + 4)],
                                     sign1T[:, kt, j0 * P:(j0 + 4) * P]))
                for kt in range(0, KH, 2):
                    jobs.append(([sgn2[:, j, k * P:(k + 1) * P] for k in (kt, kt + 1) for j in range(2)],
                                 sign2T[:, kt:kt + 2, :].rearrange("p a b -> p (a b)")))
                jobs.append(([w_out_s[:, j, k * P:(k + 1) * P] for k in range(KE) for j in range(2)],
                             woT[:].rearrange("p a b -> p (a b)")))
                jobs.append(([alpha2_wide[:, j, :] for j in range(2)], alpha2_row[:, :]))

                block = c0.enter_context(nc.Block())

                @block.sync
                def _(sp):
                    sp.dma_start(w_in_s[:], w_in.rearrange("(j p) e -> p j e", p=P)).then_inc(s_win, 16)
                    sp.dma_start(w1_s[:], w1.rearrange("(j p) e -> p j e", p=P)).then_inc(s_w1, 16)
                    sp.dma_start(w2_s[:], w2.rearrange("(j p) e -> p j e", p=P)).then_inc(s_w, 16)
                    sp.dma_start(w_out_s[:], w_out.rearrange("(j p) e -> p j e", p=P)).then_inc(s_w, 16)
                    sp.wait_ge(s_rel, 3)
                    for t in range(TERMS):
                        sp.dma_start(rel_terms[t * D:(t + 1) * D, :],
                                     rel_parts[:, TERM_K[t], :]).then_inc(s_relt, 16)
                    sp.wait_ge(s_relt, 16 * TERMS)

                @block.scalar
                def _(act):
                    def evacuate(n):
                        src, dst = jobs[n]
                        act.wait_ge(s_tr, n + 1)
                        nc.scalar.activation(dst, bank[n % 8][:, 0:len(src) * P], ACT.Copy).then_inc(s_eva, 1)

                    act.dma_start(b_col[:], b_in[0:2 * E].rearrange("(j p) -> p j", p=P),
                                  allow_slow_non_contiguous=True).then_inc(s_small, 16)
                    act.dma_start(b1_col[:], b1.rearrange("(j p) -> p j", p=P),
                                  allow_slow_non_contiguous=True).then_inc(s_small, 16)
                    act.dma_start(relT[:], rel.rearrange("r d -> d r"),
                                  allow_slow_non_contiguous=True).then_inc(s_small, 16)
                    for n, r in enumerate((0, R - 1)):
                        for h in range(P // D):
                            act.dma_start(rel_ends[h * D:(h + 1) * D, n:n + 1],
                                          flat(rel, r * D, [[1, D], [1, 1]]),
                                          allow_slow_non_contiguous=True).then_inc(s_small, 16)
                    act.dma_start(bv_row[:], flat(b_in, 2 * E, [[0, P], [1, E]])).then_inc(s_small, 16)
                    act.dma_start(bo_row[:], flat(b_out, 0, [[0, P], [1, E]])).then_inc(s_small, 16)
                    act.dma_start(b2_row[:], flat(b2, 0, [[0, P], [1, E]])).then_inc(s_small, 16)
                    for n in range(0, 4, 2):
                        evacuate(n)
                    act.wait_ge(s_w1, 16)
                    nc.scalar.activation(sgn1[:], w1_s[:], ACT.Sign).then_inc(s_sgn, 1)
                    act.wait_ge(s_w, 32)
                    nc.scalar.activation(sgn2[:], w2_s[:], ACT.Sign).then_inc(s_sgn, 1)
                    for n in range(4, len(jobs), 2):
                        evacuate(n)

                @block.gpsimd
                def _(pool):
                    pool.dma_start(x_s[:, 0], x[0].rearrange("(j p) e -> p j e", p=P)).then_inc(s_x[0], 16)
                    nc.gpsimd.memset(zeros[:], 0.0).then_inc(s_set, 1)
                    nc.gpsimd.memset(ident[:], 0.0).then_inc(s_set, 1)
                    nc.gpsimd.memset(eps_col[:], EPS).then_inc(s_set, 1)
                    pool.wait_ge(s_set, 2)
                    nc.gpsimd.affine_select(out=ident[:], in_=ident[:], compare_op=ALU.not_equal, fill=1.0,
                                            base=0, pattern=[[-1, P]], channel_multiplier=1).then_inc(s_set, 1)
                    pool.wait_ge(s_w1, 16)
                    pool.wait_ge(s_w, 32)
                    pool.dma_start(x_s[:, 1], x[1].rearrange("(j p) e -> p j e", p=P)).then_inc(s_x[1], 16)

                @block.vector
                def _(dve):
                    def evacuate(n):
                        src, dst = jobs[n]
                        dve.wait_ge(s_tr, n + 1)
                        nc.vector.tensor_copy(dst, bank[n % 8][:, 0:len(src) * P]).then_inc(s_evd, 1)

                    for n in range(1, 8, 2):
                        evacuate(n)
                    dve.wait_ge(s_small, 16 * (6 + 2 * (P // D)))
                    nc.vector.tensor_scalar(bq_col[:], b_col[:, 0:2], float(D) ** -0.5, None, ALU.mult)
                    nc.vector.tensor_scalar(bk_left[:], b_col[:, 2:4], rel_ends[:, 0:1], None, ALU.add)
                    nc.vector.tensor_scalar(bk_right[:], b_col[:, 2:4], rel_ends[:, 1:2], None, ALU.add)
                    nc.vector.tensor_scalar(rel_d[:, 0:P], relT[:, 0:P], relT[:, 0:1], None,
                                            ALU.subtract).then_inc(s_dve, 1)
                    nc.vector.tensor_scalar(rel_d[:, P:2 * P], over(relT[:, R - 1], P, 1), relT[:, 0:1], None,
                                            ALU.subtract)
                    nc.vector.tensor_scalar(rel_d[:, 2 * P:3 * P], relT[:, 0:P], relT[:, R - 1:R], None,
                                            ALU.subtract).then_inc(s_dve, 1)
                    dve.wait_ge(s_dve, 2)
                    nc.vector.tensor_copy(rel_parts[:, 0, :], rel_d[:]).then_inc(s_rel, 1)
                    dve.wait_ge(s_rel, 1)
                    nc.vector.tensor_tensor(rel_r[:], rel_d[:], rel_parts[:, 0, :], ALU.subtract).then_inc(s_dve, 1)
                    dve.wait_ge(s_dve, 3)
                    nc.vector.tensor_copy(rel_parts[:, 1, :], rel_r[:]).then_inc(s_rel, 1)
                    dve.wait_ge(s_rel, 2)
                    nc.vector.tensor_tensor(rel_parts[:, 2, :], rel_r[:], rel_parts[:, 1, :],
                                            ALU.subtract).then_inc(s_rel, 1)
                    dve.wait_ge(s_sgn, 2)
                    for j in range(2):
                        nc.vector.tensor_tensor_reduce(out=junk2[:, j, :], in0=w2_s[:, j, :], in1=sgn2[:, j, :],
                                                       scale=1.0 / HID, scalar=0.0, op0=ALU.mult, op1=ALU.add,
                                                       accum_out=alpha2[:, j:j + 1]).then_inc(s_dve, 1)
                    dve.wait_ge(s_dve, 5)
                    for j in range(2):
                        nc.vector.tensor_copy(alpha2_wide[:, j, :], over(alpha2[:, j], P, 1)).then_inc(s_src, 1)
                    for n in range(9, len(jobs), 2):
                        evacuate(n)
                    for j in range(KH):
                        nc.vector.tensor_tensor_reduce(out=junk1[:, j, :], in0=w1_s[:, j, :], in1=sgn1[:, j, :],
                                                       scale=1.0 / E, scalar=0.0, op0=ALU.mult, op1=ALU.add,
                                                       accum_out=alpha1[:, j:j + 1])

                @block.tensor
                def _(pe):
                    pe.wait_ge(s_set, 4)
                    pe.wait_ge(s_win, 16)
                    for n, (src, dst) in enumerate(jobs):
                        if n == 4:
                            pe.wait_ge(s_sgn, 1)
                        if n == 8:
                            pe.wait_ge(s_sgn, 2)
                        if n == len(jobs) - 1:
                            pe.wait_ge(s_src, 2)
                        if n >= 8:
                            pe.wait_ge(s_evd if n % 2 else s_eva, (n - 8) // 2 + 1)
                        for j, a in enumerate(src):
                            last = nc.tensor.transpose(bank[n % 8][:, j * P:(j + 1) * P], a, ident[:])
                        last.then_inc(s_tr, 1)

            WHOLES = 6
            xT = sb("xT", [P, 2, KE, HALF + T], F32)
            whole = sb("whole", [P, WHOLES, 512], F32)
            rest = sb("rest", [P, 2, 512], F32)
            parts = sb("parts", [P, 2, 3, PARTS, 2, T], BF16)
            v_s = sb("v_s", [P, 2, NG, NT, HG, PAD], F32)
            PRODUCTS = 12
            token = sb("token", [P, 4], F32)
            K_CHUNKS = [(w, m, half) for m in range(2) for half in range(2) for w in (1, 2)]
            Q_CHUNKS = [(0, m, half) for m in range(2) for half in range(2)]
            CHUNKS = len(K_CHUNKS) + len(Q_CHUNKS)
            V_AFTER = (6, 7, 8, 9)
            STORES = 3 * PARTS + NG
            s_passed = sem("waits_passed1")
            s_turned = sem("x_turned")
            s_job = sem("product_ready")
            s_xev = sem("xT_ready")
            s_vev = sem("v_ready")
            s_chunk = sem("chunk_ready")
            s_rest = sem("rest_ready")
            s_mid = [sem("middle_part_by_pool"), sem("middle_part_by_dve")]
            s_split = sem("chunk_split")
            s_store = [sem(f"stored{a}") for a in range(2)]
            block = ctx.enter_context(nc.Block())

            @block.gpsimd
            def _(pool):
                nc.gpsimd.memset(token[:, 0:1], 0.0).then_inc(s_turned, 8)
                nc.gpsimd.memset(token[:, 1:2], 0.0).then_inc(s_split, WHOLES)
                nc.gpsimd.memset(token[:, 2:3], 0.0).then_inc(s_chunk, CHUNKS)
                nc.gpsimd.memset(token[:, 3:4], 0.0).then_inc(s_vev, 4)
                nc.gpsimd.memset(v_s[:, 0, :, :, :, D:PAD], 1.0).then_inc(s_store[0], 16 * STORES)
                nc.gpsimd.memset(v_s[:, 1, :, :, :, D:PAD], 1.0).then_inc(s_store[1], 16 * STORES)
                def middle_parts(b, a):
                    for c, (w, m, half) in enumerate(K_CHUNKS + Q_CHUNKS):
                        if c % 2:
                            continue
                        pool.wait_ge(s_rest, b * CHUNKS + (c + 1))
                        pool.sem_inc(s_passed, 1)
                        nc.gpsimd.tensor_copy(parts[:, a, w, 1, m, half * 512:(half + 1) * 512],
                                              rest[:, c % 2, :]).then_inc(s_mid[0], 1)

                with pool.Fori(0, B // 2 - 1) as i:
                    for a in range(2):
                        middle_parts(i * 2 + a, a)
                        pool.wait_ge(s_turned, i * 8 + (4 * a + 12))
                        pool.dma_start(x_s[:, a], x[i * 2 + (2 + a)].rearrange("(j p) e -> p j e", p=P)).then_inc(s_x[a], 16)

                for a in range(2):
                    middle_parts(B - 2 + a, a)

            @block.sync
            def _(sp):
                for a in range(2 * HG):
                    sp.dma_start(flat(band_scr, a * NT * P * BAND_ROW,
                                      [[BAND_ROW, P], [P * BAND_ROW, NT], [1, P]]),
                                 zeros[:]).then_inc(s_zero, 16)
                sp.dma_start(band_scr[2 * HG * NT * P:, 0:P], zeros[0:1, 0]).then_inc(s_zero, 16)
                with sp.Fori(0, B // 2) as i:
                    for a in range(2):
                        b = i * 2 + a

                        def store(kinds):
                            for w in kinds:
                                for c in range(PARTS):
                                    dst = split_scr[w, c, bass.ds(b * NG, NG)].rearrange("g r t -> (g r) t")
                                    sp.dma_start(dst.rearrange("(m p) t -> p m t", p=P),
                                                 parts[:, a, w, c]).then_inc(s_store[a], 16)

                        sp.wait_ge(s_split, b * CHUNKS + (WHOLES + len(K_CHUNKS)))
                        sp.sem_inc(s_passed, 1)
                        store((1, 2))
                        sp.wait_ge(s_vev, b * 4 + 8)
                        sp.sem_inc(s_passed, 1)
                        for g in range(NG):
                            sp.dma_start(v_scr[b * NG + g],
                                         v_s[:, a, g].rearrange("p n h d -> p n (h d)")).then_inc(s_store[a], 16)
                        sp.wait_ge(s_split, b * CHUNKS + (WHOLES + CHUNKS))
                        sp.sem_inc(s_passed, 1)
                        store((0,))
                for a in range(2):
                    sp.wait_ge(s_store[a], 16 * STORES * (1 + B // 2))
                sp.wait_ge(s_zero, 16 * (2 * HG + 1))

            @block.tensor
            def _(pe):
                with pe.Fori(0, B // 2) as i:
                    for a in range(2):
                        b = i * 2 + a
                        job = 0

                        def free_bank():
                            if job < 4:
                                pe.wait_ge(s_vev, b * 4 + (job + 1))
                            elif job < 8:
                                pe.wait_ge(s_chunk, b * CHUNKS + (CHUNKS - 3 + job - 4))
                            elif job < 12:
                                pe.wait_ge(s_xev, b * 4 + (job - 7))
                            else:
                                pe.wait_ge(s_chunk, b * CHUNKS + (CHUNKS + 2 * (job - 11)))
                            return bank[job % 8]

                        pe.wait_ge(s_x[a], i * 16 + 16)
                        for half in range(2):
                            for kt in range(KE):
                                dst = free_bank()
                                for j in range(4):
                                    last = nc.tensor.transpose(dst[:, j * P:(j + 1) * P],
                                                               x_s[:, a, half * 4 + j, kt * P:(kt + 1) * P], ident[:])
                                last.then_inc(s_turned, 1)
                                job += 1
                        pe.wait_ge(s_xev, b * 4 + 4)
                        for what in (1, 2, 0):
                            if what == 2:
                                for n0 in range(0, NT, 2):
                                    dst = free_bank()
                                    for n in (n0, n0 + 1):
                                        for kt in range(KE):
                                            last = nc.tensor.matmul(dst[:, (n - n0) * E:(n - n0 + 1) * E],
                                                                    xT[:, a, kt, n * P:(n + 1) * P],
                                                                    wT[:, kt, 2 * E:3 * E],
                                                                    start=(kt == 0), stop=(kt == KE - 1))
                                    last.then_inc(s_job, 1)
                                    job += 1
                                continue
                            shift = HALF if what == 0 else 0
                            for m in range(2):
                                for half in range(2):
                                    dst = free_bank()
                                    for kt in range(KE):
                                        c0 = shift + half * 512
                                        last = nc.tensor.matmul(dst[:, :],
                                                                wT[:, kt, what * E + m * P:what * E + (m + 1) * P],
                                                                xT[:, a, kt, c0:c0 + 512],
                                                                start=(kt == 0), stop=(kt == KE - 1))
                                    last.then_inc(s_job, 1)
                                    job += 1

            @block.scalar
            def _(act):
                with act.Fori(0, B // 2) as i:
                    for a in range(2):
                        b = i * 2 + a
                        job = 0
                        for half in range(2):
                            for kt in range(KE):
                                act.wait_ge(s_turned, b * 4 + (8 + job + 1))
                                if half == 1:
                                    nc.scalar.activation(xT[:, a, kt, 0:HALF], bank[job][:, 512 - HALF:512], ACT.Copy)
                                last = nc.scalar.activation(xT[:, a, kt, HALF + half * 512:HALF + (half + 1) * 512],
                                                            bank[job][:, :], ACT.Copy)
                                last.then_inc(s_xev, 1)
                                job += 1
                        act.wait_ge(s_store[a], i * 16 * STORES + 16 * STORES)
                        chunk = 0
                        for what in (1, 0):
                            job = (12, 4)[what]
                            for m in range(2):
                                for half in range(2):
                                    act.wait_ge(s_job, b * PRODUCTS + (job - 3))
                                    src = bank[job % 8]
                                    kinds = [(0, [(0, 512, bq_col, float(D) ** -0.5)])] if what == 0 else [
                                        (1, [(0, HALF, bk_right, 1.0), (HALF, 512, bk_left, 1.0)] if half == 0
                                         else [(0, 512, bk_left, 1.0)]),
                                        (2, [(0, 512, bk_right, 1.0)])]
                                    for w, pieces in kinds:
                                        act.wait_ge(s_split, b * CHUNKS + (chunk + 1))
                                        for c0, c1, bias, scale in pieces:
                                            nc.scalar.activation(whole[:, chunk % WHOLES, c0:c1], src[:, c0:c1],
                                                                 ACT.Identity, bias=bias[:, m:m + 1], scale=scale)
                                        for c0, c1, bias, scale in pieces:
                                            last = nc.scalar.activation(
                                                parts[:, a, w, 0, m, half * 512 + c0:half * 512 + c1], src[:, c0:c1],
                                                ACT.Identity, bias=bias[:, m:m + 1], scale=scale)
                                        last.then_inc(s_chunk, 1)
                                        chunk += 1
                                    job += 1

            @block.vector
            def _(dve):
                with dve.Fori(0, B // 2) as i:
                    for a in range(2):
                        b = i * 2 + a
                        dve.wait_ge(s_store[a], i * 16 * STORES + 16 * STORES)
                        chunks = K_CHUNKS + Q_CHUNKS

                        def last_part(c):
                            w, m, half = chunks[c]
                            col = slice(half * 512, (half + 1) * 512)
                            dve.wait_ge(s_mid[c % 2], b * (CHUNKS // 2) + (c // 2 + 1))
                            nc.vector.tensor_tensor(parts[:, a, w, 2, m, col], rest[:, c % 2, :],
                                                    parts[:, a, w, 1, m, col], ALU.subtract).then_inc(s_split, 1)

                        for c, (w, m, half) in enumerate(chunks):
                            col = slice(half * 512, (half + 1) * 512)
                            dve.wait_ge(s_chunk, b * CHUNKS + (CHUNKS + c + 1))
                            dve.wait_ge(s_split, b * CHUNKS + (c + WHOLES - 1))
                            nc.vector.tensor_tensor(rest[:, c % 2, :], whole[:, c % WHOLES, :],
                                                    parts[:, a, w, 0, m, col], ALU.subtract).then_inc(s_rest, 1)
                            if c % 2:
                                dve.wait_ge(s_rest, b * CHUNKS + (c + 1))
                                nc.vector.tensor_copy(parts[:, a, w, 1, m, col],
                                                      rest[:, 1, :]).then_inc(s_mid[1], 1)
                            if c:
                                last_part(c - 1)
                            if c in V_AFTER:
                                j = V_AFTER.index(c)
                                dve.wait_ge(s_job, b * PRODUCTS + (5 + j))
                                for n in range(2):
                                    last = nc.vector.tensor_tensor(
                                        v_s[:, a, :, 2 * j + n, :, 0:D],
                                        bank[j][:, n * E:(n + 1) * E].rearrange("p (g h d) -> p g h d", g=NG, h=HG),
                                        bv_row[:].rearrange("p (g h d) -> p g h d", g=NG, h=HG), ALU.add)
                                last.then_inc(s_vev, 1)
                        last_part(CHUNKS - 1)

        with ExitStack() as ctx:
            def sb(name, shape, dt):
                return sb_in(ctx, name, shape, dt)

            def sem(name):
                return sem_in(ctx, name)

            KBUF = 3
            IP = NT // 2
            UNITS = IP * NT
            ITEMS = NT * HG
            CH = ITEMS // 2
            CHUNK_EVERY = UNITS // CH
            CHUNK_AT = 1
            CHUNKS_AHEAD = CH * 5 // 8
            PROLOGUE_CH = CH + CHUNKS_AHEAD
            PAIR_ITEMS = ITEMS // IP
            assert ITEMS == UNITS
            BAND_READS = [16 * HG // 2 * (2 if t == NT - 1 else 1) for t in range(NT)]
            UNROLL = 6
            LOOPS = (G - 2) // UNROLL
            assert LOOPS * UNROLL == G - 2

            keys = sb("keys", [QROWS, KBUF, 2, HG, T], BF16)
            queries = sb("queries", [QROWS, 2, IP, HG, 2 * P], BF16)
            values = sb("values", [P, 2, NT, HG * PAD], F32)
            band_all = sb("band_all", [P, 2 * ITEMS * 2 * P + 2 * P], F32)
            band = band_all[:, 0:2 * ITEMS * 2 * P].rearrange("p (a n h c) -> p a n h c", a=2, n=NT, h=HG)
            no_band = band_all[:, 2 * ITEMS * 2 * P:]
            BANDS_OUT = 4
            assert CH % BANDS_OUT == 0
            band_out = sb("band_out", [P, BANDS_OUT, 2, 2 * P], F32)
            probs = sb("probs", [P, 2, HG, 2 * P], F32)
            partial_max = sb("partial_max", [P, 2, ITEMS], F32)
            row_max = sb("row_max", [P, PAIR_ITEMS], F32)
            minus_max = sb("minus_max", [PAIR_ITEMS, IP, 2, P], BF16)
            weighted_s = sb("weighted_s", [P, IP, 2 * P], F32)
            token = sb("token2", [P, 8], F32)

            weigh_ps = [ctx.enter_context(nc.psum_tensor(f"weigh_ps{a}", [P, HG, 2 * P], F32)) for a in range(2)]
            look_ps = [ctx.enter_context(nc.psum_tensor(f"look_ps{a}", [P, 512], F32)) for a in range(2)]
            band_ps = ctx.enter_context(nc.psum_tensor("band_ps", [P, 2, 2 * P], F32))
            sum_ps = ctx.enter_context(nc.psum_tensor("sum_ps", [P, 2 * P], F32))

            s_set = sem("constants_set")
            s_passed = sem("waits_passed")
            s_keys_first = sem("first_keys_in")
            s_keys = [sem(f"keys_in{a}") for a in range(KBUF)]
            s_q = [[sem(f"queries_in{a}_{k}") for k in range(IP)] for a in range(2)]
            s_v = [sem(f"values_in{a}") for a in range(2)]
            s_bp = sem("band_product_ready")
            s_be = sem("band_product_read")
            s_bw = [sem(f"band_written{a}") for a in range(BANDS_OUT)]
            s_b = [sem(f"band_in{t}") for t in range(NT)]
            s_look = [sem(f"look_ready{a}") for a in range(2)]
            s_seen = [sem(f"look_read{a}") for a in range(2)]
            s_rm = sem("row_max_ready")
            s_rmT = sem("row_max_turned")
            s_hi = sem("minus_max_high_ready")
            s_mm = sem("minus_max_ready")
            s_min = [[sem(f"minus_max_in{a}_{k}") for k in range(IP)] for a in range(2)]
            s_sc = sem("scores_ready")
            s_pr = sem("probs_ready")
            s_av = sem("weighted_sum_ready")
            s_ws = sem("weighted_sum_copied")
            s_ho = [sem(f"weighted_sum_stored{k}") for k in range(IP)]

            def key_kind(n, t):
                return 0 if n <= t + 1 else 1

            def look_pieces(t):
                pieces = []
                for pos in range(NT):
                    n = (t + pos) % NT
                    kind, half = key_kind(n, t), pos // 4
                    last = pieces[-1] if pieces else None
                    if last and last[0] == half and last[2] == kind and last[3] + last[4] == n:
                        last[4] += 1
                    else:
                        pieces.append([half, pos % 4 * P, kind, n, 1])
                return pieces

            def chunk_of(j):
                n = (j + CHUNKS_AHEAD) % CH
                ahead = 1 if j + CHUNKS_AHEAD < CH else 2
                return ahead, n // 2, 2 * (n % 2)

            def wait_apart(eng, *waits):
                for what, count in waits:
                    eng.wait_ge(what, count)
                eng.sem_inc(s_passed, 1)

            def load_keys(eng, s, k, loaded, terms=range(TERMS)):
                for kind in range(2):
                    for t in terms:
                        eng.dma_start(keys[t * D:(t + 1) * D, k % KBUF, kind],
                                     split_scr[1 + kind, TERM_K[t], s].rearrange("(h d) t -> d h t", h=HG)
                                     ).then_inc(loaded, 16)

            block = ctx.enter_context(nc.Block())

            @block.sync
            def _(sp):
                def load_queries(s, k, pair):
                    col = slice(pair * 2 * P, (pair + 1) * 2 * P)
                    for t in range(TERMS):
                        sp.dma_start(queries[t * D:(t + 1) * D, k % 2, pair],
                                     split_scr[0, TERM_Q[t], s].rearrange("(h d) t -> d h t", h=HG)[:, :, col]
                                     ).then_inc(s_q[k % 2][pair], 16)

                def write_band(s, j, k, tile, h0):
                    sp.wait_ge(s_be, s * CH + (j + 1))
                    a = j % BANDS_OUT
                    sp.dma_start(flat(band_scr, (((k % 2) * HG + h0) * NT + tile) * P * BAND_ROW + P,
                                      [[BAND_ROW, P], [NT * P * BAND_ROW, 2], [1, 2 * P]]),
                                 band_out[:, a]).then_inc(s_bw[a], 16)

                def read_band(s, j, k, tile, h0):
                    a = j % BANDS_OUT
                    written = s * (16 * CH // BANDS_OUT) + 16 * (j // BANDS_OUT + 1)
                    sp.wait_ge(s_bw[a], written)
                    base = (((k % 2) * HG + h0) * NT + tile) * P * BAND_ROW + P

                    def read(c0, c1, offset):
                        sp.dma_start(band[:, k % 2, tile, h0:h0 + 2, c0:c1],
                                     flat(band_scr, base + offset,
                                          [[BAND_ROW - 1, P], [NT * P * BAND_ROW, 2], [1, c1 - c0]])
                                     ).then_inc(s_b[tile], 16)

                    if tile == 0:
                        read(HALF, 2 * P, HALF)
                    elif tile == NT - 1:
                        read(0, P, 0)
                        read(P, P + HALF, 2 * P)
                    else:
                        read(0, 2 * P, 0)

                def load_minus_max(s, k, pair):
                    sp.wait_ge(s_mm, s * IP + (pair + 1))
                    for c in range(2):
                        row = queries[ROWS + c:ROWS + c + 1, k % 2, pair]
                        sp.dma_start(flat(row, 0, [row.ap[0], [P, PAIR_ITEMS], [1, P]]),
                                     minus_max[:, pair, c, :].rearrange("r (a p) -> r a p", a=1)
                                     ).then_inc(s_min[k % 2][pair], 16)

                o_heads = o_scr.rearrange("b h r t -> (b h) r t")

                def store_sums(s, pair):
                    sp.wait_ge(s_ws, s * IP + (pair + 2))
                    for h in range(HG):
                        sp.dma_start(o_heads[s * HG + h, :, pair * 2 * P:(pair + 1) * 2 * P],
                                     weighted_s[h * PAD:h * PAD + D + 1, pair]).then_inc(s_ho[pair], 16)

                def step(s, k, look=True, ahead=True):
                    def move_band(j, to_dram):
                        d, tile, h0 = chunk_of(j)
                        if look if d == 1 else ahead:
                            if to_dram:
                                write_band(s, PROLOGUE_CH + j, k + d, tile, h0)
                            else:
                                read_band(s, PROLOGUE_CH + j, k + d, tile, h0)

                    for u in range(1, UNITS + 1):
                        if u % NT == 0 and ahead:
                            wait_apart(sp, (s_sc, s * UNITS + u))
                            load_queries(s + 2, k + 2, u // NT - 1)
                        if u % CHUNK_EVERY == 0:
                            move_band(u // CHUNK_EVERY - 1, to_dram=True)
                            if u > CHUNK_EVERY:
                                move_band(u // CHUNK_EVERY - 2, to_dram=False)
                        if u == UNITS:
                            move_band(CH - 1, to_dram=False)
                            store_sums(s, IP - 1)
                        if u == 3:
                            load_minus_max(s, k, IP - 1)
                        elif u % NT == 3:
                            if look:
                                load_minus_max(s + 1, k + 1, u // NT - 1)
                            store_sums(s, u // NT - 1)

                def read_prologue_band(j):
                    read_band(0, j, j // CH, j % CH // 2, 2 * (j % 2))

                load_queries(0, 0, 0)
                load_queries(0, 0, 1)
                for j in range(PROLOGUE_CH):
                    if j % 4 == 2 and j // 4 + 2 < 2 * IP:
                        load_queries((j // 4 + 2) // IP, (j // 4 + 2) // IP, (j // 4 + 2) % IP)
                    tile, h0 = j % CH // 2, 2 * (j % 2)
                    write_band(0, j, j // CH, tile, h0)
                    if j >= 2:
                        read_prologue_band(j - 2)
                for j in (PROLOGUE_CH - 2, PROLOGUE_CH - 1):
                    read_prologue_band(j)
                for pair in range(IP - 1):
                    load_minus_max(0, 0, pair)
                with sp.Fori(0, LOOPS) as i:
                    for k in range(UNROLL):
                        step(i * UNROLL + k, k)
                step(G - 2, G - 2, ahead=False)
                step(G - 1, G - 1, look=False, ahead=False)
                for pair in range(IP):
                    sp.wait_ge(s_ho[pair], 16 * HG * (G + 1))

            @block.gpsimd
            def _(pool):
                def load_values(s, k):
                    pool.dma_start(values[:, k % 2], v_scr[s]).then_inc(s_v[k % 2], 16)

                nc.gpsimd.memset(no_band, 0.0).then_inc(s_set, 1)
                pool.wait_ge(s_set, 1)
                for a in range(2):
                    nc.gpsimd.memset(band[:, a, 0, :, 0:HALF], 0.0).then_inc(s_set, 1)
                    nc.gpsimd.memset(band[:, a, NT - 1, :, P + HALF:2 * P], 0.0).then_inc(s_set, 1)
                load_values(0, 0)
                load_keys(pool, 1, 1, s_keys[1])
                pool.wait_ge(s_set, 5)
                for a in range(KBUF):
                    nc.gpsimd.memset(keys[ROWS:QROWS, a], 1.0).then_inc(s_set, 1)
                pool.wait_ge(s_set, 5 + KBUF)
                nc.gpsimd.memset(token[:, 0:1], 0.0).then_inc(s_ws, 1)
                for pair in range(IP):
                    nc.gpsimd.memset(token[:, pair + 1:pair + 2], 0.0).then_inc(s_ho[pair], 16 * HG)

                def step(s, k, ahead=True):
                    wait_apart(pool, (s_sc, s * UNITS + 1))
                    load_values(s + 1, k + 1)
                    if ahead:
                        load_keys(pool, s + 2, k + 2, s_keys[(k + 2) % KBUF])

                with pool.Fori(0, LOOPS) as i:
                    for k in range(UNROLL):
                        step(i * UNROLL + k, k)
                step(G - 2, G - 2, ahead=False)

            @block.scalar
            def _(act):
                def copy_band(s, j):
                    act.wait_ge(s_bp, s * CH + (j + 1))
                    if j >= BANDS_OUT:
                        act.wait_ge(s_bw[j % BANDS_OUT], s * (16 * CH // BANDS_OUT) + 16 * (j // BANDS_OUT))
                    out_s = band_out[:, j % BANDS_OUT]
                    if j % CH // 2 == NT - 1:
                        nc.scalar.activation(out_s, band_ps[:], ACT.Copy).then_inc(s_be, 1)
                    else:
                        nc.scalar.activation(out_s[:, :, 0:P], band_ps[:, :, 0:P], ACT.Copy)
                        nc.scalar.activation(out_s[:, :, P:2 * P], over(band_ps[:, :, P], P, 2),
                                             ACT.Copy).then_inc(s_be, 1)

                def copy_sums(s, pair):
                    act.wait_ge(s_av, s * IP + (pair + 1))
                    act.wait_ge(s_ho[pair], s * (16 * HG) + 16 * HG)
                    nc.scalar.activation(weighted_s[:, pair], sum_ps[:], ACT.Copy).then_inc(s_ws, 1)

                def step(s, k, look=True, ahead=True):
                    for u in range(UNITS):
                        act.wait_ge(s_sc, s * UNITS + (u + 1))
                        nc.scalar.activation(probs[:, u % 2], weigh_ps[u % 2][:], ACT.Exp).then_inc(s_pr, 1)
                        if u and u % NT == 0:
                            copy_sums(s, u // NT - 1)
                        j = u // CHUNK_EVERY
                        if u % CHUNK_EVERY == CHUNK_AT and (look if chunk_of(j)[0] == 1 else ahead):
                            copy_band(s, PROLOGUE_CH + j)
                    copy_sums(s, IP - 1)

                for j in range(PROLOGUE_CH):
                    copy_band(0, j)
                    if j < TERMS:
                        load_keys(act, 0, 0, s_keys_first, [j])
                with act.Fori(0, LOOPS) as i:
                    for k in range(UNROLL):
                        step(i * UNROLL + k, k)
                step(G - 2, G - 2, ahead=False)
                step(G - 1, G - 1, look=False, ahead=False)

            @block.vector
            def _(dve):
                def look(s, k, item):
                    tile, h = item // HG, item % HG
                    count = s * ITEMS + (item + 1)
                    col = tile // 2 * PAIR_ITEMS + h * 2 + tile % 2
                    wait_apart(dve, (s_look[0], count), (s_b[tile], (s + 1) * BAND_READS[tile]))
                    mine = band[:, k % 2, tile, h]
                    bias = flat(mine, 0, [mine.ap[0], [no_band.offset - mine.offset, 2], [1, 2 * P]])
                    both = look_ps[0][:].rearrange("p (a c) -> p a c", a=2)
                    nc.vector.tensor_tensor_reduce(
                        out=both, in0=both, in1=bias, scale=1.0, scalar=LOWEST, op0=ALU.add, op1=ALU.max,
                        accum_out=partial_max[:, 0, col:col + 1]).then_inc(s_seen[0], 1)
                    dve.wait_ge(s_look[1], count)
                    nc.vector.reduce_max(partial_max[:, 1, col:col + 1], look_ps[1][:], AX_X).then_inc(s_seen[1], 1)

                def row_maxima(s, pair):
                    col = slice(pair * PAIR_ITEMS, (pair + 1) * PAIR_ITEMS)
                    dve.wait_ge(s_seen[1], s * ITEMS + (pair + 1) * PAIR_ITEMS)
                    nc.vector.tensor_reduce(row_max[:], partial_max[:, :, col].rearrange("p a i -> p i a"), AX_X,
                                            ALU.max).then_inc(s_rm, 1)

                def negate(s, pair):
                    count = s * IP + (pair + 1)
                    turned = look_ps[0][0:PAIR_ITEMS, 0:P]
                    dve.wait_ge(s_rmT, count)
                    nc.vector.tensor_scalar(minus_max[:, pair, 0, :], turned, -1.0, None, ALU.mult).then_inc(s_hi, 1)
                    dve.wait_ge(s_hi, count)
                    nc.vector.scalar_tensor_tensor(out=minus_max[:, pair, 1, :], in0=turned, scalar=-1.0,
                                                   in1=minus_max[:, pair, 0, :], op0=ALU.mult,
                                                   op1=ALU.subtract).then_inc(s_mm, 1)

                def looks(s, k, before=True):
                    for item in range(ITEMS):
                        pair = item // PAIR_ITEMS
                        if item % PAIR_ITEMS == 0 and item:
                            row_maxima(s, pair - 1)
                        look(s, k, item)
                        if item % PAIR_ITEMS == 0 and item:
                            negate(s, pair - 1)
                        if item == 0 and before:
                            negate(s - 1, IP - 1)

                def step(s, k):
                    row_maxima(s, IP - 1)
                    looks(s + 1, k + 1)

                dve.wait_ge(s_set, 5)
                looks(0, 0, before=False)
                with dve.Fori(0, LOOPS) as i:
                    for k in range(UNROLL):
                        step(i * UNROLL + k, k)
                step(G - 2, G - 2)
                row_maxima(G - 1, IP - 1)
                negate(G - 1, IP - 1)

            @block.tensor
            def _(pe):
                def query_tile(k, h, tile):
                    return queries[0:ROWS, k % 2, tile // 2, h, tile % 2 * P:(tile % 2 + 1) * P]

                def band_product(count, k, tile, h0, first=False):
                    if not first:
                        pe.wait_ge(s_be, count)
                    for h in range(2):
                        if tile == NT - 1:
                            last = nc.tensor.matmul(band_ps[:, h], query_tile(k, h0 + h, tile),
                                                    rel_terms[:].rearrange("p (a c) -> p a c", a=3)[:, 0:3:2],
                                                    start=True, stop=True)
                        else:
                            last = nc.tensor.matmul(band_ps[:, h, 0:P + 1], query_tile(k, h0 + h, tile),
                                                    rel_terms[:, 0:P + 1], start=True, stop=True)
                    last.then_inc(s_bp, 1)

                def look(s, k, item, half, first=False):
                    tile, h = item // HG, item % HG
                    if half == 0 and item % PAIR_ITEMS == 1 and not (first and item == 1):
                        pe.wait_ge(s_mm, s * IP + item // PAIR_ITEMS)
                    elif not (first and item == 0):
                        pe.wait_ge(s_seen[half], s * ITEMS + item)
                    for bank, col, kind, n, tiles in look_pieces(tile):
                        if bank == half:
                            last = nc.tensor.matmul(look_ps[half][:, col:col + tiles * P],
                                                    query_tile(k, h, tile),
                                                    keys[0:ROWS, k % KBUF, kind, h, n * P:(n + tiles) * P],
                                                    start=True, stop=True)
                    last.then_inc(s_look[half], 1)

                def turn_max(s, pair, looking=True):
                    pe.wait_ge(s_rm, s * IP + (pair + 1))
                    if looking:
                        pe.wait_ge(s_seen[0], s * ITEMS + ((pair + 1) * PAIR_ITEMS + 1))
                    nc.tensor.transpose(look_ps[0][0:PAIR_ITEMS, 0:P], row_max[:], ident[:]).then_inc(s_rmT, 1)

                def scores(s, k, u, heads=range(HG)):
                    pair, n = u // NT, u % NT
                    for h in heads:
                        dst = weigh_ps[u % 2][:, h]
                        started = False
                        for e in range(2):
                            tile = 2 * pair + e
                            side = (n - tile) % NT
                            if side < 2:
                                nc.tensor.matmul(dst[:, e * P:(e + 1) * P], band[:, k % 2, tile, h, side * P:(side + 1) * P], ident[:],
                                                 is_transpose=True, start=not started, stop=False,
                                                 skip_group_check=True)
                                started = True
                        kinds = [key_kind(n, 2 * pair + e) for e in range(2)]
                        spans = [(0, 2, kinds[0])] if kinds[0] == kinds[1] else [(0, 1, kinds[0]), (1, 2, kinds[1])]
                        for e0, e1, kind in spans:
                            last = nc.tensor.matmul(dst[:, e0 * P:e1 * P], keys[:, k % KBUF, kind, h, n * P:(n + 1) * P],
                                                    queries[:, k % 2, pair, h, e0 * P:e1 * P],
                                                    start=not started, stop=(e1 == 2), skip_group_check=True)
                            started = True
                    if h == HG - 1:
                        last.then_inc(s_sc, 1)

                def weighted(s, k, u):
                    pair, n = u // NT, u % NT
                    pe.wait_ge(s_pr, s * UNITS + (u + 1))
                    if n == 0:
                        pe.wait_ge(s_ws, s * IP + (pair + 1))
                    for h in range(HG):
                        last = nc.tensor.matmul(sum_ps[h * PAD:(h + 1) * PAD, :],
                                                values[:, k % 2, n, h * PAD:(h + 1) * PAD], probs[:, u % 2, h],
                                                start=(n == 0), stop=(n == NT - 1), tile_position=(0, h * PAD))
                    if n == NT - 1:
                        last.then_inc(s_av, 1)

                def step(s, k, look_on=True, ahead=True):
                    pe.wait_ge(s_v[k % 2], (s + (2 - k % 2)) * 8)
                    for u in range(UNITS):
                        if u % NT == 0:
                            pe.wait_ge(s_min[k % 2][u // NT], (s + (2 - k % 2)) * 16)
                        turns = u % PAIR_ITEMS == 1 and (look_on or u == 1)
                        scores(s, k, u, range(HG - 1))
                        if turns:
                            if u > 1:
                                turn_max(s + 1, u // PAIR_ITEMS - 1)
                            else:
                                turn_max(s, IP - 1, looking=look_on)
                        scores(s, k, u, range(HG - 1, HG))
                        if look_on:
                            if u == 0:
                                pe.wait_ge(s_keys[(k + 1) % KBUF], key_count(s + 1, k + 1))
                            if u % PAIR_ITEMS == 0:
                                pe.wait_ge(s_q[(k + 1) % 2][u // PAIR_ITEMS], query_count(s + 1, k + 1))
                            if not turns:
                                look(s + 1, k + 1, u, 0)
                        j = u // CHUNK_EVERY
                        d, tile, h0 = chunk_of(j)
                        if u % CHUNK_EVERY == CHUNK_AT and (look_on if d == 1 else ahead):
                            if tile % 2 == 0 and h0 == 0:
                                pe.wait_ge(s_q[(k + d) % 2][tile // 2], query_count(s + d, k + d))
                            band_product(s * CH + (PROLOGUE_CH + j), k + d, tile, h0)
                        if u:
                            weighted(s, k, u - 1)
                        if look_on:
                            if turns:
                                look(s + 1, k + 1, u, 0)
                            look(s + 1, k + 1, u, 1)
                    weighted(s, k, UNITS - 1)

                def query_count(s, k):
                    return (s - k % 2 + 2) * (16 * TERMS // 2)

                def key_count(s, k):
                    return (s - k % KBUF + (KBUF if k % KBUF else 0)) * (16 * 2 * TERMS // KBUF)

                AHEAD = 5
                for item in range(-AHEAD, ITEMS):
                    j = item + AHEAD
                    if j < PROLOGUE_CH:
                        tile, h0 = j % CH // 2, 2 * (j % 2)
                        if j % 4 == 0:
                            pe.wait_ge(s_q[j // CH][tile // 2], 16 * TERMS)
                        band_product(j, j // CH, tile, h0, first=(j == 0))
                    if item < 0:
                        continue
                    if item == 0:
                        pe.wait_ge(s_keys_first, 16 * 2 * TERMS)
                    if item > 1 and item % PAIR_ITEMS == 1:
                        turn_max(0, item // PAIR_ITEMS - 1)
                    for half in range(2):
                        look(0, 0, item, half, first=True)
                pe.wait_ge(s_set, 5 + KBUF)
                with pe.Fori(0, LOOPS) as i:
                    for k in range(UNROLL):
                        step(i * UNROLL + k, k)
                step(G - 2, G - 2, ahead=False)
                step(G - 1, G - 1, look_on=False, ahead=False)

        with ExitStack() as ctx:
            def sb(name, shape, dt):
                return sb_in(ctx, name, shape, dt)

            def sem(name):
                return sem_in(ctx, name)

            TOK = 512
            TT = TOK // P
            IT = B * T // TOK
            HM = P // D
            SPREAD = P // H
            assert KH == 2 * TT and T == 2 * TOK and IT % 2 == 0 and IT >= 8
            INNER = (IT - 4) // 2

            sums = sb("sums", [P, 2, TOK // SPREAD], F32)
            inverse = sb("inverse", [P, 2, TOK // SPREAD], F32)
            inverse_wide = sb("inverse_wide", [P, 2, KE, TOK], F32)
            heads_raw = sb("heads_raw", [P, 2, KE, TOK], F32)
            heads = sb("heads", [P, 2, KE, TOK], F32)
            x_in = sb("x_in", [P, 2, TT, E], F32)
            x_bo = sb("x_bo", [P, 2, TT, E], F32)
            y = sb("y", [P, TT, E], F32)
            x1 = sb("x1", [P, 2, TT, E], F32)
            x1_b2 = sb("x1_b2", [P, 2, TT, E], F32)
            x1T_rest = sb("x1T_rest", [P, KE, TOK], F32)
            x1T = sb("x1T", [P, 2, PARTS, KE, TOK], BF16)
            gelu = sb("gelu", [P, 2, TOK], F32)
            gelu_rest = sb("gelu_rest", [P, 2, TOK], F32)
            hidden = sb("hidden", [P, PARTS, KH, TOK], BF16)
            z = sb("z", [P, 2, TT, E], F32)
            fin = sb("fin", [P, 2, TT, E], F32)
            stats = sb("stats", [P, 2 * TT, 6], F32)
            mean_var = sb("mean_var", [P, 2 * TT, 2], F32)
            std = sb("std", [P, 2 * TT], F32)
            rstd = sb("rstd", [P, 2 * TT], F32)
            shift = sb("shift", [P, 2 * TT], F32)
            token = sb("token3", [P, 4], F32)
            unread = sb("unread", [P, 1], F32)
            DVE_MIDDLES = range(1, KH, 2)

            att_ps = ctx.enter_context(nc.psum_tensor("att_ps", [P, TT, E], F32))
            turn_ps = ctx.enter_context(nc.psum_tensor("turn_ps", [P, KE, TOK], F32))
            hid_ps = [ctx.enter_context(nc.psum_tensor(f"hid_ps{a}", [P, TOK], F32)) for a in range(2)]
            out_ps = ctx.enter_context(nc.psum_tensor("out_ps", [P, TT, E], F32))

            s_set = sem("stats_set")
            s_passed = sem("waits_passed3")
            s_sums = [sem(f"sums_in{a}") for a in range(2)]
            s_heads = [sem(f"heads_in{a}") for a in range(2)]
            s_x = [sem(f"residual_in{a}") for a in range(2)]
            s_rec = sem("inverse_ready")
            s_invw = [sem(f"inverse_written{a}") for a in range(2)]
            s_inv = [sem(f"inverse_in{a}") for a in range(2)]
            s_hn = sem("heads_divided")
            s_xb = sem("residual_with_bias")
            s_att = sem("projection_ready")
            s_y = sem("y_ready")
            s_yst = sem("y_stats")
            s_mv = sem("mean_var_ready")
            s_sd = sem("std_ready")
            s_rs = sem("rstd_ready")
            s_shift = sem("shift_ready")
            s_x1 = sem("x1_ready")
            s_x1b = sem("x1_with_bias")
            s_turn = sem("x1_turned")
            s_xh = sem("x1T_high_ready")
            s_xr = sem("x1T_rest_ready")
            s_xm = sem("x1T_middle_ready")
            s_x1T = sem("x1T_ready")
            s_h = sem("hidden_product")
            s_g = sem("gelu_ready")
            s_gr = sem("gelu_rest_ready")
            s_gm = sem("hidden_middle_by_pool")
            s_gmd = sem("hidden_middle_by_dve")
            s_hid = sem("hidden_ready")
            s_ff = sem("out_product")
            s_zp = sem("z_scaled")
            s_z = sem("z_ready")
            s_zst = sem("z_stats")
            s_fin = sem("fin_ready")
            s_out = [sem(f"out_stored{a}") for a in range(2)]

            x_rows = x.rearrange("b t e -> (b t) e")
            out_rows = out.rearrange("b t e -> (b t) e")
            block = ctx.enter_context(nc.Block())

            @block.sync
            def _(sp):
                def load(it, b, a, first=False):
                    if not first:
                        sp.wait_ge(s_rec, it - 1)
                        sp.wait_ge(s_xb, it - 1)
                        sp.wait_ge(s_hn, it - 1)
                    col = a * TOK
                    weights = o_scr[b, :, D, col:col + TOK]
                    sp.dma_start(sums[:, a], weights.rearrange("h (c t) -> h c t", c=SPREAD)).then_inc(s_sums[a], 16)
                    for m in range(KE):
                        sp.dma_start(heads_raw[:, a, m], o_scr[b, m * HM:(m + 1) * HM, 0:D, col:col + TOK]
                                     ).then_inc(s_heads[a], 16)
                    sp.dma_start(x_in[:, a], x_rows[bass.ds(it * TOK, TOK), :]
                                 .rearrange("(j p) e -> p j e", p=P)).then_inc(s_x[a], 16)
                    sp.wait_ge(s_rec, it + 1)
                    sp.dma_start(inverse_scr[it].rearrange("h (c t) -> h c t", c=SPREAD),
                                 inverse[:, a]).then_inc(s_invw[a], 16)
                    sp.wait_ge(s_invw[a], (it + (2 - a)) * 8)
                    for m in range(KE):
                        sp.dma_start(inverse_wide[:, a, m], over(inverse_scr[it, m * HM:(m + 1) * HM, :], D, 1)
                                     ).then_inc(s_inv[a], 16)

                load(0, 0, 0, first=True)
                load(1, 0, 1, first=True)
                with sp.Fori(0, B - 1) as i:
                    for a in range(2):
                        load(i * 2 + (2 + a), i + 1, a)

            @block.gpsimd
            def _(pool):
                for a in range(2):
                    nc.gpsimd.memset(fin[:, a, 0, 0:1], 0.0).then_inc(s_out[a], 16)
                nc.gpsimd.memset(token[:, 0:1], 0.0).then_inc(s_fin, 2)
                nc.gpsimd.memset(token[:, 1:2], 0.0).then_inc(s_ff, 1)
                nc.gpsimd.memset(token[:, 2:3], 0.0).then_inc(s_gr, 2)
                nc.gpsimd.memset(token[:, 3:4], 0.0).then_inc(s_hid, 2)
                nc.gpsimd.memset(mean_var[:], 1.0).then_inc(s_set, 1)

                def divide(it, a, first=False):
                    pool.wait_ge(s_heads[a], (it + (2 - a)) * 16)
                    pool.wait_ge(s_inv[a], (it + (2 - a)) * 16)
                    if not first:
                        pool.wait_ge(s_att, it - 1)
                    nc.gpsimd.tensor_tensor(heads[:, a], heads_raw[:, a], inverse_wide[:, a],
                                            ALU.mult).then_inc(s_hn, 1)

                def residual(it, a, first=False):
                    pool.wait_ge(s_x[a], (it + (2 - a)) * 8)
                    if not first:
                        pool.wait_ge(s_y, it - 1)
                    nc.gpsimd.tensor_tensor(x_bo[:, a], x_in[:, a], over(bo_row[:], TT, 1), ALU.add).then_inc(s_xb, 1)

                def skip(it, a, early=False):
                    pool.wait_ge(s_x1, it + 1)
                    if not early:
                        pool.wait_ge(s_z, it - 1)
                    nc.gpsimd.tensor_tensor(x1_b2[:, a], x1[:, a], over(b2_row[:], TT, 1), ALU.add).then_inc(s_x1b, 1)

                def add_skip(it, a):
                    pool.wait_ge(s_zp, it + 1)
                    pool.wait_ge(s_x1b, it + 1)
                    nc.gpsimd.tensor_tensor(z[:, a], z[:, a], x1_b2[:, a], ALU.add).then_inc(s_z, 1)

                def middle_parts(it):
                    for j in range(KH):
                        if j not in DVE_MIDDLES:
                            pool.wait_ge(s_gr, it * KH + (j + 3))
                            if j == 0:
                                pool.wait_ge(s_ff, it + 1)
                            pool.sem_inc(s_passed, 1)
                            nc.gpsimd.tensor_copy(hidden[:, 1, j], gelu_rest[:, j % 2]).then_inc(s_gm, 1)

                def iteration(it, a, before=True, skips=True, ahead=True):
                    middle_parts(it)
                    if before:
                        add_skip(it - 1, 1 - a)
                    if skips:
                        skip(it + 1, 1 - a, early=not before)
                    if ahead:
                        divide(it + 3, 1 - a)
                        residual(it + 3, 1 - a)

                divide(0, 0, first=True)
                residual(0, 0, first=True)
                divide(1, 1, first=True)
                residual(1, 1, first=True)
                divide(2, 0)
                residual(2, 0)
                skip(0, 0, early=True)
                iteration(0, 0, before=False)
                with pool.Fori(0, INNER) as i:
                    for a in (1, 0):
                        iteration(i * 2 + (1 if a else 2), a)
                iteration(IT - 3, 1, ahead=False)
                iteration(IT - 2, 0, ahead=False)
                iteration(IT - 1, 1, skips=False, ahead=False)
                add_skip(IT - 1, 1)

            @block.vector
            def _(dve):
                def invert(it, a, first=False):
                    dve.wait_ge(s_sums[a], (it + (2 - a)) * 8)
                    if not first:
                        dve.wait_ge(s_invw[a], (it - a) * 8)
                    nc.vector.reciprocal(inverse[:, a], sums[:, a]).then_inc(s_rec, 1)

                def scale(it, a):
                    dve.wait_ge(s_ff, it + 2)
                    dve.wait_ge(s_fin, it + 1)
                    nc.vector.tensor_tensor(z[:, a], out_ps[:], over(alpha2_row[:], TT, 1), ALU.mult).then_inc(s_zp, 1)

                def split_hidden(it):
                    for j in range(KH + 1):
                        if j < KH:
                            count = it * KH + (j + 1)
                            dve.wait_ge(s_g, count)
                            dve.wait_ge(s_hid, count)
                            nc.vector.tensor_tensor(gelu_rest[:, j % 2], gelu[:, j % 2], hidden[:, 0, j],
                                                    ALU.subtract).then_inc(s_gr, 1)
                            if j in DVE_MIDDLES:
                                dve.wait_ge(s_gr, count + 2)
                                nc.vector.tensor_copy(hidden[:, 1, j], gelu_rest[:, j % 2]).then_inc(s_gmd, 1)
                        if j:
                            if j - 1 in DVE_MIDDLES:
                                dve.wait_ge(s_gmd, it * (KH // 2) + j // 2)
                            else:
                                dve.wait_ge(s_gm, it * (KH // 2) + (j + 1) // 2)
                            nc.vector.tensor_tensor(hidden[:, 2, j - 1], gelu_rest[:, (j - 1) % 2],
                                                    hidden[:, 1, j - 1], ALU.subtract).then_inc(s_hid, 1)

                def split_x1T(it, a, first=False, between=None):
                    dve.wait_ge(s_xh, it + 1)
                    if not first:
                        dve.wait_ge(s_x1T, it)
                    nc.vector.tensor_tensor(x1T_rest[:], turn_ps[:], x1T[:, a, 0], ALU.subtract).then_inc(s_xr, 1)
                    if between is not None:
                        add_residual(*between)
                    dve.wait_ge(s_xm, it + 1)
                    nc.vector.tensor_tensor(x1T[:, a, 2], x1T_rest[:], x1T[:, a, 1], ALU.subtract).then_inc(s_x1T, 1)

                def add_residual(it, a, first=False):
                    dve.wait_ge(s_att, it + 1)
                    dve.wait_ge(s_xb, it + 1)
                    if not first:
                        dve.wait_ge(s_x1, it)
                    nc.vector.tensor_tensor(y[:], att_ps[:], x_bo[:, a], ALU.add).then_inc(s_y, 1)

                def norms(n, z_of=None, y_of=None, early=False):
                    if y_of is not None:
                        it, a = y_of
                        dve.wait_ge(s_y, it + 1)
                        for t in range(TT):
                            last = nc.vector.bn_stats(stats[:, t, :], y[:, t])
                        last.then_inc(s_yst, 1)
                    if z_of is not None:
                        dve.wait_ge(s_z, z_of[0] + 1)
                        for t in range(TT):
                            last = nc.vector.bn_stats(stats[:, TT + t, :], z[:, z_of[1], t])
                        last.then_inc(s_zst, 1)
                    if y_of is not None:
                        dve.wait_ge(s_yst, y_of[0] + 1)
                    if z_of is not None:
                        dve.wait_ge(s_zst, z_of[0] + 1)
                        dve.wait_ge(s_fin, z_of[0] + 2)
                    dve.sem_inc(s_passed, 1)
                    cols = range(0 if y_of is not None else TT, 2 * TT if z_of is not None else TT)
                    for t in cols:
                        last = nc.vector.bn_aggr(mean_var[:, t, :], stats[:, t, :])
                    last.then_inc(s_mv, 1)
                    dve.wait_ge(s_sd, n + 1)
                    nc.vector.reciprocal(rstd[:], std[:]).then_inc(s_rs, 1)
                    dve.wait_ge(s_rs, n + 1)
                    nc.vector.scalar_tensor_tensor(out=shift[:], in0=mean_var[:, :, 0], scalar=-1.0, in1=rstd[:],
                                                   op0=ALU.mult, op1=ALU.mult).then_inc(s_shift, 1)
                    if y_of is not None:
                        it, a = y_of
                        if not early:
                            dve.wait_ge(s_turn, it - 1)
                            dve.wait_ge(s_x1b, it - 1)
                        for t in range(TT):
                            last = nc.vector.tensor_scalar(x1[:, a, t], y[:, t], mean_var[:, t, 0:1], rstd[:, t:t + 1],
                                                           ALU.subtract, ALU.mult)
                        last.then_inc(s_x1, 1)

                def iteration(it, a, before=True, turns=True, ahead=True, inverts=True):
                    if before:
                        scale(it - 1, 1 - a)
                    if inverts:
                        invert(it + 3, 1 - a)
                    split_hidden(it)
                    if turns:
                        split_x1T(it + 1, 1 - a, between=(it + 2, a) if ahead else None)
                    if before or ahead:
                        norms(it + 2, z_of=(it - 1, 1 - a) if before else None, y_of=(it + 2, a) if ahead else None)

                dve.wait_ge(s_set, 1)
                invert(0, 0, first=True)
                invert(1, 1, first=True)
                add_residual(0, 0, first=True)
                norms(0, y_of=(0, 0), early=True)
                invert(2, 0)
                split_x1T(0, 0, first=True)
                add_residual(1, 1)
                norms(1, y_of=(1, 1), early=True)
                iteration(0, 0, before=False)
                with dve.Fori(0, INNER) as i:
                    for a in (1, 0):
                        iteration(i * 2 + (1 if a else 2), a)
                iteration(IT - 3, 1, inverts=False)
                iteration(IT - 2, 0, ahead=False, inverts=False)
                iteration(IT - 1, 1, turns=False, ahead=False, inverts=False)
                scale(IT - 1, 1)
                norms(IT + 2, z_of=(IT - 1, 1))

            @block.scalar
            def _(act):
                def roots(n, more=True):
                    act.wait_ge(s_mv, n + 1)
                    nc.scalar.activation(std[:], mean_var[:, :, 1], ACT.Sqrt, bias=eps_col[:, 0:1]).then_inc(s_sd, 1)
                    if more:
                        nc.scalar.activation(unread[:], eps_col[:], ACT.Gelu)

                def gelus(it):
                    act.wait_ge(s_ff, it + 1)
                    for j in range(KH):
                        count = it * KH + (j + 1)
                        act.wait_ge(s_h, count)
                        act.wait_ge(s_gr, count)
                        nc.scalar.activation(gelu[:, j % 2], hid_ps[j % 2][:], ACT.Gelu, bias=b1_col[:, j:j + 1],
                                             scale=alpha1[:, j:j + 1])
                        nc.scalar.activation(hidden[:, 0, j], hid_ps[j % 2][:], ACT.Gelu, bias=b1_col[:, j:j + 1],
                                             scale=alpha1[:, j:j + 1]).then_inc(s_g, 1)

                def copy_turned(it, a):
                    act.wait_ge(s_turn, it + 1)
                    nc.scalar.activation(x1T[:, a, 0], turn_ps[:], ACT.Copy).then_inc(s_xh, 1)
                    act.wait_ge(s_xr, it + 1)
                    nc.scalar.activation(x1T[:, a, 1], x1T_rest[:], ACT.Copy).then_inc(s_xm, 1)

                def finish(it, a):
                    act.wait_ge(s_shift, it + 4)
                    act.wait_ge(s_out[a], (it + (2 - a)) * 8)
                    for t in range(TT):
                        col = slice(TT + t, TT + t + 1)
                        last = nc.scalar.activation(fin[:, a, t], z[:, a, t], ACT.Identity, bias=shift[:, col],
                                                    scale=rstd[:, col])
                    last.then_inc(s_fin, 1)

                def store(it, a):
                    act.wait_ge(s_fin, it + 3)
                    act.dma_start(out_rows[bass.ds(it * TOK, TOK), :].rearrange("(j p) e -> p j e", p=P),
                                  fin[:, a]).then_inc(s_out[a], 16)

                def iteration(it, a, before=True, turns=True):
                    gelus(it)
                    if turns:
                        copy_turned(it + 1, 1 - a)
                    if before:
                        finish(it - 2, a)
                        store(it - 2, a)
                    roots(it + 2, more=turns)

                roots(0)
                copy_turned(0, 0)
                roots(1)
                iteration(0, 0, before=False)
                iteration(1, 1, before=False)
                with act.Fori(0, INNER) as i:
                    for a in range(2):
                        iteration(i * 2 + (2 + a), a)
                iteration(IT - 2, 0)
                iteration(IT - 1, 1, turns=False)
                finish(IT - 2, 0)
                store(IT - 2, 0)
                roots(IT + 2, more=False)
                finish(IT - 1, 1)
                store(IT - 1, 1)
                for a in range(2):
                    act.wait_ge(s_out[a], 16 + 16 * IT // 2)

            @block.tensor
            def _(pe):
                def project(it, a, first=False, tiles=range(TT)):
                    if 0 in tiles:
                        pe.wait_ge(s_hn, it + 1)
                        if not first:
                            pe.wait_ge(s_y, it)
                    for t in tiles:
                        for m in range(KE):
                            last = nc.tensor.matmul(att_ps[:, t], heads[:, a, m, t * P:(t + 1) * P], woT[:, m],
                                                    start=(m == 0), stop=(m == KE - 1))
                    if TT - 1 in tiles:
                        last.then_inc(s_att, 1)

                def turn(it, a, first=False):
                    pe.wait_ge(s_x1, it + 1)
                    if not first:
                        pe.wait_ge(s_xr, it)
                    for kt in range(KE):
                        for t in range(TT):
                            last = nc.tensor.transpose(turn_ps[:, kt, t * P:(t + 1) * P],
                                                       x1[:, a, t, kt * P:(kt + 1) * P], ident[:])
                    last.then_inc(s_turn, 1)

                def layer1(it, a, first=False, ahead=True):
                    pe.wait_ge(s_x1T, it + 1)
                    for j in range(KH):
                        if not (first and j < 2):
                            pe.wait_ge(s_g, it * KH + (j - 1))
                        terms = [(c, kt) for c in range(PARTS) for kt in range(KE)]
                        for c, kt in terms:
                            last = nc.tensor.matmul(hid_ps[j % 2][:], sign1T[:, kt, j * P:(j + 1) * P],
                                                    x1T[:, a, c, kt], start=((c, kt) == terms[0]),
                                                    stop=((c, kt) == terms[-1]))
                        last.then_inc(s_h, 1)
                        if ahead and j % 2:
                            project(it + 2, a, tiles=range(j // 2, j // 2 + 1))

                def layer2(it, first=False):
                    pe.wait_ge(s_g, it * KH + KH)
                    if not first:
                        pe.wait_ge(s_zp, it)
                    terms = [(c, j) for c in range(PARTS) for j in range(KH)]
                    for t in range(TT):
                        for c, j in terms:
                            if t == 0 and j == 0 and c == 1:
                                pe.wait_ge(s_gm, it * (KH // 2) + KH // 2)
                                pe.wait_ge(s_gmd, it * (KH // 2) + KH // 2)
                            if t == 0 and j == 0 and c == 2:
                                pe.wait_ge(s_hid, it * KH + (KH + 2))
                            last = nc.tensor.matmul(out_ps[:, t], hidden[:, c, j, t * P:(t + 1) * P], sign2T[:, j],
                                                    start=((c, j) == terms[0]), stop=((c, j) == terms[-1]))
                    last.then_inc(s_ff, 1)

                def iteration(it, a, first=False, turns=True, ahead=True):
                    layer1(it, a, first, ahead)
                    if turns:
                        turn(it + 1, 1 - a)
                    layer2(it, first)

                project(0, 0, first=True)
                turn(0, 0, first=True)
                project(1, 1)
                iteration(0, 0, first=True)
                with pe.Fori(0, INNER) as i:
                    for a in (1, 0):
                        iteration(i * 2 + (1 if a else 2), a)
                iteration(IT - 3, 1)
                iteration(IT - 2, 0, ahead=False)
                iteration(IT - 1, 1, turns=False, ahead=False)



_INS = ['L0_attn_q', 'L0_attn_in_proj_weight', 'L0_attn_in_proj_bias', 'L0_attn_out_w', 'L0_attn_out_b',
        'L0_attn_rel_pe', 'L0_ffn_w1', 'L0_ffn_b1', 'L0_ffn_w2', 'L0_ffn_b2']
_OUTS = [((8, 1024, 256), 'float32')]


def kernel(**inputs):
    import numpy as _np
    import concourse.bacc as _bacc
    from concourse import mybir as _mybir
    from concourse.bass_utils import run_bass_kernel_spmd as _run

    nc = _bacc.Bacc("TRN2", target_bir_lowering=False, num_devices=1)
    arrays, args = {}, []
    for name in _INS:
        a = _np.ascontiguousarray(inputs[name])
        arrays[f"in_{name}_dram"] = a
        args.append(nc.dram_tensor(f"in_{name}_dram", a.shape, _mybir.dt.from_np(a.dtype), kind="ExternalInput").ap())
    for i, (shape, dtype) in enumerate(_OUTS):
        dt = _mybir.dt.from_np(_np.dtype(dtype))
        args.append(nc.dram_tensor(f"out_{i}_dram", shape, dt, kind="ExternalOutput").ap())
    post_ln_block(nc, *args)
    r = _run(nc, [arrays], core_ids=[0])
    got = tuple(r.results[0][f"out_{i}_dram"] for i in range(len(_OUTS)))
    return got[0]
```
